# Optimizing a Trainium2 kernel written in Bass

```python
import numpy as np
import jax
import jax.numpy as jnp

def _softmax(x, axis=-1):
    return jax.nn.softmax(x, axis=axis)

def _gelu(x):
    return jax.nn.gelu(x, approximate=True)

def _silu(x):
    return jax.nn.silu(x)

def _sigmoid(x):
    return jax.nn.sigmoid(x)

def _layernorm(x, axis=-1, eps=1e-05):
    m = jnp.mean(x, axis=axis, keepdims=True)
    v = jnp.var(x, axis=axis, keepdims=True)
    return (x - m) / jnp.sqrt(v + eps)

def _scatter_add(tgt, idx, src, axis=0):
    return tgt.at[idx].add(src)

def _segment_sum(src, seg, n):
    return jax.ops.segment_sum(src, seg, n)
kernel_name = 'mk_metaformer_d4_conv_nhwc128_r4_5825f9'

def setup_inputs(seed: int=0):
    np.random.seed(seed)
    _w = jnp.asarray

    def _rec_inputs():
        import jax
        import jax.numpy as jnp
        _gk = jax.random.key(seed)
        x = -0.0003929 + 0.9999 * jax.random.normal(jax.random.fold_in(_gk, 1), (32, 16, 16, 32), jnp.float32)
        return x
    x = _rec_inputs()

    def _L0_conv_setup():
        import jax, jax.numpy as jnp
        import numpy as np
        HEADS = 4
        DIM_HEAD = 32
        DIM = HEADS * DIM_HEAD
        B, H, W, C = (32, 16, 16, 32)
        LN_EPS = 1e-05
        key = jax.random.key(seed)
        k0, k1, k2, k3, k4 = jax.random.split(key, 5)
        x = jax.random.normal(k0, (B, H, W, C), dtype=jnp.float32)
        w_qkv = jax.random.normal(k1, (C, DIM * 3), dtype=jnp.float32) * (1.0 / np.sqrt(C))
        w_out = jax.random.normal(k2, (DIM, C), dtype=jnp.float32) * (1.0 / np.sqrt(DIM))
        b_out = jax.random.normal(k3, (C,), dtype=jnp.float32) * 0.01
        ln_scale = jnp.ones((C,), dtype=jnp.float32)
        return {'x': x, 'w_qkv': w_qkv, 'w_out': w_out, 'b_out': b_out, 'ln_scale': ln_scale}
    _L0_conv_all = _L0_conv_setup()
    _L0_conv_in = {k: v for k, v in _L0_conv_all.items() if k in ('w_qkv', 'w_out', 'b_out', 'ln_scale')}
    del _L0_conv_all

    def _L0_ffn_setup():
        import jax, jax.numpy as jnp
        import numpy as np
        PADDED_SL = 2048
        TEMPERATURE = 1.0
        SIGMA_POW = 0.25

        def _stu_conv(phi, u, n):
            b, sl, d = u.shape
            sgn = jnp.where(jnp.arange(sl) % 2 == 0, 1.0, -1.0).astype(u.dtype)
            sgn3 = sgn[None, :, None]
            Vf = jnp.fft.rfft(phi, n=n, axis=0)
            Uf_p = jnp.fft.rfft(u, n=n, axis=1)
            Uf_m = jnp.fft.rfft(u * sgn3, n=n, axis=1)
            U_plus = jnp.fft.irfft(Vf[None, :, :, None] * Uf_p[:, :, None, :], n=n, axis=1)[:, :sl]
            U_minus = jnp.fft.irfft(Vf[None, :, :, None] * Uf_m[:, :, None, :], n=n, axis=1)[:, :sl]
            U_minus = U_minus * sgn[None, :, None, None]
            return (U_plus, U_minus)

        def _compute_spectral(u, sigma, phi, Mpp, Mpm):
            U_plus, U_minus = _stu_conv(phi, u, PADDED_SL)
            s = sigma ** SIGMA_POW
            out = jnp.einsum('btkd,k,kde->bte', U_plus, s, Mpp)
            out = out + jnp.einsum('btkd,k,kde->bte', U_minus, s, Mpm)
            return out

        def _compute_ar_u(Mu, u):
            sl = u.shape[1]
            out = jnp.zeros(u.shape[:2] + (Mu.shape[-1],), dtype=u.dtype)
            for i in range(Mu.shape[0]):
                ui = jnp.pad(u, ((0, 0), (i, 0), (0, 0)))[:, :sl]
                out = out + jnp.einsum('btd,de->bte', ui, Mu[i])
            return out

        def _stu(u, sigma, phi, Mu, Mpp, Mpm):
            return _compute_spectral(u, sigma, phi, Mpp, Mpm) + _compute_ar_u(Mu, u)
        key = jax.random.key(seed)
        ks = jax.random.split(key, 8)
        b, sl, d, K, k_u = (2, 1024, 32, 16, 3)
        x = jax.random.normal(ks[0], (b, sl, d), dtype=jnp.float32)
        sigma = jax.random.uniform(ks[1], (K,), dtype=jnp.float32, minval=0.001, maxval=1.0)
        phi = jax.random.normal(ks[2], (sl, K), dtype=jnp.float32) / np.sqrt(sl)
        M_u = jax.random.normal(ks[3], (4, k_u, d, d), dtype=jnp.float32) * 0.02
        M_phi_plus = jax.random.normal(ks[4], (4, K, d, d), dtype=jnp.float32) * 0.02
        M_phi_minus = jax.random.normal(ks[5], (4, K, d, d), dtype=jnp.float32) * 0.02
        log_weights = jnp.ones((4,), dtype=jnp.float32)
        u01 = jax.random.uniform(ks[6], (4,), dtype=jnp.float32, minval=1e-06, maxval=1.0 - 1e-06)
        gumbel = -jnp.log(-jnp.log(u01))
        return {'x': x, 'sigma': sigma, 'phi': phi, 'M_u': M_u, 'M_phi_plus': M_phi_plus, 'M_phi_minus': M_phi_minus, 'log_weights': log_weights, 'gumbel': gumbel}
    _L0_ffn_all = _L0_ffn_setup()
    _L0_ffn_in = {k: v for k, v in _L0_ffn_all.items() if k in ('sigma', 'phi', 'M_u', 'M_phi_plus', 'M_phi_minus', 'log_weights', 'gumbel')}
    del _L0_ffn_all

    def _L1_conv_setup():
        import jax, jax.numpy as jnp
        import numpy as np
        EPS = 1e-05

        def _ln(x, g, b):
            m = jnp.mean(x, axis=-1, keepdims=True)
            v = jnp.var(x, axis=-1, keepdims=True)
            return (x - m) / jnp.sqrt(v + EPS) * g + b
        key = jax.random.key(seed)
        ks = jax.random.split(key, 16)
        B, N, CZ, C = (1, 128, 32, 16)
        s_cz = 1.0 / np.sqrt(CZ)
        s_c = 1.0 / np.sqrt(C)

        def lin(k, fan_in, shape):
            return jax.random.uniform(k, shape, jnp.float32, -1.0, 1.0) / np.sqrt(fan_in)
        return {'x': jax.random.normal(ks[0], (B, N, N, CZ), jnp.float32), 'Wa1': lin(ks[1], CZ, (CZ, C)), 'ba1': lin(ks[2], CZ, (C,)), 'Wa2': lin(ks[3], CZ, (CZ, C)), 'ba2': lin(ks[4], CZ, (C,)), 'Wb1': lin(ks[5], CZ, (CZ, C)), 'bb1': lin(ks[6], CZ, (C,)), 'Wb2': lin(ks[7], CZ, (CZ, C)), 'bb2': lin(ks[8], CZ, (C,)), 'ln2_g': jnp.ones((C,), jnp.float32), 'ln2_b': jnp.zeros((C,), jnp.float32), 'Wg': lin(ks[9], CZ, (CZ, CZ)), 'bg': lin(ks[10], CZ, (CZ,)), 'Wz': lin(ks[11], C, (C, CZ)), 'bz': lin(ks[12], C, (CZ,))}
    _L1_conv_all = _L1_conv_setup()
    _L1_conv_in = {k: v for k, v in _L1_conv_all.items() if k in ('Wa1', 'ba1', 'Wa2', 'ba2', 'Wb1', 'bb1', 'Wb2', 'bb2', 'ln2_g', 'ln2_b', 'Wg', 'bg', 'Wz', 'bz')}
    del _L1_conv_all

    def _L1_ffn_setup():
        import jax, jax.numpy as jnp
        import numpy as np
        BN_EPS = 1e-05
        key = jax.random.key(seed)
        k1, k2, k3 = jax.random.split(key, 3)
        B, T, I, H = (16, 512, 32, 32)
        x = jax.random.normal(k1, (B, T, I), dtype=jnp.float32)
        W = jax.random.normal(k2, (H, I), dtype=jnp.float32) * (1.0 / np.sqrt(I))
        V = jnp.linalg.qr(jax.random.normal(k3, (H, H), dtype=jnp.float32))[0]
        gamma = jnp.ones((H,), dtype=jnp.float32)
        beta = jnp.zeros((H,), dtype=jnp.float32)
        return {'x': x, 'W': W, 'V': V, 'gamma': gamma, 'beta': beta}
    _L1_ffn_all = _L1_ffn_setup()
    _L1_ffn_in = {k: v for k, v in _L1_ffn_all.items() if k in ('W', 'V', 'gamma', 'beta')}
    del _L1_ffn_all

    def _L2_conv_setup():
        import jax, jax.numpy as jnp
        import numpy as np
        B, H, W_DIM, C = (8, 32, 64, 32)
        K = 9

        def conv1d_same(y, W):
            return jax.lax.conv_general_dilated(y, W, window_strides=(1,), padding='SAME', dimension_numbers=('NWC', 'WIO', 'NWC'))
        key = jax.random.key(seed)
        kx, kw = jax.random.split(key)
        x = jax.random.normal(kx, (B, H, W_DIM, C), dtype=jnp.float32)
        W = jax.random.normal(kw, (K, C, C), dtype=jnp.float32) * 0.02
        return {'x': x, 'W': W}
    _L2_conv_all = _L2_conv_setup()
    _L2_conv_in = {k: v for k, v in _L2_conv_all.items() if k in ('W',)}
    del _L2_conv_all

    def _L2_ffn_setup():
        import jax, jax.numpy as jnp
        import numpy as np
        B, S, D, E, H, O, K = (128, 512, 32, 16, 128, 32, 8)
        key = jax.random.key(seed)
        k0, k1, k2, k3 = jax.random.split(key, 4)
        x = jax.random.normal(k0, (B, S, D), dtype=jnp.float32)
        gate_w = jax.random.normal(k1, (E, D), dtype=jnp.float32) * (1.0 / np.sqrt(D))
        gate_b = jnp.zeros((E,), dtype=jnp.float32)
        weight1 = jax.random.uniform(k2, (E, D + 1, H), dtype=jnp.float32, minval=-1.0, maxval=1.0) * (1.0 / np.sqrt(D + 1))
        weight2 = jax.random.uniform(k3, (E, H + 1, O), dtype=jnp.float32, minval=-1.0, maxval=1.0) * (1.0 / np.sqrt(H + 1))
        return {'x': x, 'gate_w': gate_w, 'gate_b': gate_b, 'weight1': weight1, 'weight2': weight2}
    _L2_ffn_all = _L2_ffn_setup()
    _L2_ffn_in = {k: v for k, v in _L2_ffn_all.items() if k in ('gate_w', 'gate_b', 'weight1', 'weight2')}
    del _L2_ffn_all

    def _L3_conv_setup():
        import jax, jax.numpy as jnp
        import numpy as np
        B, H, W_DIM, C = (8, 32, 64, 32)
        K = 9

        def conv1d_same(y, W):
            return jax.lax.conv_general_dilated(y, W, window_strides=(1,), padding='SAME', dimension_numbers=('NWC', 'WIO', 'NWC'))
        key = jax.random.key(seed)
        kx, kw = jax.random.split(key)
        x = jax.random.normal(kx, (B, H, W_DIM, C), dtype=jnp.float32)
        W = jax.random.normal(kw, (K, C, C), dtype=jnp.float32) * 0.02
        return {'x': x, 'W': W}
    _L3_conv_all = _L3_conv_setup()
    _L3_conv_in = {k: v for k, v in _L3_conv_all.items() if k in ('W',)}
    del _L3_conv_all

    def _L3_ffn_setup():
        import jax, jax.numpy as jnp
        import numpy as np
        BN_EPS = 1e-05
        key = jax.random.key(seed)
        k1, k2, k3 = jax.random.split(key, 3)
        B, T, I, H = (16, 512, 32, 32)
        x = jax.random.normal(k1, (B, T, I), dtype=jnp.float32)
        W = jax.random.normal(k2, (H, I), dtype=jnp.float32) * (1.0 / np.sqrt(I))
        V = jnp.linalg.qr(jax.random.normal(k3, (H, H), dtype=jnp.float32))[0]
        gamma = jnp.ones((H,), dtype=jnp.float32)
        beta = jnp.zeros((H,), dtype=jnp.float32)
        return {'x': x, 'W': W, 'V': V, 'gamma': gamma, 'beta': beta}
    _L3_ffn_all = _L3_ffn_setup()
    _L3_ffn_in = {k: v for k, v in _L3_ffn_all.items() if k in ('W', 'V', 'gamma', 'beta')}
    del _L3_ffn_all
    return {'x': x, 'L0_conv_w_qkv': _L0_conv_in['w_qkv'], 'L0_conv_w_out': _L0_conv_in['w_out'], 'L0_conv_b_out': _L0_conv_in['b_out'], 'L0_conv_ln_scale': _L0_conv_in['ln_scale'], 'L0_ffn_sigma': _L0_ffn_in['sigma'], 'L0_ffn_phi': _L0_ffn_in['phi'], 'L0_ffn_M_u': _L0_ffn_in['M_u'], 'L0_ffn_M_phi_plus': _L0_ffn_in['M_phi_plus'], 'L0_ffn_M_phi_minus': _L0_ffn_in['M_phi_minus'], 'L0_ffn_log_weights': _L0_ffn_in['log_weights'], 'L0_ffn_gumbel': _L0_ffn_in['gumbel'], 'L1_conv_Wa1': _L1_conv_in['Wa1'], 'L1_conv_ba1': _L1_conv_in['ba1'], 'L1_conv_Wa2': _L1_conv_in['Wa2'], 'L1_conv_ba2': _L1_conv_in['ba2'], 'L1_conv_Wb1': _L1_conv_in['Wb1'], 'L1_conv_bb1': _L1_conv_in['bb1'], 'L1_conv_Wb2': _L1_conv_in['Wb2'], 'L1_conv_bb2': _L1_conv_in['bb2'], 'L1_conv_ln2_g': _L1_conv_in['ln2_g'], 'L1_conv_ln2_b': _L1_conv_in['ln2_b'], 'L1_conv_Wg': _L1_conv_in['Wg'], 'L1_conv_bg': _L1_conv_in['bg'], 'L1_conv_Wz': _L1_conv_in['Wz'], 'L1_conv_bz': _L1_conv_in['bz'], 'L1_ffn_W': _L1_ffn_in['W'], 'L1_ffn_V': _L1_ffn_in['V'], 'L1_ffn_gamma': _L1_ffn_in['gamma'], 'L1_ffn_beta': _L1_ffn_in['beta'], 'L2_conv_W': _L2_conv_in['W'], 'L2_ffn_gate_w': _L2_ffn_in['gate_w'], 'L2_ffn_gate_b': _L2_ffn_in['gate_b'], 'L2_ffn_weight1': _L2_ffn_in['weight1'], 'L2_ffn_weight2': _L2_ffn_in['weight2'], 'L3_conv_W': _L3_conv_in['W'], 'L3_ffn_W': _L3_ffn_in['W'], 'L3_ffn_V': _L3_ffn_in['V'], 'L3_ffn_gamma': _L3_ffn_in['gamma'], 'L3_ffn_beta': _L3_ffn_in['beta']}

def reference(x, L0_conv_w_qkv, L0_conv_w_out, L0_conv_b_out, L0_conv_ln_scale, L0_ffn_sigma, L0_ffn_phi, L0_ffn_M_u, L0_ffn_M_phi_plus, L0_ffn_M_phi_minus, L0_ffn_log_weights, L0_ffn_gumbel, L1_conv_Wa1, L1_conv_ba1, L1_conv_Wa2, L1_conv_ba2, L1_conv_Wb1, L1_conv_bb1, L1_conv_Wb2, L1_conv_bb2, L1_conv_ln2_g, L1_conv_ln2_b, L1_conv_Wg, L1_conv_bg, L1_conv_Wz, L1_conv_bz, L1_ffn_W, L1_ffn_V, L1_ffn_gamma, L1_ffn_beta, L2_conv_W, L2_ffn_gate_w, L2_ffn_gate_b, L2_ffn_weight1, L2_ffn_weight2, L3_conv_W, L3_ffn_W, L3_ffn_V, L3_ffn_gamma, L3_ffn_beta):
    import jax
    import jax.numpy as jnp

    def _L0_conv_ref(x, w_qkv, w_out, b_out, ln_scale):
        import jax, jax.numpy as jnp
        import numpy as np
        HEADS = 4
        DIM_HEAD = 32
        DIM = HEADS * DIM_HEAD
        B, H, W, C = (32, 16, 16, 32)
        LN_EPS = 1e-05
        b, h, w, c = x.shape
        n = h * w
        qkv = jnp.einsum('bhwc,cf->bhwf', x, w_qkv)
        q, k, v = jnp.split(qkv, 3, axis=-1)
        q = q.reshape(b, n, HEADS, DIM_HEAD)
        k = k.reshape(b, n, HEADS, DIM_HEAD)
        v = v.reshape(b, n, HEADS, DIM_HEAD)
        q = jax.nn.softmax(q, axis=-1) * (1.0 / np.sqrt(DIM_HEAD))
        k = jax.nn.softmax(k, axis=1)
        v = v * (1.0 / n)
        context = jnp.einsum('bnhd,bnhe->bhde', k, v)
        out = jnp.einsum('bhde,bnhd->bnhe', context, q)
        out = out.reshape(b, h, w, DIM)
        out = jnp.einsum('bhwd,dc->bhwc', out, w_out) + b_out
        mu = jnp.mean(out, axis=-1, keepdims=True)
        var = jnp.mean(jnp.square(out - mu), axis=-1, keepdims=True)
        out = (out - mu) * jax.lax.rsqrt(var + LN_EPS) * ln_scale
        return out

    def _L0_ffn_ref(x, sigma, phi, M_u, M_phi_plus, M_phi_minus, log_weights, gumbel):
        import jax, jax.numpy as jnp
        import numpy as np
        PADDED_SL = 2048
        TEMPERATURE = 1.0
        SIGMA_POW = 0.25

        def _stu_conv(phi, u, n):
            b, sl, d = u.shape
            sgn = jnp.where(jnp.arange(sl) % 2 == 0, 1.0, -1.0).astype(u.dtype)
            sgn3 = sgn[None, :, None]
            Vf = jnp.fft.rfft(phi, n=n, axis=0)
            Uf_p = jnp.fft.rfft(u, n=n, axis=1)
            Uf_m = jnp.fft.rfft(u * sgn3, n=n, axis=1)
            U_plus = jnp.fft.irfft(Vf[None, :, :, None] * Uf_p[:, :, None, :], n=n, axis=1)[:, :sl]
            U_minus = jnp.fft.irfft(Vf[None, :, :, None] * Uf_m[:, :, None, :], n=n, axis=1)[:, :sl]
            U_minus = U_minus * sgn[None, :, None, None]
            return (U_plus, U_minus)

        def _compute_spectral(u, sigma, phi, Mpp, Mpm):
            U_plus, U_minus = _stu_conv(phi, u, PADDED_SL)
            s = sigma ** SIGMA_POW
            out = jnp.einsum('btkd,k,kde->bte', U_plus, s, Mpp)
            out = out + jnp.einsum('btkd,k,kde->bte', U_minus, s, Mpm)
            return out

        def _compute_ar_u(Mu, u):
            sl = u.shape[1]
            out = jnp.zeros(u.shape[:2] + (Mu.shape[-1],), dtype=u.dtype)
            for i in range(Mu.shape[0]):
                ui = jnp.pad(u, ((0, 0), (i, 0), (0, 0)))[:, :sl]
                out = out + jnp.einsum('btd,de->bte', ui, Mu[i])
            return out

        def _stu(u, sigma, phi, Mu, Mpp, Mpm):
            return _compute_spectral(u, sigma, phi, Mpp, Mpm) + _compute_ar_u(Mu, u)
        T = x.shape[1]
        outs = []
        for i, frac in enumerate((1, 2, 4, 8)):
            xi = x[:, :T // frac]
            si = _stu(xi, sigma, phi, M_u[i], M_phi_plus[i], M_phi_minus[i])
            si = jnp.pad(si, ((0, 0), (0, T - si.shape[1]), (0, 0)))
            outs.append(si)
        y_soft = jax.nn.softmax((log_weights + gumbel) / TEMPERATURE)
        y_hard = jax.nn.one_hot(jnp.argmax(y_soft), 4, dtype=y_soft.dtype)
        weights = y_hard - jax.lax.stop_gradient(y_soft) + y_soft
        stacked = jnp.stack(outs, axis=-1)
        return jnp.sum(stacked * weights, axis=-1)

    def _L1_conv_ref(x, Wa1, ba1, Wa2, ba2, Wb1, bb1, Wb2, bb2, ln2_g, ln2_b, Wg, bg, Wz, bz):
        import jax, jax.numpy as jnp
        import numpy as np
        EPS = 1e-05

        def _ln(x, g, b):
            m = jnp.mean(x, axis=-1, keepdims=True)
            v = jnp.var(x, axis=-1, keepdims=True)
            return (x - m) / jnp.sqrt(v + EPS) * g + b
        direction = 'outgoing'
        a = jax.nn.sigmoid((x @ Wa1 + ba1) * (x @ Wa2 + ba2))
        b = jax.nn.sigmoid((x @ Wb1 + bb1) * (x @ Wb2 + bb2))
        if direction == 'incoming':
            a = jnp.swapaxes(a, 1, 2)
            b = jnp.swapaxes(b, 1, 2)
        g = jax.nn.sigmoid(x @ Wg + bg)
        z = jnp.einsum('bikc,bkjc->bijc', a, b)
        return g * (_ln(z, ln2_g, ln2_b) @ Wz + bz)

    def _L1_ffn_ref(x, W, V, gamma, beta):
        import jax, jax.numpy as jnp
        import numpy as np
        BN_EPS = 1e-05
        B, T, H = (x.shape[0], x.shape[1], W.shape[0])
        Wx = jnp.einsum('bti,hi->bth', x, W)
        flat = Wx.reshape(B * T, H)
        mean = jnp.mean(flat, axis=0)
        var = jnp.var(flat, axis=0)
        Wx = ((flat - mean) * jax.lax.rsqrt(var + BN_EPS) * gamma + beta).reshape(B, T, H)
        Vt = V.T

        def step(yt, wx_t):
            yt = jax.nn.sigmoid(wx_t + yt @ Vt)
            return (yt, yt)
        y0 = jnp.zeros((B, H), dtype=Wx.dtype)
        _, ys = jax.lax.scan(step, y0, jnp.swapaxes(Wx, 0, 1))
        return jnp.swapaxes(ys, 0, 1)

    def _L2_conv_ref(x, W):
        import jax, jax.numpy as jnp
        import numpy as np
        B, H, W_DIM, C = (8, 32, 64, 32)
        K = 9

        def conv1d_same(y, W):
            return jax.lax.conv_general_dilated(y, W, window_strides=(1,), padding='SAME', dimension_numbers=('NWC', 'WIO', 'NWC'))
        rows = jnp.moveaxis(x, 1, 0)
        row0 = rows[0]

        def step(carry, row):
            new = row + jax.nn.relu(conv1d_same(carry, W))
            return (new, new)
        _, outs = jax.lax.scan(step, row0, rows[1:])
        out = jnp.concatenate([row0[None], outs], axis=0)
        return jnp.moveaxis(out, 0, 1)

    def _L2_ffn_ref(x, gate_w, gate_b, weight1, weight2):
        import jax, jax.numpy as jnp
        import numpy as np
        B, S, D, E, H, O, K = (128, 512, 32, 16, 128, 32, 8)
        Bn, Sn, Dn = x.shape
        logits = jnp.einsum('bsd,ed->bse', x, gate_w) + gate_b
        probs = jax.nn.softmax(logits, axis=1)
        vals, idx = jax.lax.top_k(probs.transpose(0, 2, 1), K)
        topv = vals.transpose(0, 2, 1)
        topi = idx.transpose(0, 2, 1)
        flat_idx = topi.reshape(Bn, K * E)
        gathered = jnp.take_along_axis(x, flat_idx[:, :, None], axis=1)
        gathered = gathered.reshape(Bn, K, E, Dn)
        pooled = jnp.einsum('bked,bke->bed', gathered, topv)
        ones = jnp.ones((E, Bn, 1), dtype=x.dtype)
        h = jnp.concatenate([pooled.transpose(1, 0, 2), ones], axis=-1)
        h = jax.nn.gelu(jnp.einsum('ebd,edh->ebh', h, weight1), approximate=False)
        h = jnp.concatenate([h, ones], axis=-1)
        out = jnp.einsum('ebh,eho->ebo', h, weight2)
        out = out.transpose(1, 0, 2)
        weighted = jnp.einsum('beo,bke->bkeo', out, topv).reshape(Bn, K * E, O)
        outputs = jnp.zeros((Bn, Sn, O), dtype=x.dtype)
        outputs = outputs.at[jnp.arange(Bn)[:, None], flat_idx].add(weighted)
        return outputs

    def _L3_conv_ref(x, W):
        import jax, jax.numpy as jnp
        import numpy as np
        B, H, W_DIM, C = (8, 32, 64, 32)
        K = 9

        def conv1d_same(y, W):
            return jax.lax.conv_general_dilated(y, W, window_strides=(1,), padding='SAME', dimension_numbers=('NWC', 'WIO', 'NWC'))
        rows = jnp.moveaxis(x, 1, 0)
        row0 = rows[0]

        def step(carry, row):
            new = row + jax.nn.relu(conv1d_same(carry, W))
            return (new, new)
        _, outs = jax.lax.scan(step, row0, rows[1:])
        out = jnp.concatenate([row0[None], outs], axis=0)
        return jnp.moveaxis(out, 0, 1)

    def _L3_ffn_ref(x, W, V, gamma, beta):
        import jax, jax.numpy as jnp
        import numpy as np
        BN_EPS = 1e-05
        B, T, H = (x.shape[0], x.shape[1], W.shape[0])
        Wx = jnp.einsum('bti,hi->bth', x, W)
        flat = Wx.reshape(B * T, H)
        mean = jnp.mean(flat, axis=0)
        var = jnp.var(flat, axis=0)
        Wx = ((flat - mean) * jax.lax.rsqrt(var + BN_EPS) * gamma + beta).reshape(B, T, H)
        Vt = V.T

        def step(yt, wx_t):
            yt = jax.nn.sigmoid(wx_t + yt @ Vt)
            return (yt, yt)
        y0 = jnp.zeros((B, H), dtype=Wx.dtype)
        _, ys = jax.lax.scan(step, y0, jnp.swapaxes(Wx, 0, 1))
        return jnp.swapaxes(ys, 0, 1)

    def _gn(v, G=32, eps=1e-05):
        B_, H_, W_, C_ = v.shape
        g = v.reshape(B_, H_, W_, G, C_ // G)
        m = jnp.mean(g, axis=(1, 2, 4), keepdims=True)
        s = jnp.var(g, axis=(1, 2, 4), keepdims=True)
        return ((g - m) / jnp.sqrt(s + eps)).reshape(v.shape)

    def _ln_c(v, eps=1e-06):
        m = jnp.mean(v, axis=-1, keepdims=True)
        s = jnp.var(v, axis=-1, keepdims=True)
        return (v - m) / jnp.sqrt(s + eps)

    def _ln_t(v, eps=1e-05):
        m = jnp.mean(v, axis=-1, keepdims=True)
        s = jnp.var(v, axis=-1, keepdims=True)
        return (v - m) / jnp.sqrt(s + eps)

    def _to_tokens(v):
        B_, H_, W_, C_ = v.shape
        return v.reshape(B_, H_ * W_, C_)

    def _from_tokens(t, like):
        return t.reshape(like.shape)
    x = x + _L0_conv_ref(_ln_c(x), L0_conv_w_qkv, L0_conv_w_out, L0_conv_b_out, L0_conv_ln_scale)
    t = _to_tokens(x)
    t = t + _L0_ffn_ref(_ln_t(t), L0_ffn_sigma, L0_ffn_phi, L0_ffn_M_u, L0_ffn_M_phi_plus, L0_ffn_M_phi_minus, L0_ffn_log_weights, L0_ffn_gumbel)
    x = _from_tokens(t, x)
    x = x + _L1_conv_ref(_ln_c(x), L1_conv_Wa1, L1_conv_ba1, L1_conv_Wa2, L1_conv_ba2, L1_conv_Wb1, L1_conv_bb1, L1_conv_Wb2, L1_conv_bb2, L1_conv_ln2_g, L1_conv_ln2_b, L1_conv_Wg, L1_conv_bg, L1_conv_Wz, L1_conv_bz)
    t = _to_tokens(x)
    t = t + _L1_ffn_ref(_ln_t(t), L1_ffn_W, L1_ffn_V, L1_ffn_gamma, L1_ffn_beta)
    x = _from_tokens(t, x)
    x = x + _L2_conv_ref(_ln_c(x), L2_conv_W)
    t = _to_tokens(x)
    t = t + _L2_ffn_ref(_ln_t(t), L2_ffn_gate_w, L2_ffn_gate_b, L2_ffn_weight1, L2_ffn_weight2)
    x = _from_tokens(t, x)
    x = x + _L3_conv_ref(_ln_c(x), L3_conv_W)
    t = _to_tokens(x)
    t = t + _L3_ffn_ref(_ln_t(t), L3_ffn_W, L3_ffn_V, L3_ffn_gamma, L3_ffn_beta)
    x = _from_tokens(t, x)
    return x

_drawn_inputs = setup_inputs


def setup_inputs(seed=0):
    import zlib

    import numpy as np

    out = dict(_drawn_inputs(seed))
    spreads = {'L0_conv_ln_scale': (1.0, 0.2),
     'L0_ffn_log_weights': (1.0, 0.2),
     'L1_conv_ln2_g': (1.0, 0.557),
     'L1_conv_ln2_b': (0.0, 0.599),
     'L1_ffn_gamma': (1.0, 0.6),
     'L1_ffn_beta': (0.0, 0.725),
     'L2_ffn_gate_b': (0.0, 0.8),
     'L3_ffn_gamma': (1.0, 0.6),
     'L3_ffn_beta': (0.0, 0.8)}
    factors = {'L0_conv_w_qkv': 8.0,
     'L0_conv_w_out': 8.0,
     'L1_conv_bb2': 3.368,
     'L1_conv_bg': 4.49,
     'L2_ffn_gate_w': 8.0,
     'L2_ffn_weight1': 8.0,
     'L2_ffn_weight2': 8.0}
    for name, (base, spread) in spreads.items():
        noise = np.random.default_rng([zlib.crc32(name.encode()), seed]).standard_normal(out[name].shape)
        drawn = base * np.exp(spread * noise) if base else spread * noise
        out[name] = jnp.asarray(drawn.astype(out[name].dtype))
    for name, factor in factors.items():
        out[name] = (out[name] * factor).astype(out[name].dtype)
    return out
```

```python
from contextlib import ExitStack

import concourse.bass as bass
from concourse import mybir

F32 = mybir.dt.float32
I32 = mybir.dt.int32
ALU = mybir.AluOpType
ACT = mybir.ActivationFunctionType
AX = mybir.AxisListType.X

P = 128
B, H, W, C = 32, 16, 16, 32
T = H * W
NQ = P // C
G = B // NQ
NT = T // NQ
CH = 4
CW_ = G * T // CH
HEADS, DH = 4, 32
KF = 16
FRACS = 4
AR = 3
CT = 16
E, HID, TOPK = 16, 128, 8
TAPS = 9
LN_CONV, LN_TOK = 1e-6, 1e-5
SWEEPS = 13
SETTLED = 2.0 ** -21

STAGES = 9


def build(nc, stop=STAGES, force_steps=False, **d):
    x, out = d["x"], d["out"]
    with ExitStack() as ctx:
        def sb(name, shape, dt=F32):
            return ctx.enter_context(nc.sbuf_tensor(name, shape, dt))

        def sem(name):
            return ctx.enter_context(nc.semaphore(name))

        xQ = sb("xQ", [P, G, T])
        xR = sb("xR", [P, NT, B])
        xN = xR[:, :, :].rearrange("p (g k) c -> p g k c", g=G)
        xn = sb("xn", [P, G * T])
        xnQ = xn[:, :].rearrange("p (g t) -> p g t", g=G)
        xnH = xR[:, :, :].rearrange("p t b -> p (t b)").rearrange("p (h g w) -> p h g w", h=H, g=G)
        sq = sb("sq", [P, 2, CW_])
        lnv = sb("lnv", [P, 2, CW_])
        rs = sb("rs", [P, 2, CW_])

        centre = sb("centre", [P, P])
        mean32 = sb("mean32", [P, P])
        ones32 = sb("ones32", [P, P])
        ident = sb("ident", [P, P])
        quarter = sb("quarter", [P, P])
        ones = sb("ones", [P, P])
        par16 = sb("par16", [P, 8])

        attn_scratch = sb("attn_scratch", [P, 9216])
        N_FILT, N_RAW, N_TOEP = (AR + T) * C, FRACS * C * C, (T + T // 2 + T // 4 + T // 8) * C
        arena = sb("arena", [P, N_FILT + N_RAW + N_TOEP])

        bank = ctx.enter_context(nc.psum_tensor("bank", [P, 8, CW_], F32))

        wq = sb("wq", [P, NQ, P])
        wk = sb("wk", [P, NQ, P])
        wvo = sb("wvo", [P, NQ, P])
        wv_rows = sb("wv_rows", [P, P])
        wv_t = sb("wv_t", [P, P])
        wo_bd = sb("wo_bd", [P, P])
        bout = sb("bout", [P, 1])
        lnsc = sb("lnsc", [P, 1])

        wm_raw = arena[:, N_FILT:N_FILT + N_RAW].rearrange("p (f m) -> p f m", f=FRACS)
        sigma = sb("sigma", [P, 1])
        sig4 = sb("sig4", [P, 1])
        nsig4 = sb("nsig4", [P, 1])
        phi_rows = sb("phi_rows", [P, 2, P])
        phi_cols = sb("phi_cols", [P, 2, P])
        flip = sb("flip", [P, 1])
        lw = sb("lw", [P, FRACS])
        gum = sb("gum", [P, FRACS])
        fw = sb("fw", [P, 8, FRACS])
        filt = arena[:, 0:N_FILT].rearrange("p (t e) -> p t e", e=C)
        SEG_T = [T, T // 2, T // 4, T // 8]
        SEG_AT = [0, T, T + T // 2, T + T // 2 + T // 4]
        toep = arena[:, N_FILT + N_RAW:].rearrange("p (t e) -> p t e", e=C)

        wa = sb("wa", [P, P])
        wb = sb("wb", [P, P])
        wg = sb("wg", [P, P])
        ab_bias = sb("ab_bias", [P, 2, 2 * CT])
        bg = sb("bg", [P, 1])
        wz = sb("wz", [P, 8, C])
        wz_rows = sb("wz_rows", [CT, NQ, C])
        g2 = sb("g2", [P, 1])
        b2 = sb("b2", [CT, 1])
        bz = sb("bz", [P, 1])
        bz2 = sb("bz2", [P, 1])

        rw = [sb(f"rw{i}", [P, P]) for i in range(2)]
        rv = [sb(f"rv{i}", [P, P]) for i in range(2)]
        rwt = [sb(f"rwt{i}", [P, P]) for i in range(2)]
        rvt = [sb(f"rvt{i}", [P, P]) for i in range(2)]
        rgam = [sb(f"rgam{i}", [P, 1]) for i in range(2)]
        rbet = [sb(f"rbet{i}", [P, 1]) for i in range(2)]
        taps = [sb(f"taps{i}", [P, TAPS, C]) for i in range(2)]
        band = [sb(f"band{i}", [P, 3, NQ, C]) for i in range(2)]

        gw_rows = sb("gw_rows", [P, P])
        gw = sb("gw", [P, P])
        gwc = sb("gwc", [P, NQ * E])
        gb = sb("gb", [P, 1])
        w1 = arena[0:C + 1, 24000:24000 + E * HID].rearrange("p (e h) -> p e h", e=E)
        w2 = arena[:, 26048:26048 + E * C].rearrange("p (e o) -> p e o", e=E)
        w2b_rows = sb("w2b_rows", [C, C])
        w2b = sb("w2b", [C, C])
        unsettled = sb("unsettled", [1, 2], I32)

        block = ctx.enter_context(nc.Block())
        s = {}

        def S(name):
            if name not in s:
                s[name] = sem(name)
            return s[name]

        bankQ = bank[:, :, :].rearrange("p k (g t) -> p (k g) t", t=T)

        def chunkQ(a, j):
            return a[:, 2 * j:2 * j + 2, :]

        def flat(a, j):
            return a[:, j * CW_:(j + 1) * CW_]

        xQf = xQ[:, :, :].rearrange("p g t -> p (g t)")
        xRf = xR[:, :, :].rearrange("p t b -> p (t b)")

        LNS = ["attn", "attn_out", "stu", "tri", "rnn0", "scan0", "moe", "scan1", "rnn1"]
        LN_EPS = [LN_CONV, LN_TOK, LN_TOK, LN_CONV, LN_TOK, LN_CONV, LN_TOK, LN_CONV, LN_TOK]

        def ln_pe(pe, k, src, ready):
            def centred(j):
                i = CH * k + j
                ready(j)
                if i >= 2:
                    pe.wait_ge(S("ln_applied"), i - 1)
                pe.matmul(bank[:, i % 2, :], centre[:, :], src(j), start=True, stop=True).then_inc(S("ln_centred"), 1)

            centred(0)
            for j in range(CH):
                i = CH * k + j
                if j + 1 < CH:
                    centred(j + 1)
                pe.wait_ge(S("ln_squared"), i + 1)
                if i >= 2:
                    pe.wait_ge(S("ln_logged"), i - 1)
                pe.matmul(bank[:, 2 + i % 2, :], mean32[:, :], sq[:, i % 2, :], start=True, stop=True)\
                    .then_inc(S("ln_var"), 1)

        def ln_act(act, k):
            def square(j):
                i = CH * k + j
                act.wait_ge(S("ln_centred"), i + 1)
                if i >= 2:
                    act.wait_ge(S("ln_var"), i - 1)
                act.activation(sq[:, i % 2, :], bank[:, i % 2, :], ACT.Square).then_inc(S("ln_squared"), 1)

            square(0)
            for j in range(CH):
                i = CH * k + j
                if j + 1 < CH:
                    square(j + 1)
                act.wait_ge(S("ln_var"), i + 1)
                if i >= 2:
                    act.wait_ge(S("ln_rstd"), i - 1)
                act.activation(lnv[:, i % 2, :], bank[:, 2 + i % 2, :], ACT.Ln, bias=LN_EPS[k])\
                    .then_inc(S("ln_logged"), 1)
                act.wait_ge(S("ln_logged"), i + 1)
                if i >= 2:
                    act.wait_ge(S("ln_applied"), i - 1)
                act.activation(rs[:, i % 2, :], lnv[:, i % 2, :], ACT.Exp, scale=-0.5).then_inc(S("ln_rstd"), 1)

        def ln_dve(dve, k, apply=None):
            for j in range(CH):
                i = CH * k + j
                dve.wait_ge(S("ln_rstd"), i + 1)
                if apply is None:
                    dve.tensor_tensor(flat(xn, j), bank[:, i % 2, :], rs[:, i % 2, :], ALU.mult)\
                        .then_inc(S("ln_applied"), 1)
                else:
                    apply(j, i)

        at = [0, attn_scratch]

        def cut(n):
            at[0] += n
            assert at[0] <= (9216 if at[1] is attn_scratch else 24000)
            return at[1][:, at[0] - n:at[0]]

        def buf(n, k=2):
            return cut(n * k).rearrange("p (k n) -> p k n", k=k)

        kE = buf(CW_)
        kN = buf(CW_)
        vo = buf(CW_)
        qb = buf(CW_)
        qs = buf(CW_)
        qe = buf(CW_)
        lz = buf(CW_)
        qn = buf(CW_, 3)
        cwt = cut(3 * 64).rearrange("p (k g c) -> p k g c", k=3, c=C)
        nkm = cut(32)
        kz = cut(32)
        rkz = cut(32)
        qm = cut(32).rearrange("p (k n) -> p k n", k=2)
        yb = xR[:, :, :].rearrange("p t b -> p (t b)")
        U = CH * NQ

        at[:] = [0, arena]
        a_bd = cut(64 * 8 * 16).rearrange("p (m g i) -> p m g i", m=64, g=8)
        ab_pre = cut(2048)
        a_in = cut(1024)
        a_s = cut(1024)
        b_s = cut(1024)
        zc = cut(1024)
        gate = cut(2048)
        zq = ab_pre[:, 0:1024]
        zn = ab_pre[:, 1024:2048]
        zT = a_bd.rearrange("p m g i -> p (m g i)")[:, 0:1024]
        upd = a_bd.rearrange("p m g i -> p (m g i)")[:, 2048:4096]
        zst = cut(4 * 64).rearrange("p (k n) -> p k n", k=4)

        at[0] = 0
        yS = cut(G * (T + 1)).rearrange("p (g t) -> p g t", g=G)
        yF = cut(G * (T + 1)).rearrange("p (g t) -> p g t", g=G)
        zs = cut(G * T)
        pre = buf(CW_, CH)
        moved = cut(CH + 2)
        bst = cut(CH * 6).rearrange("p (k n) -> p k n", n=6)
        mv = cut(2)
        rst = cut(16)

        at[0] = 8192
        carry = cut(H * 6 * B).rearrange("p (h w b) -> p h w b", h=H, w=6)

        at[0] = 0
        lg = cut(1024).rearrange("p (j t) -> p j t", j=4)
        ex = cut(1024).rearrange("p (j t) -> p j t", j=4)
        pm = cut(1024).rearrange("p (j t) -> p j t", j=4)
        rep = cut(1024).rearrange("p (j t) -> p j t", j=4)
        mo = cut(64)
        xtok = cut(2048).rearrange("p (g h n) -> p g h n", g=G, h=2)
        pmt = cut(1024).rearrange("p (j h n) -> p j h n", j=4, h=2)
        pool_ = cut(E * B).rearrange("p (e b) -> p e b", e=E)
        hid = cut(E * B).rearrange("p (e b) -> p e b", e=E)
        moT = cut(E * B)
        moB = cut(4 * C).rearrange("p (j o) -> p j o", o=C)
        moD = cut(4 * 256).rearrange("p (j m o) -> p j m o", j=4, m=8)

        ln_src = [lambda j: chunkQ(xQ, j), lambda j: flat(yb, j), lambda j: flat(xRf, j),
                  lambda j: chunkQ(xQ, j), lambda j: chunkQ(xQ, j), lambda j: flat(xRf, j),
                  lambda j: chunkQ(xQ, j), lambda j: flat(xRf, j), lambda j: chunkQ(xQ, j)]

        loads = []

        @block.sync
        def _(sp):
            for q in range(NQ):
                sp.dma_start(xN[C * q:C * q + C, :, :, :],
                             x.rearrange("(g q) (h v) w c -> q (h v w) g c", q=NQ, v=1)
                             [q].rearrange("(r k) g c -> r g k c", k=8)).then_inc(S("x_in"), 16)

            def load(name, dst, src):
                sp.dma_start(dst, src).then_inc(S(name), 16)

            sp.wait_ge(S("zeroed"), 1)
            load("w_stu", wm_raw[0:KF, :, :], d["L0_ffn_M_phi_plus"].rearrange("f k d e -> k f (d e)"))
            load("w_stu", wm_raw[32:32 + KF, :, :], d["L0_ffn_M_phi_minus"].rearrange("f k d e -> k f (d e)"))
            load("w_stu", wm_raw[64:64 + AR, :, :], d["L0_ffn_M_u"].rearrange("f i d e -> i f (d e)"))
            for k in range(2):
                load("w_stu", phi_rows[:, :, 32 * k:32 * k + KF],
                     d["L0_ffn_phi"][0:T, :].rearrange("(n p) k -> p n k", p=P))
                load("w_stu", sigma[32 * k:32 * k + KF, :], d["L0_ffn_sigma"].rearrange("(k o) -> k o", o=1))
            load("w_stu", lw[:, :], d["L0_ffn_log_weights"].rearrange("(o n) -> o n", o=1).to_broadcast([P, FRACS]))
            load("w_stu", gum[:, :], d["L0_ffn_gumbel"].rearrange("(o n) -> o n", o=1).to_broadcast([P, FRACS]))
            wqkv, wout = d["L0_conv_w_qkv"], d["L0_conv_w_out"]
            for q in range(NQ):
                rows = slice(C * q, C * q + C)
                load("w_attn", wq[rows, q, :], wqkv[:, 0:128])
                load("w_attn", wk[rows, q, :], wqkv[:, 128:256])
                load("w_attn", wv_rows[rows, :], wqkv[:, 256:384])
                load("w_attn", wo_bd[rows, C * q:C * q + C], wout[rows, :])
                load("w_attn", bout[rows, :], d["L0_conv_b_out"].rearrange("(c o) -> c o", o=1))
                load("w_attn", lnsc[rows, :], d["L0_conv_ln_scale"].rearrange("(c o) -> c o", o=1))
            for q in range(NQ):
                rows, c0 = slice(C * q, C * q + C), C * q
                load("w_tri", wa[rows, c0:c0 + CT], d["L1_conv_Wa1"])
                load("w_tri", wa[rows, c0 + CT:c0 + 2 * CT], d["L1_conv_Wa2"])
                load("w_tri", wb[rows, c0:c0 + CT], d["L1_conv_Wb1"])
                load("w_tri", wb[rows, c0 + CT:c0 + 2 * CT], d["L1_conv_Wb2"])
                load("w_tri", wg[rows, c0:c0 + C], d["L1_conv_Wg"])
                load("w_tri", bg[rows, :], d["L1_conv_bg"].rearrange("(c o) -> c o", o=1))
                load("w_tri", bz[rows, :], d["L1_conv_bz"].rearrange("(c o) -> c o", o=1))
                load("w_tri", wz_rows[:, q, :], d["L1_conv_Wz"])
            for n, name in enumerate(["ba1", "ba2", "bb1", "bb2"]):
                load("w_tri", ab_bias[:, n // 2, CT * (n % 2):CT * (n % 2) + CT],
                     d["L1_conv_" + name].rearrange("(o n) -> o n", o=1).to_broadcast([P, CT]))
            load("w_tri", b2[:, :], d["L1_conv_ln2_b"].rearrange("(c o) -> c o", o=1))
            for j in range(8):
                load("w_tri", wz[CT * j:CT * j + CT, j, :], d["L1_conv_Wz"])
                load("w_tri", g2[CT * j:CT * j + CT, :], d["L1_conv_ln2_g"].rearrange("(c o) -> c o", o=1))
            for i, L in enumerate(["L1_ffn_", "L3_ffn_"]):
                for q in range(NQ):
                    rows, c0 = slice(C * q, C * q + C), C * q
                    load(f"w_rnn{i}", rw[i][rows, c0:c0 + C], d[L + "W"])
                    load(f"w_rnn{i}", rv[i][rows, c0:c0 + C], d[L + "V"])
                    load(f"w_rnn{i}", rgam[i][rows, :], d[L + "gamma"].rearrange("(c o) -> c o", o=1))
                    load(f"w_rnn{i}", rbet[i][rows, :], d[L + "beta"].rearrange("(c o) -> c o", o=1))
                    load(f"w_scan{i}", taps[i][rows, :, :],
                         d[["L2_conv_W", "L3_conv_W"][i]].rearrange("k c o -> c k o"))
            for q in range(NQ):
                load("w_moe", gw_rows[C * q:C * q + E, C * q:C * q + C], d["L2_ffn_gate_w"])
            for q in range(8):
                load("w_moe", gb[E * q:E * q + E, :], d["L2_ffn_gate_b"].rearrange("(e o) -> e o", o=1))
            load("w_moe", w2b_rows[0:E, :], d["L2_ffn_weight2"][:, HID, :])

            sp.wait_ge(S("filt_done"), 1)
            sp.wait_ge(S("filt_done_a"), 1)
            for n in range(FRACS):
                for r in range(NQ):
                    sp.dma_start(toep[C * r:C * r + C, SEG_AT[n]:SEG_AT[n] + SEG_T[n], :],
                                 filt[C * n:C * n + C, AR - r:AR - r + SEG_T[n], :]).then_inc(S("toep_in"), 16)
            sp.wait_ge(S("stu_ps"), 1)
            load("w_moe", w1[:, :, :], d["L2_ffn_weight1"].rearrange("e d h -> d e h"))
            load("w_moe", w2[:, :, :], d["L2_ffn_weight2"][:, 0:HID, :].rearrange("e h o -> h e o"))
            for q in range(NQ):
                if q == 0:
                    sp.wait_ge(S("out_rows"), 1)
                sp.dma_start(out.rearrange("(g q) h w c -> q (h w) g c", q=NQ)[q]
                             .rearrange("(r k) g c -> r g k c", k=8),
                             xN[C * q:C * q + C, :, :, :]).then_inc(S("stored"), 16)
            sp.wait_ge(S("stored"), 16 * NQ)

        N_ATTN, N_STU, N_TRI = 16 * 24, 16 * 9, 16 * (32 + 4 + 1 + 16)
        N_RNN, N_SCAN, N_MOE = 16 * 16, 16 * 4, 16 * 15

        @block.gpsimd
        def _(pool):
            n = [0]

            def link(ins):
                n[0] += 1
                ins.then_inc(S("pool_step"), 1)
                pool.wait_ge(S("pool_step"), n[0])

            tiles = [wq, wk, wo_bd, wm_raw, phi_rows, wa, wb, wg, wz, rw[0], rw[1], rv[0], rv[1],
                     gw_rows, w2b_rows]
            for t in tiles:
                link(pool.memset(t[(slice(None),) * len(t.shape)], 0.0))
            link(pool.memset(sigma[:, :], 1.0))
            link(pool.memset(wvo[:, :, :], 0.0))
            link(pool.memset(band[0][:, :, :, :], 0.0))
            link(pool.memset(band[1][:, :, :, :], 0.0))
            link(pool.memset(filt[:, 0:AR, :], 0.0))
            link(pool.memset(ones[:, :], 1.0))
            for m in (mean32, ones32):
                link(pool.memset(m[:, :], 0.0))
            link(pool.memset(ident[:, :], 0.0))
            link(pool.affine_select(out=ident[:, :], in_=ident[:, :], compare_op=ALU.not_equal, fill=1.0, base=0,
                                    pattern=[[-1, P]], channel_multiplier=1))
            for q in range(NQ):
                rows = slice(C * q, C * q + C)
                link(pool.memset(mean32[rows, rows], 1.0 / C))
                link(pool.memset(ones32[rows, rows], 1.0))
            link(pool.memset(quarter[:, :], 0.0))
            for q in range(NQ):
                for p in range(NQ):
                    link(pool.tensor_scalar(quarter[C * q:C * q + C, C * p:C * p + C],
                                            ident[C * q:C * q + C, C * q:C * q + C], 0.25, None, ALU.mult))
            link(pool.memset(par16[:, :], 1.0))
            link(pool.affine_select(out=par16[:, :], in_=par16[:, :], compare_op=ALU.is_ge, fill=0.0, base=0,
                                    pattern=[[-16, 8]], channel_multiplier=1))
            link(pool.affine_select(out=par16[:, :], in_=par16[:, :], compare_op=ALU.is_ge, fill=0.0, base=15,
                                    pattern=[[16, 8]], channel_multiplier=-1))
            link(pool.memset(phi_rows[:, 0, 64:64 + AR], 0.0))
            pool.tensor_tensor(centre[:, :], ident[:, :], mean32[:, :], ALU.subtract).then_inc(S("zeroed"), 1)
            pool.wait_ge(S("zeroed"), 1)
            for i in range(2):
                pool.wait_ge(S(f"w_scan{i}"), N_SCAN)
                for rp in range(NQ):
                    rows = slice(C * rp, C * rp + C)
                    for r in range(NQ):
                        for dB in (-1, 0, 1):
                            k = 4 * dB + rp - r + 4
                            if 0 <= k < TAPS:
                                link(pool.tensor_copy(band[i][rows, dB + 1, r, :], taps[i][rows, k, :]))
                pool.sem_inc(S("band_done"), 1)

        @block.tensor
        def _(pe):
            mm = pe.matmul

            def full(ps, lhsT, rhs):
                return mm(ps, lhsT, rhs, start=True, stop=True)

            pe.wait_ge(S("w_attn"), N_ATTN)
            pe.wait_ge(S("zeroed"), 1)
            pe.transpose(bank[:, 7, 0:P], wv_rows[:, :], ident[:, :]).then_inc(S("wvt_ps"), 1)
            pe.wait_ge(S("wvt"), 1)
            full(bank[:, 6, 0:P], wv_t[:, :], wo_bd[:, :]).then_inc(S("wvo_ps"), 1)

            ln_pe(pe, 0, ln_src[0], lambda j: pe.wait_ge(S("xq_in"), j + 1))
            pe.wait_ge(S("wvo"), 1)

            pe.wait_ge(S("phi_ready"), 1)
            for n in range(2):
                last = pe.transpose(bank[:, 6, n * P:(n + 1) * P], phi_rows[:, n, :], ident[:, :])
            last.then_inc(S("phi_tr"), 1)
            pe.wait_ge(S("phi_cols"), 1)
            pe.wait_ge(S("wm_seg"), 1)
            for e in range(C):
                if e % 2 == 0 and e >= 4:
                    pe.wait_ge(S("filt_a" if (e // 2) % 2 else "filt_v"), (e // 2 - 2) // 2 + 1)
                last = full(bank[:, 4 + (e // 2) % 2, (e % 2) * T:(e % 2 + 1) * T],
                            wm_raw.rearrange("p f (d e) -> p (f d) e", e=C)[:, :, e],
                            phi_cols[:, :, :])
                if e % 2:
                    last.then_inc(S("filt_ps"), 1)

            def attn_proj(u):
                j, q = divmod(u, NQ)
                pe.wait_ge(S("ln_applied"), j + 1)
                if u == 0:
                    pe.wait_ge(S("ln_applied"), CH)
                    pe.wait_ge(S("filt_done"), 1)
                    pe.wait_ge(S("filt_done_a"), 1)
                if u >= 2:
                    pe.wait_ge(S("k_exp"), u - 1)
                full(bank[:, u % 2, :], wk[:, q, :], flat(xn, j)).then_inc(S("k_ps"), 1)
                if u >= 1:
                    pe.wait_ge(S("q_shift"), u)
                full(bank[:, 2, :], wq[:, q, :], flat(xn, j)).then_inc(S("q_ps"), 1)
                if u >= 1:
                    pe.wait_ge(S("v_sb"), u)
                for i in range(4):
                    last = full(bank[:, 4, i * P:(i + 1) * P], xn[:, j * CW_ + i * P:j * CW_ + (i + 1) * P],
                                wvo[:, q, :])
                last.then_inc(S("v_ps"), 1)

            def attn_mid(u):
                pe.wait_ge(S("k_exp"), u + 1)
                if u >= 1:
                    pe.wait_ge(S("k_rows"), u)
                for i in range(4):
                    last = pe.transpose(bank[:, 3, i * P:(i + 1) * P], kE[:, u % 2, i * P:(i + 1) * P], ident[:, :])
                last.then_inc(S("k_tr"), 1)
                pe.wait_ge(S("q_exp"), u + 1)
                if u >= 1:
                    pe.wait_ge(S("q_norm"), u)
                full(bank[:, 5, :], ones32[:, :], qe[:, u % 2, :]).then_inc(S("q_sum"), 1)

            def attn_ctx(u):
                pe.wait_ge(S("k_rows"), u + 1)
                pe.wait_ge(S("v_sb"), u + 1)
                if u >= 1:
                    pe.wait_ge(S("ctx_sb"), u)
                for g in range(2):
                    for h in range(2):
                        i = 2 * g + h
                        last = mm(bank[:, 6, g * P:(g + 1) * P], kN[:, u % 2, i * P:(i + 1) * P],
                                  vo[:, u % 2, i * P:(i + 1) * P], start=(h == 0), stop=(h == 1))
                last.then_inc(S("ctx_ps"), 1)

            def attn_out(u):
                j, q = divmod(u, NQ)
                pe.wait_ge(S("ctx_sb"), u + 1)
                pe.wait_ge(S("q_norm"), u + 1)
                if j >= 1:
                    pe.wait_ge(S("attn_y"), j)
                for g in range(2):
                    last = full(bank[C * q:C * q + C, 7, g * T:(g + 1) * T], cwt[:, u % 3, g, :],
                                qn[:, u % 3, g * T:(g + 1) * T])
                last.then_inc(S("attn_ps"), 1)

            for i in range(U + 3):
                if i < U:
                    attn_proj(i)
                if 0 <= i - 1 < U:
                    attn_mid(i - 1)
                if 0 <= i - 2 < U:
                    attn_ctx(i - 2)
                if 0 <= i - 3 < U:
                    attn_out(i - 3)
            ln_pe(pe, 1, ln_src[1], lambda j: pe.wait_ge(S("attn_y"), CH))

            pe.wait_ge(S("xr_v"), 1)
            pe.wait_ge(S("xr_a"), 1)
            ln_pe(pe, 2, ln_src[2], lambda j: None)
            pe.wait_ge(S("toep_in"), 16 * FRACS * NQ)
            pe.wait_ge(S("ln_applied"), 3 * CH)
            pe.wait_ge(S("filt_done"), 1)
            pe.wait_ge(S("filt_done_a"), 1)
            for seg, lo, hi in ((3, 0, 8), (2, 8, 16), (1, 16, 32), (0, 32, 48), (0, 48, 64)):
                for m in range(hi):
                    t0 = max(lo, m)
                    lhs = toep[:, SEG_AT[seg] + 4 * m:SEG_AT[seg] + 4 * m + 4, :]
                    last = mm(bank[:, 4 + lo // 16, (t0 % 16) * B:(t0 % 16 + hi - t0) * B], lhs,
                              xn[:, (t0 - m) * B:(hi - m) * B], start=(m == 0 and seg != 2), stop=(m == hi - 1),
                              skip_group_check=(seg >= 2))
            last.then_inc(S("stu_ps"), 1)

            ln_pe(pe, 3, ln_src[3], lambda j: pe.wait_ge(S("x_stu"), 1))
            pe.wait_ge(S("w_tri"), N_TRI)
            pe.wait_ge(S("ln_applied"), 4 * CH)
            for k in range(2):
                for m in range(16):
                    cols = (xnH[:, m, :, :].rearrange("p g w -> p (g w)") if k == 0
                            else xnQ.rearrange("p g (h w) -> p (g h) w", w=W)[:, :, m])
                    last = full(bank[:, 4 * k + m // 4, (m % 4) * P:(m % 4 + 1) * P], cols, [wa, wb][k][:, :])
                last.then_inc(S("ab_ps"), 1)
            pe.wait_ge(S("a_pre"), 1)
            for j in range(CH):
                last = full(bank[:, j, :], wg[:, :], flat(xn, j))
            last.then_inc(S("gate_ps"), 1)
            pe.wait_ge(S("b_pre"), 1)
            pe.wait_ge(S("a_bd"), 1)
            pe.wait_ge(S("b_s"), 1)
            for m in range(64):
                last = full(bank[:, 4 + m // 32, (m % 32) * 16:(m % 32 + 1) * 16],
                            a_bd[:, m, :, :], b_s[:, m * 16:(m + 1) * 16])
            last.then_inc(S("z_ps"), 1)
            full(bank[:, 6, 0:1], wz_rows[:, :, :], b2[:, :]).then_inc(S("bz_ps"), 1)
            pe.wait_ge(S("z_n"), 1)
            pe.wait_ge(S("bz2"), 1)
            for m in range(8):
                last = pe.transpose(bank[:, 6 + m // 4, (m % 4) * P:(m % 4 + 1) * P], zn[:, m * P:(m + 1) * P],
                                    ident[:, :])
            last.then_inc(S("z_tr"), 1)
            pe.wait_ge(S("z_t"), 1)
            pe.wait_ge(S("wz_g"), 1)
            pe.wait_ge(S("gate"), 1)
            for jj in range(16):
                for q in range(NQ):
                    last = full(bank[C * q:C * q + C, jj // 4, (jj % 4) * P:(jj % 4 + 1) * P], wz[:, jj % 8, :],
                                zT[:, (2 * q + jj // 8) * P:(2 * q + jj // 8 + 1) * P])
            last.then_inc(S("tri_ps"), 1)

            def rnn(i, k):
                ln_pe(pe, k, ln_src[k], lambda j: pe.wait_ge(S(["x_tri", "x_scan1"][i]), 1))
                pe.wait_ge(S("rnn_w"), i + 1)
                for j in range(CH):
                    pe.wait_ge(S("ln_applied"), CH * k + j + 1)
                    full(bank[:, 4 + j, :], rwt[i][:, :], flat(xn, j)).then_inc(S("wx_ps"), 1)
                pe.wait_ge(S("bn_mean_in"), i + 1)
                full(bank[:, 0, 0:1], quarter[:, :], mv[:, 0:1]).then_inc(S("bn_mean"), 1)
                pe.wait_ge(S("bn_var_in"), i + 1)
                full(bank[:, 1, 0:1], quarter[:, :], rst[:, 2:3]).then_inc(S("bn_var"), 1)
                for n in range(SWEEPS):
                    for j in range(CH):
                        if n == 0:
                            pe.wait_ge(S("z_in"), CH * i + j + 1)
                        else:
                            pe.wait_ge(S(f"sweep_y{i}"), CH * (n - 1) + j + 1)
                        full(bank[:, 4 + j, :], rvt[i][:, :], yS[:, 2 * j:2 * j + 2, 0:T])\
                            .then_inc(S(f"sweep_ps{i}"), 1)
                pe.wait_ge(S("settled_rows"), i + 1)
                full(bank[0:1, 2, 0:1], moved[:, CH + 1:CH + 2], ones[:, 0:1]).then_inc(S("settled_sum"), 1)
                pe.wait_ge(S("verdict"), i + 1)
                by_steps = pe.value_load(unsettled[0:1, i:i + 1], min_val=0, max_val=1)
                zt = zs.rearrange("p (g t) -> p g t", g=G)
                with pe.If(by_steps != 0):
                    with pe.Fori(0, T // 2) as t2:
                        for k2 in range(2):
                            mm(bank[:, 2 + k2, 0:G], ident[:, :], zt[:, :, bass.ds(t2 * 2 + k2, 1)], start=True, stop=False)
                            pe.wait_ge(S(f"y_step{i}"), t2 * 2 + (k2 + 1))
                            mm(bank[:, 2 + k2, 0:G], rvt[i][:, :], yF[:, :, bass.ds(t2 * 2 + k2, 1)],
                               start=False, stop=True).then_inc(S(f"v_step{i}"), 1)

            def scan(i, k):
                pe.wait_ge(S("xr_v"), 2 + i)
                pe.wait_ge(S("xr_a"), 2 + i)
                ln_pe(pe, k, ln_src[k], lambda j: None)
                pe.wait_ge(S("band_done"), i + 1)
                for h in range(1, H):
                    n = (H - 1) * i + h - 1
                    pe.wait_ge(S("row_done"), H * i + h)
                    for w in range(3):
                        last = mm(bank[:, 4 + h % 2, 0:P], band[i][:, w, :, :], carry[:, h - 1, w:w + 4, :],
                                  start=(w == 0), stop=(w == 2))
                    last.then_inc(S("row_ps"), 1)

            def experts():
                ln_pe(pe, 6, ln_src[6], lambda j: pe.wait_ge(S("x_scan0"), 1))
                pe.wait_ge(S("gw"), 1)
                for j in range(4):
                    pe.wait_ge(S("ln_applied"), CH * 6 + j + 1)
                    for gg in range(2):
                        last = full(bank[64 * gg:64 * gg + 64, 4 + j // 2, (j % 2) * T:(j % 2 + 1) * T],
                                    gwc[:, :], xnQ[:, 2 * j + gg, :])
                last.then_inc(S("gate_l"), 1)
                pe.wait_ge(S("ln_applied"), CH * 7)
                for g in range(G):
                    for h in range(2):
                        m = 2 * g + h
                        last = pe.transpose(bank[:, m // 4, (m % 4) * P:(m % 4 + 1) * P],
                                            xnQ[:, g, h * P:(h + 1) * P], ident[:, :])
                last.then_inc(S("xtok_ps"), 1)
                pe.wait_ge(S("pm"), 1)
                for j in range(4):
                    for h in range(2):
                        m = 2 * j + h
                        last = pe.transpose(bank[:, 6 + m // 4, (m % 4) * P:(m % 4 + 1) * P],
                                            pm[:, j, h * P:(h + 1) * P], ident[:, :])
                last.then_inc(S("pmt_ps"), 1)
                pe.wait_ge(S("xtok"), 1)
                pe.wait_ge(S("pmt"), 1)
                for g in range(G):
                    for h in range(2):
                        last = mm(bank[:, 0, g * 64:(g + 1) * 64], xtok[:, g, h, :],
                                  pmt[:, g // 2, h, 64 * (g % 2):64 * (g % 2) + 64], start=(h == 0), stop=(h == 1))
                last.then_inc(S("pool_ps"), 1)
                pe.wait_ge(S("pooled"), 1)
                pe.wait_ge(S("w_moe"), N_MOE)
                for e in range(E):
                    last = full(bank[:, 1, e * B:(e + 1) * B], w1[:, e, :], pool_[0:C + 1, e, :])
                last.then_inc(S("hid_ps"), 1)
                pe.wait_ge(S("hid"), 1)
                for e in range(E):
                    last = full(bank[0:C, 2, e * B:(e + 1) * B], w2[:, e, :], hid[:, e, :])
                last.then_inc(S("eo_ps"), 1)
                pe.wait_ge(S("eo_bd"), 1)
                for g in range(G):
                    last = full(bank[:, 4 + g // 2, (g % 2) * T:(g % 2 + 1) * T],
                                moD[:, g // 2, 4 * (g % 2):4 * (g % 2) + 4, :], pm[:, g // 2, :])
                last.then_inc(S("moe_ps"), 1)

            rnn(0, 4)
            scan(0, 5)
            experts()
            scan(1, 7)
            rnn(1, 8)

        @block.scalar
        def _(act):
            n = [0]

            def link(ins):
                n[0] += 1
                ins.then_inc(S("act_step"), 1)
                act.wait_ge(S("act_step"), n[0])

            def lnexp():
                act.preload_act_table_set("natural_log_exp_and_others")

            lnexp()
            act.wait_ge(S("wvt_ps"), 1)
            act.activation(wv_t[:, :], bank[:, 7, 0:P], ACT.Copy).then_inc(S("wvt"), 1)
            act.wait_ge(S("wvo_ps"), 1)
            for q in range(NQ):
                rows = slice(C * q, C * q + C)
                last = act.activation(wvo[rows, q, :], bank[rows, 6, 0:P], ACT.Copy)
            last.then_inc(S("wvo"), 1)
            ln_act(act, 0)

            act.wait_ge(S("fw_z"), 1)
            act.activation(fw[:, 1, :], fw[:, 0, :], ACT.Exp, bias=fw[:, 2, 0:1], accum_out=fw[:, 2, 1:2])\
                .then_inc(S("fw_exp"), 1)
            act.wait_ge(S("w_stu"), N_STU)
            link(act.activation(sig4[0:64, :], sigma[0:64, :], ACT.Ln))
            link(act.activation(sig4[0:64, :], sig4[0:64, :], ACT.Exp, scale=0.25))
            act.activation(nsig4[0:64, :], sig4[0:64, :], ACT.Copy, scale=-1.0).then_inc(S("sig4"), 1)
            for m in range(1, 16, 2):
                act.wait_ge(S("filt_ps"), m + 1)
                act.activation(filt[:, AR:, 2 * m:2 * m + 2].rearrange("p t e -> p e t"),
                               bank[:, 4 + m % 2, :].rearrange("p (e t) -> p e t", e=2), ACT.Copy)\
                    .then_inc(S("filt_a") if m < 15 else S("filt_done_a"), 1)
            def a_k(u):
                act.wait_ge(S("k_max"), u + 1)
                if u >= 2:
                    act.wait_ge(S("k_tr"), u - 1)
                for g in range(2):
                    last = act.activation(kE[:, u % 2, g * T:(g + 1) * T], bank[:, u % 2, g * T:(g + 1) * T], ACT.Exp,
                                          bias=nkm[:, 2 * u + g:2 * u + g + 1],
                                          accum_out=kz[:, 2 * u + g:2 * u + g + 1])
                last.then_inc(S("k_exp"), 1)

            def a_v(u):
                act.wait_ge(S("v_ps"), u + 1)
                if u >= 2:
                    act.wait_ge(S("ctx_ps"), u - 1)
                act.activation(vo[:, u % 2, :], bank[:, 4, :], ACT.Copy).then_inc(S("v_sb"), 1)

            def a_q(u):
                act.wait_ge(S("q_shift"), u + 1)
                if u >= 2:
                    act.wait_ge(S("q_norm"), u - 1)
                act.activation(qe[:, u % 2, :], qs[:, u % 2, :], ACT.Exp).then_inc(S("q_exp"), 1)

            def a_z(u):
                act.wait_ge(S("q_sum"), u + 1)
                act.activation(lz[:, u % 2, :], bank[:, 5, :], ACT.Ln).then_inc(S("q_log"), 1)
                act.wait_ge(S("q_log"), u + 1)
                act.activation(bank[:, 5, :], lz[:, u % 2, :], ACT.Exp, scale=-1.0).then_inc(S("q_rz"), 1)

            def a_y(j):
                act.wait_ge(S("attn_ps"), NQ * (j + 1))
                act.activation(flat(yb, j), bank[:, 7, :], ACT.Identity, bias=bout[:, :]).then_inc(S("attn_y"), 1)

            for i in range(U + 3):
                if i < U:
                    a_k(i)
                    a_v(i)
                    a_q(i)
                if 0 <= i - 1 < U:
                    a_z(i - 1)
                if i >= 3 and (i - 3) % NQ == NQ - 1:
                    a_y((i - 3) // NQ)
            ln_act(act, 1)

            def evens_to_r(k, dep, v):
                act.wait_ge(S(dep), v)
                for q in range(NQ):
                    for r in (0, 2):
                        last = act.activation(
                            xR[C * r:C * r + C, :, q:B:NQ].rearrange("p t g -> p g t"),
                            xQ[C * q:C * q + C, :, r:T:NQ], ACT.Copy)
                last.then_inc(S("xr_a"), 1)

            evens_to_r(0, "x_attn", CH)
            ln_act(act, 2)
            ln_act(act, 3)

            def sigmoids():
                act.preload_act_table_set("sigmoid_and_others")

            sigmoids()
            act.wait_ge(S("a_in"), 1)
            act.activation(a_s[:, :], a_in[:, :].rearrange("p (h m) -> p m h", h=16), ACT.Sigmoid).then_inc(S("a_s"), 1)
            act.wait_ge(S("gate_ps"), 1)
            act.activation(gate[:, :], bank[:, 0:4, :], ACT.Sigmoid, bias=bg[:, :]).then_inc(S("gate"), 1)
            act.wait_ge(S("b_in"), 1)
            act.activation(b_s[:, :], a_in[:, :].rearrange("p (h m) -> p m h", h=16), ACT.Sigmoid).then_inc(S("b_s"), 1)
            lnexp()
            act.wait_ge(S("z_c"), 1)
            act.activation(zq[:, :], zc[:, :], ACT.Square).then_inc(S("z_sq"), 1)
            act.wait_ge(S("z_var"), 1)
            link(act.activation(zst[:, 2, :], zst[:, 1, :], ACT.Ln, bias=LN_TOK, scale=1.0 / CT))
            act.activation(zst[:, 3, :], zst[:, 2, :], ACT.Exp, scale=-0.5).then_inc(S("z_rstd"), 1)
            act.wait_ge(S("z_tr"), 1)
            act.activation(zT[:, :], bank[:, 6:8, :], ACT.Copy).then_inc(S("z_t"), 1)

            def rnn(i, k):
                ln_act(act, k)
                act.wait_ge(S("bn_v"), i + 1)
                link(act.activation(rst[:, 5:6], rst[:, 4:5], ACT.Ln, bias=LN_TOK))
                act.activation(rst[:, 6:7], rst[:, 5:6], ACT.Exp, scale=-0.5).then_inc(S("bn_rstd"), 1)
                sigmoids()
                for n in range(SWEEPS):
                    y = yF if n == SWEEPS - 1 else yS
                    for j in range(CH):
                        act.wait_ge(S(f"sweep_pre{i}"), CH * n + j + 1)
                        act.activation(y[:, 2 * j:2 * j + 2, 1:T + 1], pre[:, j, :].rearrange("p (g t) -> p g t", g=2),
                                       ACT.Sigmoid).then_inc(S(f"sweep_y{i}"), 1)
                act.wait_ge(S("verdict"), i + 1)
                by_steps = act.value_load(unsettled[0:1, i:i + 1], min_val=0, max_val=1)
                with act.If(by_steps != 0):
                    act.sem_inc(S(f"y_step{i}"), 1)
                    with act.Fori(0, T // 2) as t2:
                        for k2 in range(2):
                            act.wait_ge(S(f"v_step{i}"), t2 * 2 + (k2 + 1))
                            act.activation(yF[:, :, bass.ds(t2 * 2 + (k2 + 1), 1)], bank[:, 2 + k2, 0:G],
                                           ACT.Sigmoid).then_inc(S(f"y_step{i}"), 1)
                    act.wait_ge(S(f"y_step{i}"), T + 1)
                act.sem_inc(S("y_final"), 1)
                lnexp()

            rnn(0, 4)
            evens_to_r(1, "x_rnn0", 1)
            ln_act(act, 5)
            ln_act(act, 6)
            for j in range(4):
                act.wait_ge(S("moe_max"), j + 1)
                act.activation(ex[:, j, :], lg[:, j, :], ACT.Exp, bias=mo[:, j:j + 1], accum_out=mo[:, 4 + j:5 + j])\
                    .then_inc(S("moe_exp"), 1)
            act.wait_ge(S("xtok_ps"), 1)
            act.activation(xtok.rearrange("p g h n -> p (g h n)"), bank[:, 0:4, :].rearrange("p k n -> p (k n)"), ACT.Copy).then_inc(S("xtok"), 1)
            act.preload_act_table_set("gelu_and_others")
            act.wait_ge(S("hid_ps"), 1)
            act.activation(hid.rearrange("p e b -> p (e b)"), bank[:, 1, :], ACT.Gelu).then_inc(S("hid"), 1)
            lnexp()
            evens_to_r(2, "x_moe", 1)
            ln_act(act, 7)
            rnn(1, 8)

        @block.vector
        def _(dve):
            n = [0]

            def link(ins):
                n[0] += 1
                ins.then_inc(S("dve_step"), 1)
                dve.wait_ge(S("dve_step"), n[0])

            dve.wait_ge(S("x_in"), 16 * NQ)
            for g in range(G):
                last = dve.transpose(xQ[:, g, :].rearrange("p (r k) -> p k r", k=8), xN[:, g, :, :])
                if g % 2:
                    last.then_inc(S("xq_in"), 1)
            ln_dve(dve, 0)
            dve.wait_ge(S("w_stu"), N_STU)
            link(dve.tensor_tensor(fw[:, 0, :], lw[:, :], gum[:, :], ALU.add))
            dve.tensor_reduce(out=fw[:, 2, 0:1], in_=fw[:, 0, :], axis=AX, op=ALU.max, negate=True).then_inc(S("fw_z"), 1)
            dve.wait_ge(S("fw_exp"), 1)
            link(dve.reciprocal(fw[:, 2, 2:3], fw[:, 2, 1:2]))
            link(dve.tensor_scalar(fw[:, 3, :], fw[:, 1, :], fw[:, 2, 2:3], None, ALU.mult))
            link(dve.tensor_reduce(out=fw[:, 2, 3:4], in_=fw[:, 3, :], axis=AX, op=ALU.max))
            link(dve.tensor_scalar(fw[:, 4, :], fw[:, 3, :], fw[:, 2, 3:4], None, ALU.is_equal))
            link(dve.memset(fw[:, 5, :], 0.0))
            for f in range(1, FRACS):
                link(dve.tensor_tensor(fw[:, 5, f:f + 1], fw[:, 5, f - 1:f], fw[:, 4, f - 1:f], ALU.max))
            link(dve.tensor_tensor(fw[:, 4, :], fw[:, 4, :], fw[:, 5, :], ALU.is_gt))
            link(dve.tensor_tensor(fw[:, 6, :], fw[:, 4, :], fw[:, 3, :], ALU.subtract))
            link(dve.tensor_tensor(fw[:, 7, :], fw[:, 6, :], fw[:, 3, :], ALU.add))
            for n_ in range(FRACS):
                m = wm_raw[:, n_, :]
                if n_ == 0:
                    link(dve.tensor_scalar(m, m, fw[:, 7, 0:1], None, ALU.mult))
                else:
                    ins = dve.scalar_tensor_tensor(out=m, in0=m, scalar=fw[:, 7, n_:n_ + 1], in1=wm_raw[:, n_ - 1, :],
                                                   op0=ALU.mult, op1=ALU.add)
                    if n_ < FRACS - 1:
                        link(ins)
                    else:
                        ins.then_inc(S("wm_seg"), 1)
            dve.tensor_copy(phi_rows[:, 0, 64:64 + AR], ident[:, 0:AR]).then_inc(S("phi_ready"), 1)
            dve.wait_ge(S("phi_tr"), 1)
            dve.wait_ge(S("sig4"), 1)
            pt = bank[:, 6, 0:T].rearrange("p (n t) -> p n t", n=2)
            dve.tensor_scalar(phi_cols[0:32, :, :], pt[0:32, :, :], sig4[0:32, :], None, ALU.mult)
            dve.tensor_scalar(phi_cols[32:64, :, 0:P:2], pt[32:64, :, 0:P:2], sig4[32:64, :], None, ALU.mult)
            dve.tensor_scalar(phi_cols[32:64, :, 1:P:2], pt[32:64, :, 1:P:2], nsig4[32:64, :], None, ALU.mult)
            dve.tensor_copy(phi_cols[64:128, :, :], pt[64:128, :, :]).then_inc(S("phi_cols"), 1)
            for m in range(0, 16, 2):
                dve.wait_ge(S("filt_ps"), m + 1)
                dve.tensor_copy(filt[:, AR:, 2 * m:2 * m + 2].rearrange("p t e -> p e t"),
                                bank[:, 4 + m % 2, :].rearrange("p (e t) -> p e t", e=2))\
                    .then_inc(S("filt_v") if m < 14 else S("filt_done"), 1)


            def v_k(u):
                dve.wait_ge(S("k_ps"), u + 1)
                dve.tensor_reduce(out=nkm[:, 2 * u:2 * u + 2],
                                  in_=bank[:, u % 2, :].rearrange("p (g t) -> p g t", g=2),
                                  axis=AX, op=ALU.max, negate=True).then_inc(S("k_max"), 1)

            def v_q(u):
                dve.wait_ge(S("q_ps"), u + 1)
                link(dve.tensor_reduce(out=qm[:, u % 2, :], in_=bank[:, 2, :].rearrange("p (k r) -> p k r", r=32),
                                       axis=AX, op=ALU.max, negate=True, apply_transpose=True))
                link(dve.transpose(qb[:, u % 2, :].rearrange("p (k r) -> p k r", r=32),
                                   qm[:, u % 2, :].rearrange("p (k o) -> p k o", o=1).to_broadcast([P, 16, 32])))
                if u >= 2:
                    dve.wait_ge(S("q_exp"), u - 1)
                dve.tensor_tensor(qs[:, u % 2, :], bank[:, 2, :], qb[:, u % 2, :], ALU.add).then_inc(S("q_shift"), 1)

            def v_kn(u):
                dve.wait_ge(S("k_tr"), u + 1)
                if u >= 2:
                    dve.wait_ge(S("ctx_ps"), u - 1)
                dve.tensor_copy(kN[:, u % 2, :], bank[:, 3, :]).then_inc(S("k_rows"), 1)

            def v_qn(u):
                dve.wait_ge(S("q_rz"), u + 1)
                if u >= 3:
                    dve.wait_ge(S("attn_ps"), u - 2)
                dve.tensor_tensor(qn[:, u % 3, :], qe[:, u % 2, :], bank[:, 5, :], ALU.mult).then_inc(S("q_norm"), 1)

            def v_ctx(u):
                link(dve.reciprocal(rkz[:, 2 * u:2 * u + 2], kz[:, 2 * u:2 * u + 2]))
                dve.wait_ge(S("ctx_ps"), u + 1)
                if u >= 3:
                    dve.wait_ge(S("attn_ps"), u - 2)
                for h in range(HEADS):
                    rows = slice(C * h, C * h + C)
                    for g in range(2):
                        last = dve.tensor_scalar(cwt[rows, u % 3, g, :], bank[rows, 6, g * P + C * h:g * P + C * h + C],
                                                 rkz[rows, 2 * u + g:2 * u + g + 1], DH ** -0.5 / T, ALU.mult, ALU.mult)
                last.then_inc(S("ctx_sb"), 1)

            for i in range(U + 2):
                if i < U:
                    v_k(i)
                    v_q(i)
                if 0 <= i - 1 < U:
                    v_kn(i - 1)
                    v_qn(i - 1)
                if 0 <= i - 2 < U:
                    v_ctx(i - 2)

            def attn_apply(j, i):
                dve.tensor_tensor(flat(xn, j), bank[:, i % 2, :], rs[:, i % 2, :], ALU.mult).then_inc(S("ln_applied"), 1)
                dve.wait_ge(S("ln_applied"), i + 1)
                dve.scalar_tensor_tensor(out=flat(xQf, j), in0=flat(xn, j), scalar=lnsc[:, :],
                                         in1=flat(xQf, j), op0=ALU.mult, op1=ALU.add).then_inc(S("x_attn"), 1)

            ln_dve(dve, 1, attn_apply)

            def odds_to_r(dep, v):
                dve.wait_ge(S(dep), v)
                for q in range(NQ):
                    for r in (1, 3):
                        last = dve.tensor_copy(xR[C * r:C * r + C, :, q:B:NQ].rearrange("p t g -> p g t"),
                                               xQ[C * q:C * q + C, :, r:T:NQ])
                last.then_inc(S("xr_v"), 1)

            odds_to_r("x_attn", CH)
            ln_dve(dve, 2)
            dve.wait_ge(S("stu_ps"), 1)
            dve.wait_ge(S("xr_a"), 1)
            stu = bank[:, 4:8, :].rearrange("p k (t b) -> p (k t) b", b=B)
            for q in range(NQ):
                for r in range(NQ):
                    xs = xQ[C * q:C * q + C, :, r:T:NQ]
                    last = dve.tensor_tensor(xs, stu[C * r:C * r + C, :, q:B:NQ].rearrange("p t g -> p g t"), xs,
                                             ALU.add)
            last.then_inc(S("x_stu"), 1)

            def twice(j, i):
                h4 = xnH[:, :, 2 * j:2 * j + 2, :].rearrange("p h g w -> p g h w")
                for out_ in (chunkQ(xnQ, j).rearrange("p g (h w) -> p g h w", w=W), h4):
                    last = dve.tensor_tensor(out_, bank[:, i % 2, :].rearrange("p (g h w) -> p g h w", g=2, w=W),
                                             rs[:, i % 2, :].rearrange("p (g h w) -> p g h w", g=2, w=W), ALU.mult)
                last.then_inc(S("ln_applied"), 1)

            ln_dve(dve, 3, twice)
            dve.wait_ge(S("w_tri"), N_TRI)
            for k in range(2):
                dve.wait_ge(S("ab_ps"), k + 1)
                pre4 = ab_pre.rearrange("p (m n) -> p m n", n=2 * CT)
                dve.tensor_tensor(pre4, bank[:, 4 * k:4 * k + 4, :].rearrange("p k (m n) -> p (k m) n", n=2 * CT),
                                  ab_bias[:, k:k + 1, :].to_broadcast([P, 64, 2 * CT]), ALU.add)\
                    .then_inc(S(["a_pre", "b_pre"][k]), 1)
                dve.wait_ge(S(["a_pre", "b_pre"][k]), 1)
                if k:
                    dve.wait_ge(S("a_s"), 1)
                dve.tensor_tensor(a_in.rearrange("p (m c) -> p m c", c=CT), pre4[:, :, 0:CT], pre4[:, :, CT:2 * CT],
                                  ALU.mult).then_inc(S(["a_in", "b_in"][k]), 1)
                if k == 0:
                    dve.wait_ge(S("a_s"), 1)
                    for g in range(8):
                        last = dve.tensor_scalar(a_bd[:, :, g, :], a_s.rearrange("p (m i) -> p m i", i=16),
                                                 par16[:, g:g + 1], None, ALU.mult)
                    last.then_inc(S("a_bd"), 1)
            dve.wait_ge(S("z_ps"), 1)
            zp = bank[:, 4:6, :].rearrange("p k n -> p (k n)").rearrange("p (q c j) -> p q j c", q=NQ, c=CT)
            z4 = [a.rearrange("p (q j c) -> p q j c", q=NQ, j=16) for a in (zc, zq, zn)]
            link(dve.tensor_reduce(out=zst[:, 0, :], in_=zp, axis=AX, op=ALU.add))
            link(dve.tensor_scalar(zst[:, 0, :], zst[:, 0, :], -1.0 / CT, None, ALU.mult))
            zm = zst[:, 0, :].rearrange("p (q j o) -> p q j o", q=NQ, o=1).to_broadcast([P, NQ, 16, CT])
            dve.tensor_tensor(z4[0], zp, zm, ALU.add).then_inc(S("z_c"), 1)
            dve.wait_ge(S("bz_ps"), 1)
            dve.tensor_tensor(bz2[:, :], bank[:, 6, 0:1], bz[:, :], ALU.add).then_inc(S("bz2"), 1)
            dve.tensor_scalar(wz[:, :, :], wz[:, :, :], g2[:, :], None, ALU.mult).then_inc(S("wz_g"), 1)
            dve.wait_ge(S("z_sq"), 1)
            dve.tensor_reduce(out=zst[:, 1, :], in_=z4[1], axis=AX, op=ALU.add).then_inc(S("z_var"), 1)
            dve.wait_ge(S("z_rstd"), 1)
            zr = zst[:, 3, :].rearrange("p (m o) -> p m o", o=1).to_broadcast([P, 64, CT])
            dve.wait_ge(S("z_c"), 1)
            dve.tensor_tensor(zn.rearrange("p (m c) -> p m c", c=CT), zc.rearrange("p (m c) -> p m c", c=CT), zr,
                              ALU.mult).then_inc(S("z_n"), 1)
            dve.wait_ge(S("tri_ps"), 1)
            dve.wait_ge(S("gate"), 1)
            dve.wait_ge(S("bz2"), 1)
            link(dve.scalar_tensor_tensor(
                out=upd.rearrange("p (n j) -> p n j", j=16),
                in0=bank[:, 0:4, :].rearrange("p k n -> p (k n)").rearrange("p (j n) -> p n j", j=16),
                scalar=bz2[:, :], in1=gate.rearrange("p (n j) -> p n j", j=16), op0=ALU.add, op1=ALU.mult))
            dve.tensor_tensor(xQf, xQf, upd, ALU.add).then_inc(S("x_tri"), 1)

            def rnn(i, k):
                dve.wait_ge(S(f"w_rnn{i}"), N_RNN)
                dve.transpose(rwt[i][:, :].rearrange("p (k r) -> p k r", r=32), rw[i][:, :].rearrange("p (k r) -> p k r", r=32))
                dve.transpose(rvt[i][:, :].rearrange("p (k r) -> p k r", r=32), rv[i][:, :].rearrange("p (k r) -> p k r", r=32)).then_inc(S("rnn_w"), 1)
                ln_dve(dve, k)
                for j in range(CH):
                    dve.wait_ge(S("wx_ps"), CH * i + j + 1)
                    link(dve.bn_stats(out=bst[:, j, :], in_=bank[:, 4 + j, :]))
                dve.bn_aggr(out=mv[:, :], in_=bst[:, :, :]).then_inc(S("bn_mean_in"), 1)
                dve.wait_ge(S("bn_mean_in"), i + 1)
                dve.wait_ge(S("bn_mean"), i + 1)
                link(dve.tensor_copy(rst[:, 0:1], bank[:, 0, 0:1]))
                link(dve.tensor_tensor(rst[:, 1:2], mv[:, 0:1], rst[:, 0:1], ALU.subtract))
                link(dve.tensor_tensor(rst[:, 3:4], rst[:, 1:2], rst[:, 1:2], ALU.mult))
                dve.tensor_tensor(rst[:, 2:3], rst[:, 3:4], mv[:, 1:2], ALU.add).then_inc(S("bn_var_in"), 1)
                dve.wait_ge(S("bn_var"), i + 1)
                dve.tensor_copy(rst[:, 4:5], bank[:, 1, 0:1]).then_inc(S("bn_v"), 1)
                dve.wait_ge(S("bn_rstd"), i + 1)
                link(dve.tensor_tensor(rst[:, 7:8], rst[:, 6:7], rgam[i][:, :], ALU.mult))
                link(dve.tensor_tensor(rst[:, 8:9], rst[:, 7:8], rst[:, 0:1], ALU.mult))
                link(dve.tensor_tensor(rst[:, 9:10], rbet[i][:, :], rst[:, 8:9], ALU.subtract))
                dve.memset(yS[:, :, 1:T + 1], 0.5)
                dve.memset(yS[:, :, 0:1], 0.0)
                dve.memset(yF[:, :, 0:1], 0.0)
                for j in range(CH):
                    dve.tensor_scalar(flat(zs, j), bank[:, 4 + j, :], rst[:, 7:8], rst[:, 9:10], ALU.mult, ALU.add)\
                        .then_inc(S("z_in"), 1)
                dve.wait_ge(S("z_in"), CH * (i + 1))
                for n in range(SWEEPS):
                    for j in range(CH):
                        dve.wait_ge(S(f"sweep_ps{i}"), CH * n + j + 1)
                        dve.tensor_tensor(pre[:, j, :], bank[:, 4 + j, :], flat(zs, j), ALU.add)\
                            .then_inc(S(f"sweep_pre{i}"), 1)
                for j in range(CH):
                    dve.wait_ge(S(f"sweep_y{i}"), CH * (SWEEPS - 1) + j + 1)
                    link(dve.tensor_tensor(pre[:, j, :].rearrange("p (g t) -> p g t", g=2),
                                           yF[:, 2 * j:2 * j + 2, 1:T + 1], yS[:, 2 * j:2 * j + 2, 1:T + 1], ALU.subtract))
                    link(dve.tensor_reduce(out=moved[:, j:j + 1], in_=pre[:, j, :], axis=AX, op=ALU.max,
                                           apply_absolute_value=True))
                link(dve.tensor_reduce(out=moved[:, CH:CH + 1], in_=moved[:, 0:CH], axis=AX, op=ALU.max))
                dve.tensor_scalar(moved[:, CH + 1:CH + 2], moved[:, CH:CH + 1], -1.0 if force_steps else SETTLED, None,
                                  ALU.is_le).then_inc(S("settled_rows"), 1)
                dve.wait_ge(S("settled_sum"), i + 1)
                dve.tensor_scalar(unsettled[0:1, i:i + 1], bank[0:1, 2, 0:1], P - 0.5, None, ALU.is_lt)\
                    .then_inc(S("verdict"), 1)
                dve.wait_ge(S("y_final"), i + 1)
                dve.tensor_tensor(xQ[:, :, :], xQ[:, :, :], yF[:, :, 1:T + 1], ALU.add).then_inc(S(f"x_rnn{i}"), 1)

            def scan(i, k):
                odds_to_r(["x_rnn0", "x_moe"][i], 1)
                ln_dve(dve, k)
                dve.memset(carry[:, :, 0, :], 0.0)
                dve.memset(carry[:, :, 5, :], 0.0)
                link(dve.tensor_copy(rst[:, 15:16], ident[:, 0:1]))
                dve.wait_ge(S("ln_applied"), CH * (k + 1))
                dve.tensor_copy(carry[:, 0, 1:5, :], xn[:, 0:P].rearrange("p (w b) -> p w b", b=B)).then_inc(S("row_done"), 1)
                for h in range(1, H):
                    dve.wait_ge(S("row_ps"), (H - 1) * i + h)
                    dve.scalar_tensor_tensor(out=carry[:, h, 1:5, :],
                                             in0=bank[:, 4 + h % 2, 0:P].rearrange("p (w b) -> p w b", b=B), scalar=0.0,
                                             in1=xn[:, h * P:(h + 1) * P].rearrange("p (w b) -> p w b", b=B),
                                             op0=ALU.max, op1=ALU.add).then_inc(S("row_done"), 1)
                dve.wait_ge(S("row_done"), H * (i + 1))
                dve.wait_ge(S("xr_a"), 2 + i)
                xr4 = xR[:, :, :].rearrange("p (h w) b -> p h w b", w=4)
                link(dve.tensor_tensor(xr4, xr4, carry[:, :, 1:5, :], ALU.add))
                for q in range(NQ):
                    for r in range(NQ):
                        last = dve.tensor_copy(xQ[C * q:C * q + C, :, r:T:NQ],
                                               xR[C * r:C * r + C, :, q:B:NQ].rearrange("p t g -> p g t"))
                last.then_inc(S(f"x_scan{i}"), 1)

            def experts():
                dve.wait_ge(S("w_moe"), N_MOE)
                dve.transpose(w2b[:, :], w2b_rows[:, :])
                dve.transpose(gw[:, :].rearrange("p (k r) -> p k r", r=32), gw_rows[:, :].rearrange("p (k r) -> p k r", r=32)).then_inc(S("gw_t"), 1)
                dve.wait_ge(S("gw_t"), 1)
                dve.tensor_copy(gwc[:, :].rearrange("p (q e) -> p q e", q=NQ),
                                gw[:, :].rearrange("p (q e) -> p q e", q=NQ)[:, :, 0:E]).then_inc(S("gw"), 1)
                ln_dve(dve, 6)
                dve.wait_ge(S("gate_l"), 1)
                link(dve.tensor_scalar(lg.rearrange("p j t -> p (j t)"), bank[:, 4:6, :].rearrange("p k n -> p (k n)"), gb[:, :], None, ALU.add))
                for j in range(4):
                    dve.tensor_reduce(out=mo[:, j:j + 1], in_=lg[:, j, :], axis=AX, op=ALU.max, negate=True)\
                        .then_inc(S("moe_max"), 1)
                for j in range(4):
                    dve.wait_ge(S("moe_exp"), j + 1)
                    link(dve.reciprocal(mo[:, 8 + j:9 + j], mo[:, 4 + j:5 + j]))
                    link(dve.tensor_scalar(ex[:, j, :], ex[:, j, :], mo[:, 8 + j:9 + j], None, ALU.mult))
                    link(dve.max(mo[:, 16 + 8 * j:24 + 8 * j], ex[:, j, :]))
                    link(dve.match_replace(out=rep[:, j, :], in_to_replace=mo[:, 16 + 8 * j:24 + 8 * j],
                                           in_values=ex[:, j, :], imm_value=0.0))
                    last = dve.tensor_tensor(pm[:, j, :], ex[:, j, :], rep[:, j, :], ALU.subtract)
                last.then_inc(S("pm"), 1)
                dve.wait_ge(S("pmt_ps"), 1)
                dve.tensor_copy(pmt.rearrange("p j h n -> p (j h n)"), bank[:, 6:8, :].rearrange("p k n -> p (k n)")).then_inc(S("pmt"), 1)
                dve.wait_ge(S("pool_ps"), 1)
                dve.memset(pool_[32:33, :, :], 1.0)
                pp = bank[:, 0, :].rearrange("p (g m) -> p g m", g=G)
                for q in range(NQ):
                    last = dve.tensor_copy(pool_[0:C, :, q:B:NQ].rearrange("p e g -> p g e"),
                                           pp[C * q:C * q + C, :, E * q:E * q + E])
                last.then_inc(S("pooled"), 1)
                dve.wait_ge(S("eo_ps"), 1)
                link(dve.tensor_tensor(moT[0:C, :].rearrange("p (b e) -> p b e", e=E),
                                       bank[0:C, 2, :].rearrange("p (e b) -> p b e", e=E),
                                       w2b[:, 0:E].rearrange("p (o e) -> p o e", o=1).to_broadcast([C, B, E]), ALU.add))
                for gg in range(2):
                    for qp in range(2):
                        m4 = moT[0:C, :].rearrange("p (j n r) -> p j n r", j=4, r=32)[:, :, 2 * gg + qp, :]
                        last = dve.transpose(moB[64 * gg + 32 * qp:64 * gg + 32 * qp + 32, :, :], m4)
                link(last)
                for m in range(8):
                    last = dve.tensor_scalar(moD[:, :, m, :], moB[:, :, :], par16[:, m:m + 1], None, ALU.mult)
                last.then_inc(S("eo_bd"), 1)
                dve.wait_ge(S("moe_ps"), 1)
                dve.tensor_tensor(xQf, xQf, bank[:, 4:8, :].rearrange("p k n -> p (k n)"), ALU.add).then_inc(S("x_moe"), 1)

            rnn(0, 4)
            scan(0, 5)
            experts()
            scan(1, 7)
            rnn(1, 8)
            dve.wait_ge(S("x_rnn1"), 1)
            dve.wait_ge(S("xq_in"), CH)
            for g in range(G):
                last = dve.transpose(xN[:, g, :, :], xQ[:, g, :].rearrange("p (r k) -> p k r", k=8))
            last.then_inc(S("out_rows"), 1)


_INS = ["x", "L0_conv_w_qkv", "L0_conv_w_out", "L0_conv_b_out", "L0_conv_ln_scale",
        "L0_ffn_sigma", "L0_ffn_phi", "L0_ffn_M_u", "L0_ffn_M_phi_plus", "L0_ffn_M_phi_minus",
        "L0_ffn_log_weights", "L0_ffn_gumbel", "L1_conv_Wa1", "L1_conv_ba1", "L1_conv_Wa2",
        "L1_conv_ba2", "L1_conv_Wb1", "L1_conv_bb1", "L1_conv_Wb2", "L1_conv_bb2",
        "L1_conv_ln2_g", "L1_conv_ln2_b", "L1_conv_Wg", "L1_conv_bg", "L1_conv_Wz",
        "L1_conv_bz", "L1_ffn_W", "L1_ffn_V", "L1_ffn_gamma", "L1_ffn_beta",
        "L2_conv_W", "L2_ffn_gate_w", "L2_ffn_gate_b", "L2_ffn_weight1", "L2_ffn_weight2",
        "L3_conv_W", "L3_ffn_W", "L3_ffn_V", "L3_ffn_gamma", "L3_ffn_beta"]
_OUT = (B, H, W, C)


def kernel(**inputs):
    import numpy as _np
    import concourse.bacc as _bacc
    from concourse import mybir as _mybir
    from concourse.bass_utils import run_bass_kernel_spmd as _run

    nc = _bacc.Bacc("TRN2", target_bir_lowering=False, num_devices=1)
    arrays, args = {}, {}
    for name in _INS:
        a = _np.ascontiguousarray(inputs[name])
        arrays[f"in_{name}"] = a
        args[name] = nc.dram_tensor(f"in_{name}", a.shape, _mybir.dt.from_np(a.dtype), kind="ExternalInput").ap()
    args["out"] = nc.dram_tensor("out_0", _OUT, _mybir.dt.float32, kind="ExternalOutput").ap()
    build(nc, **args)
    r = _run(nc, [arrays], core_ids=[0])
    return r.results[0]["out_0"]
```

```python
from contextlib import ExitStack

import concourse.bass as bass
from concourse import mybir

F32 = mybir.dt.float32
I32 = mybir.dt.int32
ALU = mybir.AluOpType
ACT = mybir.ActivationFunctionType
AX = mybir.AxisListType.X

P = 128
B, H, W, C = 32, 16, 16, 32
T = H * W
NQ = P // C
G = B // NQ
NT = T // NQ
CH = 4
CW_ = G * T // CH
TC = T // CH
HEADS, DH = 4, 32
KF = 16
FRACS = 4
AR = 3
CT = 16
E, HID, TOPK = 16, 128, 8
TAPS = 9
LN_CONV, LN_TOK = 1e-6, 1e-5
BUSY = {2: 7, 3: 3, 4: 1, 5: 6, 6: 2, 7: 8, 8: 0}
BUSY_ROW = 1
ROW_LN = 7
FILT_FROM = 3
ACT_BD = 3
SWEEPS = 11
SETTLED = 2.0 ** -20

CONSTS = [("centre", P), ("mean32", P), ("ones32", P), ("ident", P), ("quarter", P), ("ones", 1), ("par16", 8)]
W_ATTN = [("wv_t", P), ("wo_bd", P), ("wk", NQ * P), ("wq", NQ * P), ("bout", 1), ("lnsc", 1)]
W_STU = [("phi_cols", T), ("sigma", 1), ("lw", FRACS), ("gum", FRACS)]
W_LATE = [("wa", P), ("wb", P), ("wg", P), ("ab_bias", 4 * CT), ("bg", 1), ("wz", 8 * C), ("wz_rows", P), ("g2", 1),
          ("b2", 1), ("bz", 1),
          ("rwt0", P), ("rvt0", P), ("rgam0", 1), ("rbet0", 1), ("band0", 3 * P),
          ("rwt1", P), ("rvt1", P), ("rgam1", 1), ("rbet1", 1), ("band1", 3 * P),
          ("gwc", NQ * E), ("gb", 1), ("w2b", E)]


def width(parts):
    return sum(n for _, n in parts)


def build(nc, force_steps=False, **d):
    x, out = d["x"], d["out"]
    with ExitStack() as ctx:
        def sb(name, shape, dt=F32):
            return ctx.enter_context(nc.sbuf_tensor(name, shape, dt))

        def sem(name):
            return ctx.enter_context(nc.semaphore(name))

        xQ = sb("xQ", [P, G, T])
        xR = sb("xR", [P, NT, B])
        xN = xR[:, :, :].rearrange("p (g k) c -> p g k c", g=G)
        xn = sb("xn", [P, G * T])
        xnQ = xn[:, :].rearrange("p (g t) -> p g t", g=G)
        xnH = xR[:, :, :].rearrange("p t b -> p (t b)").rearrange("p (h g w) -> p h g w", h=H, g=G)
        sq = sb("sq", [P, 2, CW_])
        lnv = sb("lnv", [P, 2, CW_])
        rs = sb("rs", [P, 2, CW_])


        attn_scratch = sb("attn_scratch", [P, 9216])
        N_FILT, N_RAW, N_TOEP = (AR + T) * C, FRACS * C * C, (T + T // 2 + T // 4 + T // 8) * C
        arena = sb("arena", [P, N_FILT + N_RAW + N_TOEP])

        bank = ctx.enter_context(nc.psum_tensor("bank", [P, 8, CW_], F32))

        def pack(name, parts):
            tile = sb("sb_" + name, [P, width(parts)])
            at, cols = 0, {}
            for part, n in parts:
                cols[part] = tile[:, at:at + n]
                at += n
            return tile, cols

        consts, c_ = pack("consts", CONSTS)
        centre = c_["centre"]
        mean32 = c_["mean32"]
        ones32 = c_["ones32"]
        ident, ones, quarter = c_["ident"], c_["ones"], c_["quarter"]
        par16 = c_["par16"]
        w_attn, c_ = pack("w_attn", W_ATTN)
        wq = c_["wq"].rearrange("p (q n) -> p q n", q=NQ)
        wk = c_["wk"].rearrange("p (q n) -> p q n", q=NQ)
        wv_t, wo_bd, bout, lnsc = c_["wv_t"], c_["wo_bd"], c_["bout"], c_["lnsc"]
        wvo = sb("wvo", [P, NQ, P])

        wm_raw = arena[:, N_FILT:N_FILT + N_RAW].rearrange("p (f m) -> p f m", f=FRACS)
        w_stu, c_ = pack("w_stu", W_STU)
        phi_cols = c_["phi_cols"]
        sigma, lw, gum = c_["sigma"], c_["lw"], c_["gum"]
        sig4 = sb("sig4", [P, 1])
        nsig4 = sb("nsig4", [P, 1])
        fw = sb("fw", [P, 8, FRACS])
        filt = arena[:, 0:N_FILT].rearrange("p (t e) -> p t e", e=C)
        SEG_T = [T, T // 2, T // 4, T // 8]
        SEG_AT = [0, T, T + T // 2, T + T // 2 + T // 4]
        toep = arena[:, N_FILT + N_RAW:].rearrange("p (t e) -> p t e", e=C)

        w_late, c_ = pack("w_late", W_LATE)
        wa, wb, wg, bg, g2, bz = (c_[n] for n in ("wa", "wb", "wg", "bg", "g2", "bz"))
        ab_bias = c_["ab_bias"].rearrange("p (k n) -> p k n", k=2)
        wz = c_["wz"].rearrange("p (j o) -> p j o", j=8)
        wz_rows, b2 = c_["wz_rows"][0:CT, :], c_["b2"][0:CT, :]
        bz2 = sb("bz2", [P, 1])
        rwt, rvt, rgam, rbet, band = ([c_[f"{n}{i}"] for i in range(2)]
                                      for n in ("rwt", "rvt", "rgam", "rbet", "band"))
        band = [b.rearrange("p (k n) -> p k n", k=3) for b in band]
        gwc, gb, w2b = c_["gwc"], c_["gb"], c_["w2b"][0:C, :]
        w1 = arena[0:C + 1, 24000:24000 + E * HID].rearrange("p (e h) -> p e h", e=E)
        w2 = arena[:, 26048:26048 + E * C].rearrange("p (e o) -> p e o", e=E)
        unsettled = sb("unsettled", [1, 2], I32)

        block = ctx.enter_context(nc.Block())
        s = {}

        def S(name):
            if name not in s:
                s[name] = sem(name)
            return s[name]

        bankQ = bank[:, :, :].rearrange("p k (g t) -> p (k g) t", t=T)

        def chunkQ(a, j):
            return a[:, 2 * j:2 * j + 2, :]

        def tokens(a, j):
            return a[:, :, TC * j:TC * j + TC]

        def by_batch(a):
            return a.rearrange("p (g t) -> p g t", g=G)

        def flat(a, j):
            return a[:, j * CW_:(j + 1) * CW_]

        xQf = xQ[:, :, :].rearrange("p g t -> p (g t)")
        xRf = xR[:, :, :].rearrange("p t b -> p (t b)")

        LN_TRI = 3
        LN_EPS = [LN_CONV, LN_TOK, LN_TOK, LN_CONV, LN_TOK, LN_CONV, LN_TOK, LN_CONV, LN_TOK]

        def var_bank(i):
            return (4 if i // CH == LN_TRI else 6) + i % 2

        def ln_centre(pe, i, src):
            pe.matmul(bank[:, i % CH, :], centre, src, start=True, stop=True).then_inc(S("ln_centred"), 1)

        def ln_spread(pe, i):
            pe.wait_ge(S("ln_squared"), i + 1)
            if i >= 2:
                pe.wait_ge(S("ln_logged"), i - 1)
            pe.matmul(bank[:, var_bank(i), :], mean32, sq[:, i % 2, :], start=True, stop=True)\
                .then_inc(S("ln_var"), 1)

        def ln_pe(pe, k, src, ready):
            ready(0)
            ln_centre(pe, CH * k, src(0))
            for j in range(CH):
                if j + 1 < CH:
                    ready(j + 1)
                    ln_centre(pe, CH * k + j + 1, src(j + 1))
                ln_spread(pe, CH * k + j)

        def ln_square(act, i):
            act.wait_ge(S("ln_centred"), i + 1)
            if i >= 2:
                act.wait_ge(S("ln_var"), i - 1)
            act.activation(sq[:, i % 2, :], bank[:, i % CH, :], ACT.Square).then_inc(S("ln_squared"), 1)

        def ln_rstd(act, i):
            act.wait_ge(S("ln_var"), i + 1)
            if i >= 2:
                act.wait_ge(S("ln_rstd"), i - 1)
            act.activation(lnv[:, i % 2, :], bank[:, var_bank(i), :], ACT.Ln, bias=LN_EPS[i // CH])\
                .then_inc(S("ln_logged"), 1)
            act.wait_ge(S("ln_logged"), i + 1)
            if i >= 2:
                act.wait_ge(S("ln_applied"), i - 1)
            act.activation(rs[:, i % 2, :], lnv[:, i % 2, :], ACT.Exp, scale=-0.5).then_inc(S("ln_rstd"), 1)

        def ln_act(act, k):
            ln_square(act, CH * k)
            for j in range(CH):
                if j + 1 < CH:
                    ln_square(act, CH * k + j + 1)
                ln_rstd(act, CH * k + j)

        def ln_dve(dve, k, apply=None):
            for j in range(CH):
                i = CH * k + j
                dve.wait_ge(S("ln_rstd"), i + 1)
                if apply is None:
                    dve.tensor_tensor(flat(xn, j), bank[:, j, :], rs[:, i % 2, :], ALU.mult)\
                        .then_inc(S("ln_applied"), 1)
                else:
                    apply(j, i)

        at = [0, attn_scratch]

        def cut(n):
            at[0] += n
            assert at[0] <= (9216 if at[1] is attn_scratch else 24000)
            return at[1][:, at[0] - n:at[0]]

        def buf(n, k=2):
            return cut(n * k).rearrange("p (k n) -> p k n", k=k)

        kE = buf(CW_)
        kN = buf(CW_)
        vo = buf(CW_)
        qb = buf(CW_)
        qs = buf(CW_)
        qe = buf(CW_)
        lz = buf(CW_)
        qn = buf(CW_, 3)
        cwt = cut(3 * 64).rearrange("p (k g c) -> p k g c", k=3, c=C)
        nkm = cut(32)
        kz = cut(32)
        rkz = cut(32)
        qm = cut(32).rearrange("p (k n) -> p k n", k=2)
        yb = xR[:, :, :].rearrange("p t b -> p (t b)")
        U = CH * NQ

        XM_END = 12288
        at[:] = [0, arena]
        a_bd = cut(64 * 8 * 16).rearrange("p (m g i) -> p m g i", m=64, g=8)
        ab_pre = cut(2048)
        xm = cut(G * T)
        assert at[0] == XM_END
        xmQ = by_batch(xm)
        a_in = cut(1024)
        b_in = cut(1024)
        a_s = cut(1024)
        b_s = cut(1024)
        zc = cut(1024)
        gate = cut(2048)
        zq = ab_pre[:, 0:1024]
        zn = ab_pre[:, 1024:2048]
        zT = a_bd.rearrange("p m g i -> p (m g i)")[:, 0:1024]
        upd = a_bd.rearrange("p m g i -> p (m g i)")[:, 2048:4096]
        zst = cut(4 * 64).rearrange("p (k n) -> p k n", k=4)

        at[0] = 0
        yS = cut(G * (T + 1)).rearrange("p (g t) -> p g t", g=G)
        yF = cut(G * (T + 1)).rearrange("p (g t) -> p g t", g=G)
        zs = cut(G * T)
        pre = buf(CW_, CH)
        moved = cut(CH + 2)
        bst = cut(CH * 6).rearrange("p (k n) -> p k n", n=6)
        mv = cut(2)
        rst = cut(16)

        at[0] = XM_END
        carry = cut(H * 6 * B).rearrange("p (h w b) -> p h w b", h=H, w=6)

        at[0] = 0
        lg = cut(1024).rearrange("p (j t) -> p j t", j=4)
        ex = cut(1024).rearrange("p (j t) -> p j t", j=4)
        pm = cut(1024).rearrange("p (j t) -> p j t", j=4)
        rep = cut(1024).rearrange("p (j t) -> p j t", j=4)
        mo = cut(64)
        xtok = cut(2048).rearrange("p (g h n) -> p g h n", g=G, h=2)
        pmt = cut(1024).rearrange("p (j h n) -> p j h n", j=4, h=2)
        pool_ = cut(E * B).rearrange("p (e b) -> p e b", e=E)
        hid = cut(E * B).rearrange("p (e b) -> p e b", e=E)
        moT = cut(E * B)
        moB = cut(4 * C).rearrange("p (j o) -> p j o", o=C)
        assert at[0] + 1024 <= XM_END - G * T
        moD = cut(4 * 256).rearrange("p (j m o) -> p j m o", j=4, m=8)

        ln_src = [lambda j: chunkQ(xQ, j), lambda j: flat(yb, j), lambda j: flat(xRf, j),
                  lambda j: tokens(xQ, j), lambda j: chunkQ(xQ, j), lambda j: flat(xRf, j),
                  lambda j: tokens(xQ, j), lambda j: flat(xRf, j), lambda j: tokens(xQ, j)]

        ACT_PHASES = [(0, 2)] * (CH - 1) + [(0,)]

        def back(j, q, r):
            return (xQ[C * q:C * q + C, :, TC * j + r:TC * j + TC:NQ],
                    xR[C * r:C * r + C, NT // CH * j:NT // CH * (j + 1), q:B:NQ].rearrange("p t g -> p g t"))

        loads = []

        @block.sync
        def _(sp):
            for q in range(NQ):
                sp.dma_start(xN[C * q:C * q + C, :, :, :],
                             x.rearrange("(g q) (h v) w c -> q (h v w) g c", q=NQ, v=1)
                             [q].rearrange("(r k) g c -> r g k c", k=8)).then_inc(S("x_in"), 16)

            def load(name, dst, src):
                sp.dma_start(dst, src).then_inc(S(name), 16)

            load("consts_in", consts[:, :], d["consts"])
            load("w_attn_in", w_attn[:, :], d["w_attn"])
            load("w_stu_in", w_stu[:, :], d["w_stu"])
            half = FRACS // 2
            for n in range(2):
                load("w_spec_in", wm_raw[:, half * n:half * n + half, :].rearrange("p f m -> p (f m)"),
                     d["w_spec"][:, half * n * C * C:half * (n + 1) * C * C])
            load("w_late_in", w_late[:, :], d["w_late"])

            sp.wait_ge(S("filt_zero"), 1)
            sp.wait_ge(S("filt_sb"), C // 2)
            for n in range(FRACS):
                for r in range(NQ):
                    sp.dma_start(toep[C * r:C * r + C, SEG_AT[n]:SEG_AT[n] + SEG_T[n], :],
                                 filt[C * n:C * n + C, AR - r:AR - r + SEG_T[n], :]).then_inc(S("toep_in"), 16)
            sp.wait_ge(S("stu_ps"), CH)
            load("w_moe", w1[:, :, :], d["w1"].rearrange("e d h -> d e h"))
            load("w_moe", w2[:, :, :], d["w2"][:, 0:HID, :].rearrange("e h o -> h e o"))
            for q in range(NQ):
                if q == 0:
                    sp.wait_ge(S("out_rows"), 1)
                sp.dma_start(out.rearrange("(g q) h w c -> q (h w) g c", q=NQ)[q]
                             .rearrange("(r k) g c -> r g k c", k=8),
                             xN[C * q:C * q + C, :, :, :]).then_inc(S("stored"), 16)
            sp.wait_ge(S("stored"), 16 * NQ)

        @block.gpsimd
        def _(pool):
            n = [0]

            def link(ins):
                n[0] += 1
                ins.then_inc(S("pool_step"), 1)
                pool.wait_ge(S("pool_step"), n[0])

            link(pool.memset(wvo[:, :, :], 0.0))
            pool.sem_inc(S("wvo_zero"), 1)
            link(pool.memset(filt[:, 0:AR, :], 0.0))
            pool.sem_inc(S("filt_zero"), 1)
            for n_ in range(1, FRACS):
                pool.wait_ge(S("wm_scaled"), n_ + 1)
                m = wm_raw[:, n_, :]
                link(pool.tensor_tensor(m, m, wm_raw[:, n_ - 1, :], ALU.add))
            pool.sem_inc(S("wm_seg"), 1)
            pool.wait_ge(S("sig4"), 1)
            link(pool.tensor_scalar(phi_cols[0:32, :], phi_cols[0:32, :], sig4[0:32, :], None, ALU.mult))
            link(pool.tensor_scalar(phi_cols[32:64, 0:T:2], phi_cols[32:64, 0:T:2], sig4[32:64, :], None, ALU.mult))
            pool.tensor_scalar(phi_cols[32:64, 1:T:2], phi_cols[32:64, 1:T:2], nsig4[32:64, :], None, ALU.mult)\
                .then_inc(S("phi_cols"), 1)

            xr4 = xR[:, :, :].rearrange("p (h w) b -> p h w b", w=4)
            for i in range(2):
                for j in range(CH):
                    pool.wait_ge(S("row_done"), H * i + 4 * j + 4)
                    rows = xr4[:, 4 * j:4 * j + 4]
                    link(pool.tensor_tensor(rows, rows, carry[:, 4 * j:4 * j + 4, 1:5, :], ALU.add))
                    pool.sem_inc(S("back_sum"), 1)

        @block.tensor
        def _(pe):
            mm = pe.matmul

            def full(ps, lhsT, rhs):
                return mm(ps, lhsT, rhs, start=True, stop=True)

            def keep_busy(n, k, cols=CW_):
                for _ in range(n):
                    full(bank[:, k, 0:cols], ident, consts[:, 0:cols])

            pe.wait_ge(S("consts_in"), 16)
            ln_pe(pe, 0, ln_src[0], lambda j: pe.wait_ge(S("xq_in"), j + 1))

            def filters(m):
                if m == 0:
                    pe.wait_ge(S("phi_cols"), 1)
                    pe.wait_ge(S("wm_seg"), 1)
                else:
                    pe.wait_ge(S("filt_sb"), m)
                for e in (2 * m, 2 * m + 1):
                    last = full(bank[:, 1, (e % 2) * T:(e % 2 + 1) * T],
                                wm_raw.rearrange("p f (d e) -> p (f d) e", e=C)[:, :, e], phi_cols)
                last.then_inc(S("filt_ps"), 1)

            pe.wait_ge(S("w_attn_in"), 16)
            pe.wait_ge(S("ln_logged"), CH)
            full(bank[:, 6, 0:P], wv_t, wo_bd).then_inc(S("wvo_ps"), 1)

            def attn_proj(u):
                j, q = divmod(u, NQ)
                pe.wait_ge(S("ln_applied"), j + 1)
                if u == 0:
                    pe.wait_ge(S("ln_applied"), CH)
                    pe.wait_ge(S("wvo"), 1)
                if u >= 1:
                    pe.wait_ge(S("k_exp"), u)
                full(bank[:, 0, :], wk[:, q, :], flat(xn, j)).then_inc(S("k_ps"), 1)
                if u >= 1:
                    pe.wait_ge(S("q_shift"), u)
                full(bank[:, 2, :], wq[:, q, :], flat(xn, j)).then_inc(S("q_ps"), 1)
                if u >= 1:
                    pe.wait_ge(S("v_sb"), u)
                for i in range(4):
                    last = full(bank[:, 4, i * P:(i + 1) * P], xn[:, j * CW_ + i * P:j * CW_ + (i + 1) * P],
                                wvo[:, q, :])
                last.then_inc(S("v_ps"), 1)

            def attn_mid(u):
                pe.wait_ge(S("k_exp"), u + 1)
                if u >= 1:
                    pe.wait_ge(S("k_rows"), u)
                for i in range(4):
                    last = pe.transpose(bank[:, 3, i * P:(i + 1) * P], kE[:, u % 2, i * P:(i + 1) * P], ident)
                last.then_inc(S("k_tr"), 1)
                pe.wait_ge(S("q_exp"), u + 1)
                if u >= 1:
                    pe.wait_ge(S("q_norm"), u)
                full(bank[:, 5, :], ones32, qe[:, u % 2, :]).then_inc(S("q_sum"), 1)

            def attn_ctx(u):
                pe.wait_ge(S("k_rows"), u + 1)
                pe.wait_ge(S("v_sb"), u + 1)
                if u >= 1:
                    pe.wait_ge(S("ctx_sb"), u)
                for g in range(2):
                    for h in range(2):
                        i = 2 * g + h
                        last = mm(bank[:, 6, g * P:(g + 1) * P], kN[:, u % 2, i * P:(i + 1) * P],
                                  vo[:, u % 2, i * P:(i + 1) * P], start=(h == 0), stop=(h == 1))
                last.then_inc(S("ctx_ps"), 1)

            def attn_out(u):
                j, q = divmod(u, NQ)
                pe.wait_ge(S("ctx_sb"), u + 1)
                pe.wait_ge(S("q_norm"), u + 1)
                if j >= 1:
                    pe.wait_ge(S("attn_y"), j)
                for g in range(2):
                    last = full(bank[C * q:C * q + C, 7, g * T:(g + 1) * T], cwt[:, u % 3, g, :],
                                qn[:, u % 3, g * T:(g + 1) * T])
                last.then_inc(S("attn_ps"), 1)

            for i in range(U + 3):
                if i < U:
                    attn_proj(i)
                if 0 <= i - 1 < U:
                    attn_mid(i - 1)
                if i >= FILT_FROM:
                    filters(i - FILT_FROM)
                if 0 <= i - 2 < U:
                    attn_ctx(i - 2)
                if 0 <= i - 3 < U:
                    attn_out(i - 3)
            ln_pe(pe, 1, ln_src[1], lambda j: pe.wait_ge(S("attn_y"), CH))

            keep_busy(BUSY[2], 4)
            pe.wait_ge(S("xr_v"), 1)
            pe.wait_ge(S("xr_a"), 1)
            ln_pe(pe, 2, ln_src[2], lambda j: None)
            pe.wait_ge(S("toep_in"), 16 * FRACS * NQ)
            pe.wait_ge(S("ln_applied"), 3 * CH)
            for seg, lo, hi in ((3, 0, 8), (2, 8, 16), (1, 16, 32), (0, 32, 48), (0, 48, 64)):
                for m in range(hi):
                    t0 = max(lo, m)
                    lhs = toep[:, SEG_AT[seg] + 4 * m:SEG_AT[seg] + 4 * m + 4, :]
                    last = mm(bank[:, 4 + lo // 16, (t0 % 16) * B:(t0 % 16 + hi - t0) * B], lhs,
                              xn[:, (t0 - m) * B:(hi - m) * B], start=(m == 0 and seg != 2), stop=(m == hi - 1),
                              skip_group_check=(seg >= 2))
                    for j, block, m_centre, m_spread in ((0, 32, 8, 12), (1, 32, 16, 20), (2, 48, 8, 12)):
                        if lo == block and m == m_centre:
                            pe.wait_ge(S("x_stu"), j + 1)
                            ln_centre(pe, CH * LN_TRI + j, tokens(xQ, j))
                        if lo == block and m == m_spread:
                            ln_spread(pe, CH * LN_TRI + j)
                if hi % 16 == 0:
                    last.then_inc(S("stu_ps"), 1)

            keep_busy(BUSY[3], 6)
            pe.wait_ge(S("x_stu"), CH)
            ln_centre(pe, CH * LN_TRI + CH - 1, tokens(xQ, CH - 1))
            ln_spread(pe, CH * LN_TRI + CH - 1)
            pe.wait_ge(S("w_late_in"), 16)
            pe.wait_ge(S("ln_applied"), 4 * CH)
            for k in range(2):
                for m in range(16):
                    cols = (xnH[:, m, :, :].rearrange("p g w -> p (g w)") if k == 0
                            else xmQ.rearrange("p g (h w) -> p (g h) w", w=W)[:, :, m])
                    last = full(bank[:, 4 * k + m // 4, (m % 4) * P:(m % 4 + 1) * P], cols, [wa, wb][k])
                last.then_inc(S("ab_ps"), 1)
            pe.wait_ge(S("a_pre"), 1)
            for j in range(CH):
                last = full(bank[:, j, :], wg, flat(xm, j))
            last.then_inc(S("gate_ps"), 1)
            pe.wait_ge(S("b_pre"), 1)
            pe.wait_ge(S("a_bd"), 2)
            pe.wait_ge(S("b_s"), 1)
            for m in range(64):
                last = full(bank[:, 4 + m // 32, (m % 32) * 16:(m % 32 + 1) * 16],
                            a_bd[:, m, :, :], b_s[:, m * 16:(m + 1) * 16])
            last.then_inc(S("z_ps"), 1)
            full(bank[:, 6, 0:1], wz_rows, b2).then_inc(S("bz_ps"), 1)
            pe.wait_ge(S("z_n"), 1)
            pe.wait_ge(S("bz2"), 1)
            for m in range(8):
                last = pe.transpose(bank[:, 6 + m // 4, (m % 4) * P:(m % 4 + 1) * P], zn[:, m * P:(m + 1) * P],
                                    ident)
            last.then_inc(S("z_tr"), 1)
            pe.wait_ge(S("z_t"), 1)
            pe.wait_ge(S("wz_g"), 1)
            pe.wait_ge(S("gate"), 1)
            for jj in range(16):
                for q in range(NQ):
                    last = full(bank[C * q:C * q + C, jj // 4, (jj % 4) * P:(jj % 4 + 1) * P], wz[:, jj % 8, :],
                                zT[:, (2 * q + jj // 8) * P:(2 * q + jj // 8 + 1) * P])
                if jj % 4 == 3:
                    last.then_inc(S("tri_ps"), 1)

            def rnn(i, k):
                if i == 0:
                    keep_busy(BUSY[k], 4)
                    ln_pe(pe, k, ln_src[k], lambda j: pe.wait_ge(S("x_tri"), 1))
                for j in range(CH):
                    pe.wait_ge(S("ln_applied"), CH * k + (j + 1 if i == 0 else CH))
                    full(bank[:, j, :], rwt[i], flat([xn, xm][i], j)).then_inc(S("wx_ps"), 1)
                pe.wait_ge(S("bn_mean_in"), i + 1)
                full(bank[:, 4, 0:1], quarter, mv[:, 0:1]).then_inc(S("bn_mean"), 1)
                pe.wait_ge(S("bn_var_in"), i + 1)
                full(bank[:, 5, 1:2], rvt[i], rst[:, 12:13])
                full(bank[:, 5, 0:1], quarter, rst[:, 2:3]).then_inc(S("bn_var"), 1)
                for n in range(1, SWEEPS):
                    for j in range(CH):
                        pe.wait_ge(S(f"sweep_y{i}"), CH * (n - 1) + j + 1)
                        full(bank[:, j, :], rvt[i], yS[:, 2 * j:2 * j + 2, 0:T])\
                            .then_inc(S(f"sweep_ps{i}"), 1)
                pe.wait_ge(S("settled_rows"), i + 1)
                full(bank[0:1, 4, 0:1], moved[:, CH + 1:CH + 2], ones[:, 0:1]).then_inc(S("settled_sum"), 1)
                pe.wait_ge(S("verdict"), i + 1)
                by_steps = pe.value_load(unsettled[0:1, i:i + 1], min_val=0, max_val=1)
                zt = zs.rearrange("p (g t) -> p g t", g=G)
                with pe.If(by_steps != 0):
                    with pe.Fori(0, T // 2) as t2:
                        for k2 in range(2):
                            mm(bank[:, 6 + k2, 0:G], ident, zt[:, :, bass.ds(t2 * 2 + k2, 1)], start=True, stop=False)
                            pe.wait_ge(S(f"y_step{i}"), t2 * 2 + (k2 + 1))
                            mm(bank[:, 6 + k2, 0:G], rvt[i], yF[:, :, bass.ds(t2 * 2 + k2, 1)],
                               start=False, stop=True).then_inc(S(f"v_step{i}"), 1)

            def scan(i, k):
                keep_busy(BUSY[k], [5, 0][i])
                pe.wait_ge(S("xr_v"), 2 + i)
                pe.wait_ge(S("xr_a"), 2 + i)
                ln_pe(pe, k, ln_src[k], lambda j: None)

                def centre_next(j):
                    pe.wait_ge(S("back_v"), CH * i + j + 1)
                    pe.wait_ge(S("back_a"), CH * i + j + 1)
                    ln_centre(pe, CH * (k + 1) + j, tokens(xQ, j))

                for h in range(1, H):
                    pe.wait_ge(S("row_done"), H * i + h)
                    for w in range(3):
                        last = mm(bank[:, 4 + h % 2, 0:P], band[i][:, w, :], carry[:, h - 1, w:w + 4, :],
                                  start=(w == 0), stop=(w == 2))
                    last.then_inc(S("row_ps"), 1)
                    if h >= ROW_LN and (h - ROW_LN) % 4 == 0:
                        centre_next((h - ROW_LN) // 4)
                    elif h > ROW_LN and (h - ROW_LN) % 4 == 1:
                        ln_spread(pe, CH * (k + 1) + (h - ROW_LN) // 4)
                    else:
                        keep_busy(BUSY_ROW, 3, P)
                ln_spread(pe, CH * (k + 1) + 2)
                keep_busy(BUSY[k + 1], 4)
                centre_next(3)
                ln_spread(pe, CH * (k + 1) + 3)

            def experts():
                pe.wait_ge(S("ln_applied"), CH * 7)
                for j in range(4):
                    for gg in range(2):
                        last = full(bank[64 * gg:64 * gg + 64, 4 + j // 2, (j % 2) * T:(j % 2 + 1) * T],
                                    gwc, xmQ[:, 2 * j + gg, :])
                last.then_inc(S("gate_l"), 1)
                pe.wait_ge(S("ln_applied"), CH * 7)
                for g in range(G):
                    for h in range(2):
                        m = 2 * g + h
                        last = pe.transpose(bank[:, m // 4, (m % 4) * P:(m % 4 + 1) * P],
                                            xmQ[:, g, h * P:(h + 1) * P], ident)
                last.then_inc(S("xtok_ps"), 1)
                pe.wait_ge(S("pm"), 1)
                for j in range(4):
                    for h in range(2):
                        m = 2 * j + h
                        last = pe.transpose(bank[:, 6 + m // 4, (m % 4) * P:(m % 4 + 1) * P],
                                            pm[:, j, h * P:(h + 1) * P], ident)
                last.then_inc(S("pmt_ps"), 1)
                pe.wait_ge(S("xtok"), 1)
                pe.wait_ge(S("pmt"), 1)
                for g in range(G):
                    for h in range(2):
                        last = mm(bank[:, 0, g * 64:(g + 1) * 64], xtok[:, g, h, :],
                                  pmt[:, g // 2, h, 64 * (g % 2):64 * (g % 2) + 64], start=(h == 0), stop=(h == 1))
                last.then_inc(S("pool_ps"), 1)
                pe.wait_ge(S("pooled"), 1)
                pe.wait_ge(S("w_moe"), 32)
                for e in range(E):
                    last = full(bank[:, 1, e * B:(e + 1) * B], w1[:, e, :], pool_[0:C + 1, e, :])
                last.then_inc(S("hid_ps"), 1)
                pe.wait_ge(S("hid"), 1)
                for e in range(E):
                    last = full(bank[0:C, 2, e * B:(e + 1) * B], w2[:, e, :], hid[:, e, :])
                last.then_inc(S("eo_ps"), 1)
                pe.wait_ge(S("eo_bd"), 1)
                for g in range(G):
                    last = full(bank[:, 4 + g // 2, (g % 2) * T:(g % 2 + 1) * T],
                                moD[:, g // 2, 4 * (g % 2):4 * (g % 2) + 4, :], pm[:, g // 2, :])
                last.then_inc(S("moe_ps"), 1)

            rnn(0, 4)
            scan(0, 5)
            experts()
            scan(1, 7)
            rnn(1, 8)

        @block.scalar
        def _(act):
            n = [0]

            def link(ins):
                n[0] += 1
                ins.then_inc(S("act_step"), 1)
                act.wait_ge(S("act_step"), n[0])

            def lnexp():
                act.preload_act_table_set("natural_log_exp_and_others")

            lnexp()
            ln_act(act, 0)

            act.wait_ge(S("fw_z"), 1)
            act.activation(fw[:, 1, :], fw[:, 0, :], ACT.Exp, bias=fw[:, 2, 0:1], accum_out=fw[:, 2, 1:2])\
                .then_inc(S("fw_exp"), 1)
            act.wait_ge(S("w_stu_in"), 16)
            link(act.activation(sig4[0:64, :], sigma[0:64, :], ACT.Ln))
            link(act.activation(sig4[0:64, :], sig4[0:64, :], ACT.Exp, scale=0.25))
            act.activation(nsig4[32:64, :], sig4[32:64, :], ACT.Copy, scale=-1.0).then_inc(S("sig4"), 1)
            act.wait_ge(S("wvo_ps"), 1)
            act.wait_ge(S("wvo_zero"), 1)
            for q in range(NQ):
                rows = slice(C * q, C * q + C)
                last = act.activation(wvo[rows, q, :], bank[rows, 6, 0:P], ACT.Copy)
            last.then_inc(S("wvo"), 1)

            def a_k(u):
                act.wait_ge(S("k_max"), u + 1)
                if u >= 2:
                    act.wait_ge(S("k_tr"), u - 1)
                for g in range(2):
                    last = act.activation(kE[:, u % 2, g * T:(g + 1) * T], bank[:, 0, g * T:(g + 1) * T], ACT.Exp,
                                          bias=nkm[:, 2 * u + g:2 * u + g + 1],
                                          accum_out=kz[:, 2 * u + g:2 * u + g + 1])
                last.then_inc(S("k_exp"), 1)

            def a_v(u):
                act.wait_ge(S("v_ps"), u + 1)
                if u >= 2:
                    act.wait_ge(S("ctx_ps"), u - 1)
                act.activation(vo[:, u % 2, :], bank[:, 4, :], ACT.Copy).then_inc(S("v_sb"), 1)

            def a_q(u):
                act.wait_ge(S("q_shift"), u + 1)
                if u >= 2:
                    act.wait_ge(S("q_norm"), u - 1)
                act.activation(qe[:, u % 2, :], qs[:, u % 2, :], ACT.Exp).then_inc(S("q_exp"), 1)

            def a_z(u):
                act.wait_ge(S("q_sum"), u + 1)
                act.activation(lz[:, u % 2, :], bank[:, 5, :], ACT.Ln).then_inc(S("q_log"), 1)
                act.wait_ge(S("q_log"), u + 1)
                act.activation(bank[:, 5, :], lz[:, u % 2, :], ACT.Exp, scale=-1.0).then_inc(S("q_rz"), 1)

            def a_y(j):
                act.wait_ge(S("attn_ps"), NQ * (j + 1))
                act.activation(flat(yb, j), bank[:, 7, :], ACT.Identity, bias=bout).then_inc(S("attn_y"), 1)

            def a_filters(m):
                act.wait_ge(S("filt_ps"), m + 1)
                act.activation(filt[:, AR:, 2 * m:2 * m + 2].rearrange("p t e -> p e t"),
                               bank[:, 1, :].rearrange("p (e t) -> p e t", e=2), ACT.Copy).then_inc(S("filt_sb"), 1)

            for i in range(U + 3):
                if i == 1:
                    act.wait_ge(S("w_spec_in"), 32)
                    act.wait_ge(S("fw_done"), 1)
                    for n_ in range(FRACS):
                        act.activation(wm_raw[:, n_, :], wm_raw[:, n_, :], ACT.Copy, scale=fw[:, 7, n_:n_ + 1])\
                            .then_inc(S("wm_scaled"), 1)
                if i < U:
                    a_k(i)
                if 0 <= i - 1 < U:
                    a_z(i - 1)
                if i < U:
                    a_v(i)
                    a_q(i)
                if i >= FILT_FROM:
                    a_filters(i - FILT_FROM)
                if i >= 3 and (i - 3) % NQ == NQ - 1:
                    a_y((i - 3) // NQ)
            ln_act(act, 1)

            def evens_to_r(k, dep, v):
                act.wait_ge(S(dep), v)
                for q in range(NQ):
                    for r in (0, 2):
                        last = act.activation(
                            xR[C * r:C * r + C, :, q:B:NQ].rearrange("p t g -> p g t"),
                            xQ[C * q:C * q + C, :, r:T:NQ], ACT.Copy)
                last.then_inc(S("xr_a"), 1)

            evens_to_r(0, "x_attn", CH)
            ln_act(act, 2)
            for i in range(CH * LN_TRI, CH * LN_TRI + CH):
                ln_square(act, i)
                ln_rstd(act, i)

            def sigmoids():
                act.preload_act_table_set("sigmoid_and_others")

            sigmoids()
            act.wait_ge(S("a_in"), 1)
            act.activation(a_s[:, :], a_in[:, :].rearrange("p (h m) -> p m h", h=16), ACT.Sigmoid).then_inc(S("a_s"), 1)
            act.wait_ge(S("b_in"), 1)
            act.activation(b_s[:, :], b_in[:, :].rearrange("p (h m) -> p m h", h=16), ACT.Sigmoid).then_inc(S("b_s"), 1)
            act.wait_ge(S("a_s"), 1)
            for g in range(ACT_BD):
                last = act.activation(a_bd[:, :, g, :], a_s.rearrange("p (m i) -> p m i", i=16), ACT.Copy,
                                      scale=par16[:, g:g + 1])
            last.then_inc(S("a_bd"), 1)
            act.wait_ge(S("gate_ps"), 1)
            act.activation(gate[:, :], bank[:, 0:4, :], ACT.Sigmoid, bias=bg).then_inc(S("gate"), 1)
            lnexp()
            act.wait_ge(S("z_c"), 1)
            act.activation(zq[:, :], zc[:, :], ACT.Square).then_inc(S("z_sq"), 1)
            act.wait_ge(S("z_var"), 1)
            link(act.activation(zst[:, 2, :], zst[:, 1, :], ACT.Ln, bias=LN_TOK, scale=1.0 / CT))
            act.activation(zst[:, 3, :], zst[:, 2, :], ACT.Exp, scale=-0.5).then_inc(S("z_rstd"), 1)
            act.wait_ge(S("z_tr"), 1)
            act.activation(zT[:, :], bank[:, 6:8, :], ACT.Copy).then_inc(S("z_t"), 1)

            def rnn(i, k):
                if i == 0:
                    ln_act(act, k)
                act.wait_ge(S("bn_v"), i + 1)
                link(act.activation(rst[:, 5:6], rst[:, 10:11], ACT.Ln, bias=LN_TOK))
                act.activation(rst[:, 6:7], rst[:, 5:6], ACT.Exp, scale=-0.5).then_inc(S("bn_rstd"), 1)
                sigmoids()
                for j in range(CH):
                    act.wait_ge(S("z_in"), CH * i + j + 1)
                    act.activation(yS[:, 2 * j:2 * j + 2, 1:T + 1], flat(zs, j).rearrange("p (g t) -> p g t", g=2),
                                   ACT.Sigmoid, bias=rst[:, 11:12]).then_inc(S(f"sweep_y{i}"), 1)
                for n in range(1, SWEEPS):
                    y = yF if n == SWEEPS - 1 else yS
                    for j in range(CH):
                        act.wait_ge(S(f"sweep_pre{i}"), CH * (n - 1) + j + 1)
                        act.activation(y[:, 2 * j:2 * j + 2, 1:T + 1], pre[:, j, :].rearrange("p (g t) -> p g t", g=2),
                                       ACT.Sigmoid).then_inc(S(f"sweep_y{i}"), 1)
                act.wait_ge(S("verdict"), i + 1)
                by_steps = act.value_load(unsettled[0:1, i:i + 1], min_val=0, max_val=1)
                with act.If(by_steps != 0):
                    act.sem_inc(S(f"y_step{i}"), 1)
                    with act.Fori(0, T // 2) as t2:
                        for k2 in range(2):
                            act.wait_ge(S(f"v_step{i}"), t2 * 2 + (k2 + 1))
                            act.activation(yF[:, :, bass.ds(t2 * 2 + (k2 + 1), 1)], bank[:, 6 + k2, 0:G],
                                           ACT.Sigmoid).then_inc(S(f"y_step{i}"), 1)
                    act.wait_ge(S(f"y_step{i}"), T + 1)
                act.sem_inc(S("y_final"), 1)
                lnexp()

            def scan_back(i, k):
                for j in range(CH):
                    act.wait_ge(S("back_sum"), CH * i + j + 1)
                    for q in range(NQ):
                        for r in ACT_PHASES[j]:
                            last = act.activation(*back(j, q, r), ACT.Copy)
                    last.then_inc(S("back_a"), 1)
                    if j == CH - 1:
                        ln_rstd(act, CH * (k + 1) + j - 1)
                    ln_square(act, CH * (k + 1) + j)
                    if j != CH - 2:
                        ln_rstd(act, CH * (k + 1) + j)

            rnn(0, 4)
            evens_to_r(1, "x_rnn0", 1)
            ln_act(act, 5)
            scan_back(0, 5)
            for j in range(4):
                act.wait_ge(S("moe_max"), j + 1)
                act.activation(ex[:, j, :], lg[:, j, :], ACT.Exp, bias=mo[:, j:j + 1], accum_out=mo[:, 4 + j:5 + j])\
                    .then_inc(S("moe_exp"), 1)
            act.wait_ge(S("xtok_ps"), 1)
            act.activation(xtok.rearrange("p g h n -> p (g h n)"), bank[:, 0:4, :].rearrange("p k n -> p (k n)"), ACT.Copy).then_inc(S("xtok"), 1)
            act.preload_act_table_set("gelu_and_others")
            act.wait_ge(S("hid_ps"), 1)
            act.activation(hid.rearrange("p e b -> p (e b)"), bank[:, 1, :], ACT.Gelu).then_inc(S("hid"), 1)
            lnexp()
            evens_to_r(2, "x_moe", 1)
            ln_act(act, 7)
            scan_back(1, 7)
            rnn(1, 8)

        @block.vector
        def _(dve):
            n = [0]

            def link(ins):
                n[0] += 1
                ins.then_inc(S("dve_step"), 1)
                dve.wait_ge(S("dve_step"), n[0])

            dve.wait_ge(S("x_in"), 16 * NQ)
            for g in range(G):
                last = dve.transpose(xQ[:, g, :].rearrange("p (r k) -> p k r", k=8), xN[:, g, :, :])
                if g % 2:
                    last.then_inc(S("xq_in"), 1)
            ln_dve(dve, 0)
            dve.wait_ge(S("w_stu_in"), 16)
            link(dve.tensor_tensor(fw[:, 0, :], lw, gum, ALU.add))
            dve.tensor_reduce(out=fw[:, 2, 0:1], in_=fw[:, 0, :], axis=AX, op=ALU.max, negate=True).then_inc(S("fw_z"), 1)
            dve.wait_ge(S("fw_exp"), 1)
            link(dve.reciprocal(fw[:, 2, 2:3], fw[:, 2, 1:2]))
            link(dve.tensor_scalar(fw[:, 3, :], fw[:, 1, :], fw[:, 2, 2:3], None, ALU.mult))
            link(dve.tensor_reduce(out=fw[:, 2, 3:4], in_=fw[:, 3, :], axis=AX, op=ALU.max))
            link(dve.tensor_scalar(fw[:, 4, :], fw[:, 3, :], fw[:, 2, 3:4], None, ALU.is_equal))
            link(dve.memset(fw[:, 5, :], 0.0))
            for f in range(1, FRACS):
                link(dve.tensor_tensor(fw[:, 5, f:f + 1], fw[:, 5, f - 1:f], fw[:, 4, f - 1:f], ALU.max))
            link(dve.tensor_tensor(fw[:, 4, :], fw[:, 4, :], fw[:, 5, :], ALU.is_gt))
            link(dve.tensor_tensor(fw[:, 6, :], fw[:, 4, :], fw[:, 3, :], ALU.subtract))
            dve.tensor_tensor(fw[:, 7, :], fw[:, 6, :], fw[:, 3, :], ALU.add).then_inc(S("fw_done"), 1)

            def v_k(u):
                dve.wait_ge(S("k_ps"), u + 1)
                dve.tensor_reduce(out=nkm[:, 2 * u:2 * u + 2],
                                  in_=bank[:, 0, :].rearrange("p (g t) -> p g t", g=2),
                                  axis=AX, op=ALU.max, negate=True).then_inc(S("k_max"), 1)

            def v_q(u):
                dve.wait_ge(S("q_ps"), u + 1)
                link(dve.tensor_reduce(out=qm[:, u % 2, :], in_=bank[:, 2, :].rearrange("p (k r) -> p k r", r=32),
                                       axis=AX, op=ALU.max, negate=True, apply_transpose=True))
                link(dve.transpose(qb[:, u % 2, :].rearrange("p (k r) -> p k r", r=32),
                                   qm[:, u % 2, :].rearrange("p (k o) -> p k o", o=1).to_broadcast([P, 16, 32])))
                if u >= 2:
                    dve.wait_ge(S("q_exp"), u - 1)
                dve.tensor_tensor(qs[:, u % 2, :], bank[:, 2, :], qb[:, u % 2, :], ALU.add).then_inc(S("q_shift"), 1)

            def v_kn(u):
                dve.wait_ge(S("k_tr"), u + 1)
                if u >= 2:
                    dve.wait_ge(S("ctx_ps"), u - 1)
                dve.tensor_copy(kN[:, u % 2, :], bank[:, 3, :]).then_inc(S("k_rows"), 1)

            def v_qn(u):
                dve.wait_ge(S("q_rz"), u + 1)
                if u >= 3:
                    dve.wait_ge(S("attn_ps"), u - 2)
                dve.tensor_tensor(qn[:, u % 3, :], qe[:, u % 2, :], bank[:, 5, :], ALU.mult).then_inc(S("q_norm"), 1)

            def v_ctx(u):
                link(dve.reciprocal(rkz[:, 2 * u:2 * u + 2], kz[:, 2 * u:2 * u + 2]))
                dve.wait_ge(S("ctx_ps"), u + 1)
                if u >= 3:
                    dve.wait_ge(S("attn_ps"), u - 2)
                for h in range(HEADS):
                    rows = slice(C * h, C * h + C)
                    for g in range(2):
                        last = dve.tensor_scalar(cwt[rows, u % 3, g, :], bank[rows, 6, g * P + C * h:g * P + C * h + C],
                                                 rkz[rows, 2 * u + g:2 * u + g + 1], DH ** -0.5 / T, ALU.mult, ALU.mult)
                last.then_inc(S("ctx_sb"), 1)

            for i in range(U + 2):
                if i < U:
                    v_k(i)
                    v_q(i)
                if 0 <= i - 1 < U:
                    v_kn(i - 1)
                    v_qn(i - 1)
                if 0 <= i - 2 < U:
                    v_ctx(i - 2)

            def attn_apply(j, i):
                dve.tensor_tensor(flat(xn, j), bank[:, j, :], rs[:, i % 2, :], ALU.mult).then_inc(S("ln_applied"), 1)
                dve.wait_ge(S("ln_applied"), i + 1)
                dve.scalar_tensor_tensor(out=flat(xQf, j), in0=flat(xn, j), scalar=lnsc,
                                         in1=flat(xQf, j), op0=ALU.mult, op1=ALU.add).then_inc(S("x_attn"), 1)

            ln_dve(dve, 1, attn_apply)

            def odds_to_r(dep, v):
                dve.wait_ge(S(dep), v)
                for q in range(NQ):
                    for r in (1, 3):
                        last = dve.tensor_copy(xR[C * r:C * r + C, :, q:B:NQ].rearrange("p t g -> p g t"),
                                               xQ[C * q:C * q + C, :, r:T:NQ])
                last.then_inc(S("xr_v"), 1)

            odds_to_r("x_attn", CH)
            ln_dve(dve, 2)
            dve.wait_ge(S("xr_a"), 1)

            def add_stu(j):
                dve.wait_ge(S("stu_ps"), j + 1)
                stu = bank[:, 4 + j, :].rearrange("p (t b) -> p t b", b=B)
                for q in range(NQ):
                    for r in range(NQ):
                        xs, _ = back(j, q, r)
                        last = dve.tensor_tensor(xs, stu[C * r:C * r + C, :, q:B:NQ].rearrange("p t g -> p g t"), xs,
                                                 ALU.add)
                last.then_inc(S("x_stu"), 1)

            def twice(j, i):
                h4 = xnH[:, 4 * j:4 * j + 4, :, :].rearrange("p h g w -> p g h w")
                for out_ in (tokens(xmQ, j).rearrange("p g (h w) -> p g h w", w=W), h4):
                    last = dve.tensor_tensor(out_, bank[:, j, :].rearrange("p (g h w) -> p g h w", g=G, w=W),
                                             rs[:, i % 2, :].rearrange("p (g h w) -> p g h w", g=G, w=W), ALU.mult)
                last.then_inc(S("ln_applied"), 1)

            def normalise(j):
                dve.wait_ge(S("ln_rstd"), CH * LN_TRI + j + 1)
                twice(j, CH * LN_TRI + j)

            add_stu(0)
            add_stu(1)
            normalise(0)
            normalise(1)
            add_stu(2)
            normalise(2)
            add_stu(3)
            normalise(3)
            dve.wait_ge(S("w_late_in"), 16)
            for k in range(2):
                dve.wait_ge(S("ab_ps"), k + 1)
                if k:
                    dve.wait_ge(S("a_in"), 1)
                pre4 = ab_pre.rearrange("p (m n) -> p m n", n=2 * CT)
                dve.tensor_tensor(pre4, bank[:, 4 * k:4 * k + 4, :].rearrange("p k (m n) -> p (k m) n", n=2 * CT),
                                  ab_bias[:, k:k + 1, :].to_broadcast([P, 64, 2 * CT]), ALU.add)\
                    .then_inc(S(["a_pre", "b_pre"][k]), 1)
                dve.wait_ge(S(["a_pre", "b_pre"][k]), 1)
                dve.tensor_tensor((b_in if k else a_in).rearrange("p (m c) -> p m c", c=CT), pre4[:, :, 0:CT], pre4[:, :, CT:2 * CT],
                                  ALU.mult).then_inc(S(["a_in", "b_in"][k]), 1)
            dve.wait_ge(S("a_s"), 1)
            for g in range(ACT_BD, 8):
                last = dve.tensor_scalar(a_bd[:, :, g, :], a_s.rearrange("p (m i) -> p m i", i=16),
                                         par16[:, g:g + 1], None, ALU.mult)
            last.then_inc(S("a_bd"), 1)
            dve.wait_ge(S("z_ps"), 1)
            zp = bank[:, 4:6, :].rearrange("p k n -> p (k n)").rearrange("p (q c j) -> p q j c", q=NQ, c=CT)
            z4 = [a.rearrange("p (q j c) -> p q j c", q=NQ, j=16) for a in (zc, zq, zn)]
            link(dve.tensor_reduce(out=zst[:, 0, :], in_=zp, axis=AX, op=ALU.add))
            link(dve.tensor_scalar(zst[:, 0, :], zst[:, 0, :], -1.0 / CT, None, ALU.mult))
            zm = zst[:, 0, :].rearrange("p (q j o) -> p q j o", q=NQ, o=1).to_broadcast([P, NQ, 16, CT])
            dve.tensor_tensor(z4[0], zp, zm, ALU.add).then_inc(S("z_c"), 1)
            dve.wait_ge(S("bz_ps"), 1)
            dve.tensor_tensor(bz2[:, :], bank[:, 6, 0:1], bz, ALU.add).then_inc(S("bz2"), 1)
            dve.tensor_scalar(wz[:, :, :], wz[:, :, :], g2, None, ALU.mult).then_inc(S("wz_g"), 1)
            dve.wait_ge(S("z_sq"), 1)
            dve.tensor_reduce(out=zst[:, 1, :], in_=z4[1], axis=AX, op=ALU.add).then_inc(S("z_var"), 1)
            dve.wait_ge(S("z_rstd"), 1)
            zr = zst[:, 3, :].rearrange("p (m o) -> p m o", o=1).to_broadcast([P, 64, CT])
            dve.wait_ge(S("z_c"), 1)
            dve.tensor_tensor(zn.rearrange("p (m c) -> p m c", c=CT), zc.rearrange("p (m c) -> p m c", c=CT), zr,
                              ALU.mult).then_inc(S("z_n"), 1)
            dve.wait_ge(S("gate"), 1)
            dve.wait_ge(S("bz2"), 1)
            for k in range(4):
                dve.wait_ge(S("tri_ps"), k + 1)
                cols = [a.rearrange("p (n j) -> p n j", j=16)[:, :, 4 * k:4 * k + 4] for a in (upd, gate, xQf)]
                link(dve.scalar_tensor_tensor(out=cols[0], in0=bank[:, k, :].rearrange("p (j n) -> p n j", j=4),
                                              scalar=bz2[:, :], in1=cols[1], op0=ALU.add, op1=ALU.mult))
                last = dve.tensor_tensor(cols[2], cols[2], cols[0], ALU.add)
            last.then_inc(S("x_tri"), 1)

            def rnn(i, k):
                dve.wait_ge(S(["x_tri", "back_v"][i]), [1, 2 * CH][i])
                dve.memset(yS[:, :, 0:1], 0.0)
                dve.memset(yF[:, :, 0:1], 0.0)
                dve.memset(rst[:, 12:13], 0.5)
                if i == 0:
                    ln_dve(dve, k)
                for j in range(CH):
                    dve.wait_ge(S("wx_ps"), CH * i + j + 1)
                    link(dve.bn_stats(out=bst[:, j, :], in_=bank[:, j, :]))
                dve.bn_aggr(out=mv[:, :], in_=bst[:, :, :]).then_inc(S("bn_mean_in"), 1)
                dve.wait_ge(S("bn_mean_in"), i + 1)
                dve.wait_ge(S("bn_mean"), i + 1)
                link(dve.tensor_copy(rst[:, 0:1], bank[:, 4, 0:1]))
                link(dve.tensor_tensor(rst[:, 1:2], mv[:, 0:1], rst[:, 0:1], ALU.subtract))
                link(dve.tensor_tensor(rst[:, 3:4], rst[:, 1:2], rst[:, 1:2], ALU.mult))
                dve.tensor_tensor(rst[:, 2:3], rst[:, 3:4], mv[:, 1:2], ALU.add).then_inc(S("bn_var_in"), 1)
                dve.wait_ge(S("bn_var"), i + 1)
                dve.tensor_copy(rst[:, 10:12], bank[:, 5, 0:2]).then_inc(S("bn_v"), 1)
                dve.wait_ge(S("bn_rstd"), i + 1)
                link(dve.tensor_tensor(rst[:, 7:8], rst[:, 6:7], rgam[i], ALU.mult))
                link(dve.tensor_tensor(rst[:, 8:9], rst[:, 7:8], rst[:, 0:1], ALU.mult))
                link(dve.tensor_tensor(rst[:, 9:10], rbet[i], rst[:, 8:9], ALU.subtract))
                for j in range(CH):
                    dve.tensor_scalar(flat(zs, j), bank[:, j, :], rst[:, 7:8], rst[:, 9:10], ALU.mult, ALU.add)\
                        .then_inc(S("z_in"), 1)
                dve.wait_ge(S("z_in"), CH * (i + 1))
                for n in range(1, SWEEPS):
                    for j in range(CH):
                        dve.wait_ge(S(f"sweep_ps{i}"), CH * (n - 1) + j + 1)
                        dve.tensor_tensor(pre[:, j, :], bank[:, j, :], flat(zs, j), ALU.add)\
                            .then_inc(S(f"sweep_pre{i}"), 1)
                for j in range(CH):
                    dve.wait_ge(S(f"sweep_y{i}"), CH * (SWEEPS - 1) + j + 1)
                    link(dve.tensor_tensor(pre[:, j, :].rearrange("p (g t) -> p g t", g=2),
                                           yF[:, 2 * j:2 * j + 2, 1:T + 1], yS[:, 2 * j:2 * j + 2, 1:T + 1], ALU.subtract))
                    link(dve.tensor_reduce(out=moved[:, j:j + 1], in_=pre[:, j, :], axis=AX, op=ALU.max,
                                           apply_absolute_value=True))
                link(dve.tensor_reduce(out=moved[:, CH:CH + 1], in_=moved[:, 0:CH], axis=AX, op=ALU.max))
                dve.tensor_scalar(moved[:, CH + 1:CH + 2], moved[:, CH:CH + 1], -1.0 if force_steps else SETTLED, None,
                                  ALU.is_le).then_inc(S("settled_rows"), 1)
                dve.wait_ge(S("settled_sum"), i + 1)
                dve.tensor_scalar(unsettled[0:1, i:i + 1], bank[0:1, 4, 0:1], P - 0.5, None, ALU.is_lt)\
                    .then_inc(S("verdict"), 1)
                dve.wait_ge(S("y_final"), i + 1)
                if i == 1:
                    dve.wait_ge(S("back_a"), 2 * CH)
                dve.tensor_tensor(xQ[:, :, :], xQ[:, :, :], yF[:, :, 1:T + 1], ALU.add).then_inc(S(f"x_rnn{i}"), 1)

            def scan(i, k):
                odds_to_r(["x_rnn0", "x_moe"][i], 1)
                ln_dve(dve, k)
                dve.memset(carry[:, :, 0, :], 0.0)
                dve.memset(carry[:, :, 5, :], 0.0)
                dve.wait_ge(S("ln_applied"), CH * (k + 1))
                dve.tensor_copy(carry[:, 0, 1:5, :], xn[:, 0:P].rearrange("p (w b) -> p w b", b=B)).then_inc(S("row_done"), 1)
                def back_half(j, qs):
                    dve.wait_ge(S("back_sum"), CH * i + j + 1)
                    for q in qs:
                        for r in range(NQ):
                            if r not in ACT_PHASES[j]:
                                last = dve.tensor_copy(*back(j, q, r))
                    if qs[-1] == NQ - 1:
                        last.then_inc(S("back_v"), 1)

                def normalise(j):
                    n = CH * (k + 1) + j
                    dve.wait_ge(S("ln_rstd"), n + 1)
                    dve.tensor_tensor(tokens(xmQ, j), by_batch(bank[:, j, :]), by_batch(rs[:, n % 2, :]), ALU.mult)\
                        .then_inc(S("ln_applied"), 1)

                for h in range(1, H):
                    dve.wait_ge(S("row_ps"), (H - 1) * i + h)
                    dve.scalar_tensor_tensor(out=carry[:, h, 1:5, :],
                                             in0=bank[:, 4 + h % 2, 0:P].rearrange("p (w b) -> p w b", b=B), scalar=0.0,
                                             in1=xn[:, h * P:(h + 1) * P].rearrange("p (w b) -> p w b", b=B),
                                             op0=ALU.max, op1=ALU.add).then_inc(S("row_done"), 1)
                    if h in (5, 9, 13):
                        back_half(h // 4 - 1, (0, 1))
                    if h in (6, 10, 14):
                        back_half(h // 4 - 1, (2, 3))
                    if h in (9, 13):
                        normalise(h // 4 - 2)
                back_half(3, (0, 1, 2, 3))
                normalise(2)
                normalise(3)

            def experts():
                dve.wait_ge(S("gate_l"), 1)
                link(dve.tensor_scalar(lg.rearrange("p j t -> p (j t)"), bank[:, 4:6, :].rearrange("p k n -> p (k n)"), gb, None, ALU.add))
                for j in range(4):
                    dve.tensor_reduce(out=mo[:, j:j + 1], in_=lg[:, j, :], axis=AX, op=ALU.max, negate=True)\
                        .then_inc(S("moe_max"), 1)
                for j in range(4):
                    dve.wait_ge(S("moe_exp"), j + 1)
                    link(dve.reciprocal(mo[:, 8 + j:9 + j], mo[:, 4 + j:5 + j]))
                    link(dve.tensor_scalar(ex[:, j, :], ex[:, j, :], mo[:, 8 + j:9 + j], None, ALU.mult))
                    link(dve.max(mo[:, 16 + 8 * j:24 + 8 * j], ex[:, j, :]))
                    link(dve.match_replace(out=rep[:, j, :], in_to_replace=mo[:, 16 + 8 * j:24 + 8 * j],
                                           in_values=ex[:, j, :], imm_value=0.0))
                    last = dve.tensor_tensor(pm[:, j, :], ex[:, j, :], rep[:, j, :], ALU.subtract)
                last.then_inc(S("pm"), 1)
                dve.wait_ge(S("pmt_ps"), 1)
                dve.tensor_copy(pmt.rearrange("p j h n -> p (j h n)"), bank[:, 6:8, :].rearrange("p k n -> p (k n)")).then_inc(S("pmt"), 1)
                dve.wait_ge(S("pool_ps"), 1)
                dve.memset(pool_[32:33, :, :], 1.0)
                pp = bank[:, 0, :].rearrange("p (g m) -> p g m", g=G)
                for q in range(NQ):
                    last = dve.tensor_copy(pool_[0:C, :, q:B:NQ].rearrange("p e g -> p g e"),
                                           pp[C * q:C * q + C, :, E * q:E * q + E])
                last.then_inc(S("pooled"), 1)
                dve.wait_ge(S("eo_ps"), 1)
                link(dve.tensor_tensor(moT[0:C, :].rearrange("p (b e) -> p b e", e=E),
                                       bank[0:C, 2, :].rearrange("p (e b) -> p b e", e=E),
                                       w2b.rearrange("p (o e) -> p o e", o=1).to_broadcast([C, B, E]), ALU.add))
                for gg in range(2):
                    for qp in range(2):
                        m4 = moT[0:C, :].rearrange("p (j n r) -> p j n r", j=4, r=32)[:, :, 2 * gg + qp, :]
                        last = dve.transpose(moB[64 * gg + 32 * qp:64 * gg + 32 * qp + 32, :, :], m4)
                link(last)
                for m in range(8):
                    last = dve.tensor_scalar(moD[:, :, m, :], moB[:, :, :], par16[:, m:m + 1], None, ALU.mult)
                last.then_inc(S("eo_bd"), 1)
                dve.wait_ge(S("moe_ps"), 1)
                dve.wait_ge(S("back_a"), CH)
                dve.tensor_tensor(xQf, xQf, bank[:, 4:8, :].rearrange("p k n -> p (k n)"), ALU.add).then_inc(S("x_moe"), 1)

            rnn(0, 4)
            scan(0, 5)
            experts()
            scan(1, 7)
            rnn(1, 8)
            dve.wait_ge(S("x_rnn1"), 1)
            dve.wait_ge(S("xq_in"), CH)
            for g in range(G):
                last = dve.transpose(xN[:, g, :, :], xQ[:, g, :].rearrange("p (r k) -> p k r", k=8))
            last.then_inc(S("out_rows"), 1)


def lay_out(x, **w):
    import numpy as np

    w = {k: np.asarray(v) for k, v in w.items()}
    f = np.float32

    def blocks(m, n=NQ):
        r, c = m.shape
        out = np.zeros((n * r, n * c), f)
        for q in range(n):
            out[q * r:(q + 1) * r, q * c:(q + 1) * c] = m
        return out

    def by_block(m):
        out = np.zeros((NQ, C, NQ, m.shape[-1]), f)
        for q in range(NQ):
            out[q, :, q] = m[q] if m.ndim == 3 else m
        return out.reshape(P, -1)

    def rows(v, n=P):
        return np.tile(v.reshape(1, -1), (n, 1))

    def column(v):
        return np.tile(v.reshape(-1, 1), (P // v.size, 1))

    def padded(m):
        return np.concatenate([m, np.zeros((P - m.shape[0], m.shape[1]), f)])

    def gather(parts, table):
        for name, n in parts:
            assert table[name].shape == (P, n), (name, table[name].shape)
        return np.ascontiguousarray(np.concatenate([table[n] for n, _ in parts], axis=1))

    eye = np.eye(P, dtype=f)
    mean = blocks(np.full((C, C), 1.0 / C, f))
    consts = {"centre": blocks(np.eye(C, dtype=f) - f(1.0 / C)), "mean32": mean, "ones32": blocks(np.ones((C, C), f)), "ident": eye,
              "quarter": np.tile(np.eye(C, dtype=f) / NQ, (NQ, NQ)), "ones": np.ones((P, 1), f),
              "par16": np.kron(np.eye(8, dtype=f), np.ones((16, 1), f))}

    qkv = w["L0_conv_w_qkv"]
    attn = {"wv_t": np.tile(qkv[:, 2 * P:].T, (1, NQ)),
            "wo_bd": by_block(w["L0_conv_w_out"].reshape(HEADS, C, C)),
            "wk": by_block(qkv[:, P:2 * P]), "wq": by_block(qkv[:, 0:P]),
            "bout": column(w["L0_conv_b_out"]), "lnsc": column(w["L0_conv_ln_scale"])}

    spec = np.zeros((P, FRACS, C, C), f)
    spec[0:KF] = w["L0_ffn_M_phi_plus"].transpose(1, 0, 2, 3)
    spec[32:32 + KF] = w["L0_ffn_M_phi_minus"].transpose(1, 0, 2, 3)
    spec[64:64 + AR] = w["L0_ffn_M_u"].transpose(1, 0, 2, 3)
    phi, sigma = np.zeros((P, T), f), np.ones((P, 1), f)
    for k in (0, 32):
        phi[k:k + KF] = w["L0_ffn_phi"][0:T].T
        sigma[k:k + KF, 0] = w["L0_ffn_sigma"]
    phi[64:64 + AR, 0:AR] = np.eye(AR, dtype=f)
    stu = {"phi_cols": phi, "sigma": sigma, "lw": rows(w["L0_ffn_log_weights"]), "gum": rows(w["L0_ffn_gumbel"])}

    t = {k[len("L1_conv_"):]: v for k, v in w.items() if k.startswith("L1_conv_")}
    late = {"wa": blocks(np.concatenate([t["Wa1"], t["Wa2"]], axis=1)),
            "wb": blocks(np.concatenate([t["Wb1"], t["Wb2"]], axis=1)), "wg": blocks(t["Wg"]),
            "ab_bias": rows(np.concatenate([t["ba1"], t["ba2"], t["bb1"], t["bb2"]])), "bg": column(t["bg"]),
            "wz": blocks(t["Wz"], 8), "wz_rows": padded(np.tile(t["Wz"], (1, NQ))), "g2": column(t["ln2_g"]),
            "b2": column(t["ln2_b"]), "bz": column(t["bz"])}
    for i, (cell, scan) in enumerate((("L1_ffn_", "L2_conv_W"), ("L3_ffn_", "L3_conv_W"))):
        band = np.zeros((NQ, C, 3, NQ, C), f)
        for p in range(NQ):
            for b in range(3):
                for r in range(NQ):
                    k = 4 * (b - 1) + p - r + 4
                    if 0 <= k < TAPS:
                        band[p, :, b, r] = w[scan][k]
        late |= {f"rwt{i}": blocks(w[cell + "W"].T), f"rvt{i}": blocks(w[cell + "V"].T),
                 f"rgam{i}": column(w[cell + "gamma"]), f"rbet{i}": column(w[cell + "beta"]),
                 f"band{i}": band.reshape(P, -1)}
    late |= {"gwc": blocks(w["L2_ffn_gate_w"].T), "gb": column(w["L2_ffn_gate_b"]),
             "w2b": padded(w["L2_ffn_weight2"][:, HID, :].T)}
    return {"x": np.asarray(x), "consts": gather(CONSTS, consts), "w_attn": gather(W_ATTN, attn),
            "w_stu": gather(W_STU, stu), "w_spec": spec.reshape(P, -1), "w_late": gather(W_LATE, late),
            "w1": w["L2_ffn_weight1"], "w2": w["L2_ffn_weight2"]}


def kernel(**inputs):
    import numpy as _np
    import concourse.bacc as _bacc
    from concourse import mybir as _mybir
    from concourse.bass_utils import run_bass_kernel_spmd as _run

    nc = _bacc.Bacc("TRN2", target_bir_lowering=False, num_devices=1)
    arrays, args = {}, {}
    for name, a in lay_out(**inputs).items():
        arrays[f"in_{name}"] = _np.ascontiguousarray(a)
        args[name] = nc.dram_tensor(f"in_{name}", a.shape, _mybir.dt.from_np(a.dtype), kind="ExternalInput").ap()
    args["out"] = nc.dram_tensor("out_0", (B, H, W, C), _mybir.dt.float32, kind="ExternalOutput").ap()
    build(nc, **args)
    r = _run(nc, [arrays], core_ids=[0])
    return r.results[0]["out_0"]
```

```python
from contextlib import ExitStack

import concourse.bass as bass
from concourse import mybir

F32 = mybir.dt.float32
I32 = mybir.dt.int32
ALU = mybir.AluOpType
ACT = mybir.ActivationFunctionType
AX = mybir.AxisListType.X

P = 128
B, H, W, C = 32, 16, 16, 32
T = H * W
NQ = P // C
G = B // NQ
NT = T // NQ
CH = 4
BANK = G * T // CH
QH = NT // CH
TC = T // CH
HEADS, DH = 4, 32
KF = 16
FRACS = 4
AR = 3
CT = 16
E, HID, TOPK = 16, 128, 8
TAPS = 9
LN_CONV, LN_TOK = 1e-6, 1e-5
BUSY = {2: 6, 3: 2, 4: 1, 5: 3, 6: 1, 7: 5, 8: 0}
BUSY_ROW, BUSY_START, BUSY_MOE = 1, 3, 2
WX_EARLY = [0, 2]
ROW_LN = 7
FILT_FROM = 5
ACT_BD = 3
SWEEPS = 11
SETTLED = 2.0 ** -20

CONSTS = [("centre", P), ("mean32", P), ("ident", P), ("quarter", P), ("ones", 1), ("par16", 8)]
W_ATTN = [("wv_t", P), ("wo_bd", P), ("wk", NQ * P), ("wq", NQ * P), ("bout", 1), ("lnsc", 1)]
W_STU = [("phi_cols", T), ("sigma", 1), ("lw", FRACS), ("gum", FRACS)]
W_LATE = [("wa", P), ("wb", P), ("wg", P), ("ab_bias", 4 * CT), ("bg", 1), ("wz", 8 * C), ("wz_rows", P), ("g2", 1),
          ("b2", 1), ("bz", 1),
          ("rwt0", P), ("rvt0", P), ("rgam0", 1), ("rbet0", 1), ("band0", 3 * P),
          ("rwt1", P), ("rvt1", P), ("rgam1", 1), ("rbet1", 1), ("band1", 3 * P),
          ("gwc", NQ * E), ("gb", 1), ("w2b", E)]


def width(parts):
    return sum(n for _, n in parts)


def build(nc, force_steps=False, **d):
    x, out = d["x"], d["out"]
    with ExitStack() as ctx:
        def sb(name, shape, dt=F32):
            return ctx.enter_context(nc.sbuf_tensor(name, shape, dt))

        def sem(name):
            return ctx.enter_context(nc.semaphore(name))

        xQ = sb("xQ", [P, G, T])
        xR = sb("xR", [P, NT, B])
        xN = xR[:, :, :].rearrange("p (g k) c -> p g k c", g=G)
        xn = sb("xn", [P, G * T])
        xnQ = xn[:, :].rearrange("p (g t) -> p g t", g=G)
        xnH = xR[:, :, :].rearrange("p t b -> p (t b)").rearrange("p (h g w) -> p h g w", h=H, g=G)
        sq = sb("sq", [P, 2, BANK])
        lnv = sb("lnv", [P, 2, BANK])
        rs = sb("rs", [P, 2, BANK])

        attn_scratch = sb("attn_scratch", [P, 9216])
        N_FILT, N_RAW, N_TOEP = (AR + T) * C, FRACS * C * C, (T + T // 2 + T // 4 + T // 8) * C
        arena = sb("arena", [P, N_FILT + N_RAW + N_TOEP])

        bank = ctx.enter_context(nc.psum_tensor("bank", [P, 8, BANK], F32))

        def pack(name, parts):
            tile = sb("sb_" + name, [P, width(parts)])
            at, cols = 0, {}
            for part, n in parts:
                cols[part] = tile[:, at:at + n]
                at += n
            return tile, cols

        consts, c_ = pack("consts", CONSTS)
        centre = c_["centre"]
        mean32 = c_["mean32"]
        ident, ones, quarter = c_["ident"], c_["ones"], c_["quarter"]
        par16 = c_["par16"]
        w_attn, c_ = pack("w_attn", W_ATTN)
        wq = c_["wq"].rearrange("p (q n) -> p q n", q=NQ)
        wk = c_["wk"].rearrange("p (q n) -> p q n", q=NQ)
        wv_t, wo_bd, bout, lnsc = c_["wv_t"], c_["wo_bd"], c_["bout"], c_["lnsc"]
        wvo = sb("wvo", [P, NQ, P])

        wm_raw = arena[:, N_FILT:N_FILT + N_RAW].rearrange("p (f m) -> p f m", f=FRACS)
        w_stu, c_ = pack("w_stu", W_STU)
        phi_cols = c_["phi_cols"]
        sigma, lw, gum = c_["sigma"], c_["lw"], c_["gum"]
        sig4 = sb("sig4", [P, 1])
        nsig4 = sb("nsig4", [P, 1])
        fw = sb("fw", [P, 8, FRACS])
        filt = arena[:, 0:N_FILT].rearrange("p (t e) -> p t e", e=C)
        SEG_T = [T, T // 2, T // 4, T // 8]
        SEG_AT = [0, T, T + T // 2, T + T // 2 + T // 4]
        toep = arena[:, N_FILT + N_RAW:].rearrange("p (t e) -> p t e", e=C)

        N_DIFF = (2 * QH - 1) * 4 * C
        diff12, diff32 = (arena[:, n * N_DIFF:(n + 1) * N_DIFF].rearrange("p (t e) -> p t e", e=C) for n in range(2))
        x01 = arena[:, 2 * N_DIFF:2 * N_DIFF + QH * B]
        both = arena[:, 2 * N_DIFF + QH * B:2 * N_DIFF + 2 * QH * B]

        w_late, c_ = pack("w_late", W_LATE)
        wa, wb, wg, bg, g2, bz = (c_[n] for n in ("wa", "wb", "wg", "bg", "g2", "bz"))
        ab_bias = c_["ab_bias"].rearrange("p (k n) -> p k n", k=2)
        wz = c_["wz"].rearrange("p (j o) -> p j o", j=8)
        wz_rows, b2 = c_["wz_rows"][0:CT, :], c_["b2"][0:CT, :]
        bz2 = sb("bz2", [P, 1])
        rwt, rvt, rgam, rbet, band = ([c_[f"{n}{i}"] for i in range(2)]
                                      for n in ("rwt", "rvt", "rgam", "rbet", "band"))
        band = [b.rearrange("p (k n) -> p k n", k=3) for b in band]
        gwc, gb, w2b = c_["gwc"], c_["gb"], c_["w2b"][0:C, :]
        w1 = arena[0:C + 1, 24000:24000 + E * HID].rearrange("p (e h) -> p e h", e=E)
        w2 = arena[:, 26048:26048 + E * C].rearrange("p (e o) -> p e o", e=E)
        unsettled = sb("unsettled", [1, 2], I32)

        block = ctx.enter_context(nc.Block())
        s = {}

        def S(name):
            if name not in s:
                s[name] = sem(name)
            return s[name]

        def chunkQ(a, j):
            return a[:, 2 * j:2 * j + 2, :]

        def tokens(a, j):
            return a[:, :, TC * j:TC * j + TC]

        def by_batch(a):
            return a.rearrange("p (g t) -> p g t", g=G)

        def flat(a, j):
            return a[:, j * BANK:(j + 1) * BANK]

        xQf = xQ[:, :, :].rearrange("p g t -> p (g t)")
        xRf = xR[:, :, :].rearrange("p t b -> p (t b)")

        LN_TRI, LN_RNN = 3, 4

        def grid_cols(a, k):
            return a.rearrange("p (n j) -> p n j", j=W)[:, :, 4 * k:4 * k + 4]

        LN_EPS = [LN_CONV, LN_TOK, LN_TOK, LN_CONV, LN_TOK, LN_CONV, LN_TOK, LN_CONV, LN_TOK]

        def var_bank(i):
            return (4 if i // CH == LN_TRI else 6) + i % 2

        def ln_centre(pe, i, src):
            pe.matmul(bank[:, i % CH, :], centre, src, start=True, stop=True).then_inc(S("ln_centred"), 1)

        def ln_spread(pe, i):
            pe.wait_ge(S("ln_squared"), i + 1)
            if i >= 2:
                pe.wait_ge(S("ln_logged"), i - 1)
            pe.matmul(bank[:, var_bank(i), :], mean32, sq[:, i % 2, :], start=True, stop=True)\
                .then_inc(S("ln_var"), 1)

        def ln_pe(pe, k, src, ready):
            ready(0)
            ln_centre(pe, CH * k, src(0))
            for j in range(CH):
                if j + 1 < CH:
                    ready(j + 1)
                    ln_centre(pe, CH * k + j + 1, src(j + 1))
                ln_spread(pe, CH * k + j)

        def ln_square(act, i):
            act.wait_ge(S("ln_centred"), i + 1)
            if i >= 2:
                act.wait_ge(S("ln_var"), i - 1)
            act.activation(sq[:, i % 2, :], bank[:, i % CH, :], ACT.Square).then_inc(S("ln_squared"), 1)

        def ln_rstd(act, i):
            act.wait_ge(S("ln_var"), i + 1)
            if i >= 2:
                act.wait_ge(S("ln_rstd"), i - 1)
            act.activation(lnv[:, i % 2, :], bank[:, var_bank(i), :], ACT.Ln, bias=LN_EPS[i // CH])\
                .then_inc(S("ln_logged"), 1)
            act.wait_ge(S("ln_logged"), i + 1)
            if i >= 2:
                act.wait_ge(S("ln_applied"), i - 1)
            act.activation(rs[:, i % 2, :], lnv[:, i % 2, :], ACT.Exp, scale=-0.5).then_inc(S("ln_rstd"), 1)

        def ln_act(act, k):
            ln_square(act, CH * k)
            for j in range(CH):
                if j + 1 < CH:
                    ln_square(act, CH * k + j + 1)
                ln_rstd(act, CH * k + j)

        def ln_dve(dve, k, apply=None):
            for j in range(CH):
                i = CH * k + j
                dve.wait_ge(S("ln_rstd"), i + 1)
                if apply is None:
                    dve.tensor_tensor(flat(xn, j), bank[:, j, :], rs[:, i % 2, :], ALU.mult)\
                        .then_inc(S("ln_applied"), 1)
                else:
                    apply(j, i)

        at = [0, attn_scratch]

        def cut(n):
            at[0] += n
            assert at[0] <= (9216 if at[1] is attn_scratch else 24000)
            return at[1][:, at[0] - n:at[0]]

        def buf(n, k=2):
            return cut(n * k).rearrange("p (k n) -> p k n", k=k)

        kE = buf(BANK)
        kN = buf(BANK)
        vo = buf(BANK)
        qb = buf(BANK)
        qs = buf(BANK)
        qe = buf(BANK)
        qw = buf(BANK)
        qn = buf(BANK, 3)
        cwt = cut(3 * 64).rearrange("p (k g c) -> p k g c", k=3, c=C)
        nkm = cut(32)
        kz = cut(32)
        rkz = cut(32)
        qm = cut(32).rearrange("p (k n) -> p k n", k=2)
        qz = cut(32).rearrange("p (k n) -> p k n", k=2)
        qrz = cut(32).rearrange("p (k n) -> p k n", k=2)
        yb = xR[:, :, :].rearrange("p t b -> p (t b)")
        U = CH * NQ

        XM_END = 12288
        at[:] = [0, arena]
        a_bd = cut(64 * 8 * 16).rearrange("p (m g i) -> p m g i", m=64, g=8)
        ab_pre = cut(2048)
        xm = cut(G * T)
        assert at[0] == XM_END
        xmQ = by_batch(xm)
        a_in = cut(1024)
        b_in = cut(1024)
        a_s = cut(1024)
        b_s = cut(2048).rearrange("p (m h) -> p m h", h=2 * W)
        zc = cut(1024)
        gate = cut(2048)
        zq = ab_pre[:, 0:1024]
        zn = ab_pre[:, 1024:2048]
        z_cols = zn
        zT = a_bd.rearrange("p m g i -> p (m g i)")[:, 0:1024]
        upd = a_bd.rearrange("p m g i -> p (m g i)")[:, 2048:4096]
        zst = cut(4 * 64).rearrange("p (k n) -> p k n", k=4)

        at[0] = 0
        yS = cut(G * (T + 1)).rearrange("p (g t) -> p g t", g=G)
        yF = cut(G * (T + 1)).rearrange("p (g t) -> p g t", g=G)
        zs = cut(G * T)
        pre = buf(BANK, CH)
        moved = cut(CH + 2)
        bst = cut(CH * 6).rearrange("p (k n) -> p k n", n=6)
        mv = cut(2)
        rst = cut(16)

        at[0] = XM_END
        carry = cut(H * 6 * B).rearrange("p (h w b) -> p h w b", h=H, w=6)

        at[0] = 0
        lg = cut(1024).rearrange("p (j t) -> p j t", j=4)
        ex = cut(1024).rearrange("p (j t) -> p j t", j=4)
        pm = cut(1024).rearrange("p (j t) -> p j t", j=4)
        rep = cut(1024).rearrange("p (j t) -> p j t", j=4)
        mo = cut(64)
        xtok = cut(2048).rearrange("p (g h n) -> p g h n", g=G, h=2)
        pmt = cut(1024).rearrange("p (j h n) -> p j h n", j=4, h=2)
        pool_ = cut(E * B).rearrange("p (e b) -> p e b", e=E)
        hid = cut(E * B).rearrange("p (e b) -> p e b", e=E)
        moT = cut(E * B)
        moB = cut(4 * C).rearrange("p (j o) -> p j o", o=C)
        assert at[0] + 1024 <= XM_END - G * T
        moD = cut(4 * 256).rearrange("p (j m o) -> p j m o", j=4, m=8)

        ln_src = [lambda j: chunkQ(xQ, j), lambda j: flat(yb, j), lambda j: flat(xRf, j),
                  lambda j: tokens(xQ, j), lambda j: grid_cols(xQf, j), lambda j: flat(xRf, j),
                  lambda j: tokens(xQ, j), lambda j: flat(xRf, j), lambda j: tokens(xQ, j)]

        ACT_PHASES = [(0, 2)] * (CH - 1) + [(0,)]

        ACT_TO_R = [(q, 0) for q in range(NQ)] + [(0, 2), (2, 2)]

        def filter_turns(i):
            late = U + 3 - FILT_FROM
            extra = C // 2 - late

            def first(n):
                return n + max(0, n - (late - extra))

            n = i - FILT_FROM
            return range(first(n), first(n + 1)) if n >= 0 else range(0)

        def back(j, q, r):
            return (xQ[C * q:C * q + C, :, TC * j + r:TC * j + TC:NQ],
                    xR[C * r:C * r + C, NT // CH * j:NT // CH * (j + 1), q:B:NQ].rearrange("p t g -> p g t"))

        def store(engine, qs):
            for half in range(2):
                engine.wait_ge(S("out_rows"), half + 1)
                gs = slice(G // 2 * half, G // 2 * half + G // 2)
                for q in qs:
                    engine.dma_start(out.rearrange("(g q) h w c -> q (h w) g c", q=NQ)[q]
                                     .rearrange("(r k) g c -> r g k c", k=8)[:, gs],
                                     xN[C * q:C * q + C, gs, :, :]).then_inc(S("stored"), 16)

        @block.sync
        def _(sp):
            for q in range(NQ):
                sp.dma_start(xN[C * q:C * q + C, :, :, :],
                             x.rearrange("(g q) (h v) w c -> q (h v w) g c", q=NQ, v=1)
                             [q].rearrange("(r k) g c -> r g k c", k=8)).then_inc(S("x_in"), 16)

            def load(name, dst, src):
                sp.dma_start(dst, src).then_inc(S(name), 16)

            load("consts_in", consts[:, :], d["consts"])
            load("w_attn_in", w_attn[:, :], d["w_attn"])
            load("w_stu_in", w_stu[:, :], d["w_stu"])
            half = FRACS // 2
            for n in range(2):
                load("w_spec_in", wm_raw[:, half * n:half * n + half, :].rearrange("p f m -> p (f m)"),
                     d["w_spec"][:, half * n * C * C:half * (n + 1) * C * C])
            load("w_late_in", w_late[:, :], d["w_late"])

            sp.wait_ge(S("filt_zero"), 1)
            sp.wait_ge(S("filt_sb"), C // 2)
            for n in range(FRACS):
                for r in range(NQ):
                    sp.dma_start(toep[C * r:C * r + C, SEG_AT[n]:SEG_AT[n] + SEG_T[n], :],
                                 filt[C * n:C * n + C, AR - r:AR - r + SEG_T[n], :]).then_inc(S("toep_in"), 16)
            sp.wait_ge(S("stu_ps"), CH)
            load("w_moe", w1[:, :, :], d["w1"].rearrange("e d h -> d e h"))
            load("w_moe", w2[:, :, :], d["w2"][:, 0:HID, :].rearrange("e h o -> h e o"))
            store(sp, (0, 1))
            sp.wait_ge(S("stored"), 16 * 2 * NQ)

        @block.gpsimd
        def _(pool):
            n = [0]

            def link(ins):
                n[0] += 1
                ins.then_inc(S("pool_step"), 1)
                pool.wait_ge(S("pool_step"), n[0])

            link(pool.memset(wvo[:, :, :], 0.0))
            pool.sem_inc(S("wvo_zero"), 1)
            link(pool.memset(filt[:, 0:AR, :], 0.0))
            pool.sem_inc(S("filt_zero"), 1)
            def q_normalise(u):
                pool.wait_ge(S("q_weight"), u + 1)
                if u >= 3:
                    pool.wait_ge(S("attn_ps"), u - 2)
                link(pool.tensor_tensor(qn[:, u % 3, :], qe[:, u % 2, :], qw[:, u % 2, :], ALU.mult))
                pool.sem_inc(S("q_norm"), 1)

            pool.wait_ge(S("sig4"), 1)
            link(pool.tensor_scalar(phi_cols[0:32, :], phi_cols[0:32, :], sig4[0:32, :], None, ALU.mult))
            link(pool.tensor_scalar(phi_cols[32:64, 0:T:2], phi_cols[32:64, 0:T:2], sig4[32:64, :], None, ALU.mult))
            link(pool.tensor_scalar(phi_cols[32:64, 1:T:2], phi_cols[32:64, 1:T:2], nsig4[32:64, :], None, ALU.mult))
            pool.sem_inc(S("phi_cols"), 1)

            for u in range(U):
                q_normalise(u)
                if u < FRACS - 1:
                    pool.wait_ge(S("wm_scaled"), u + 2)
                    m = wm_raw[:, u + 1, :]
                    link(pool.tensor_tensor(m, m, wm_raw[:, u, :], ALU.add))
                if u == FRACS - 2:
                    pool.sem_inc(S("wm_seg"), 1)

            pool.wait_ge(S("stu_ps"), CH)
            for par in range(2):
                link(pool.memset(b_s[:, par::2, W * (1 - par):W * (1 - par) + W], 0.0))
            pool.sem_inc(S("b_zero"), 1)

            xr4 = xR[:, :, :].rearrange("p (h w) b -> p h w b", w=4)

            def add_rows(i):
                for j in range(CH):
                    pool.wait_ge(S("row_done"), H * i + 4 * j + 4)
                    rows = xr4[:, 4 * j:4 * j + 4]
                    link(pool.tensor_tensor(rows, rows, carry[:, 4 * j:4 * j + 4, 1:5, :], ALU.add))
                    pool.sem_inc(S("back_sum"), 1)

            def add_states(i):
                def add(j):
                    link(pool.tensor_tensor(chunkQ(xnQ, j), chunkQ(xQ, j), yF[:, 2 * j:2 * j + 2, 1:T + 1], ALU.add))

                if i == 1:
                    pool.wait_ge(S("back_v"), 2 * CH)
                    pool.wait_ge(S("back_a"), 2 * CH)
                for j in range(CH):
                    pool.wait_ge(S(f"sweep_y{i}"), CH * (SWEEPS - 1) + j + 1)
                    add(j)
                pool.sem_inc(S(f"x_early{i}"), 1)
                pool.wait_ge(S("verdict"), i + 1)
                by_steps = pool.value_load(unsettled[0:1, i:i + 1], min_val=0, max_val=1)
                with pool.If(by_steps != 0):
                    pool.wait_ge(S("y_final"), i + 1)
                    for j in range(CH):
                        pool.tensor_tensor(chunkQ(xnQ, j), chunkQ(xQ, j), yF[:, 2 * j:2 * j + 2, 1:T + 1], ALU.add)\
                            .then_inc(S(f"x_again{i}"), 1)
                        pool.wait_ge(S(f"x_again{i}"), j + 1)
                pool.sem_inc(S(f"x_rnn{i}"), 1)

            pool.wait_ge(S("x_tri"), CH)
            link(pool.memset(carry[:, :, 0, :], 0.0))
            link(pool.memset(carry[:, :, 5, :], 0.0))
            pool.sem_inc(S("edges"), 1)
            add_states(0)
            add_rows(0)
            add_rows(1)
            add_states(1)

        @block.tensor
        def _(pe):
            mm = pe.matmul

            def full(ps, lhsT, rhs):
                return mm(ps, lhsT, rhs, start=True, stop=True)

            def keep_busy(n, k, cols=BANK):
                for _ in range(n):
                    full(bank[:, k, 0:cols], ident, consts[:, 0:cols])

            pe.wait_ge(S("wvo_zero"), 1)
            for _ in range(BUSY_START):
                full(bank[:, 4, :], wvo[:, 0, :], wvo[:, :, :])
            pe.wait_ge(S("consts_in"), 16)
            ln_pe(pe, 0, ln_src[0], lambda j: pe.wait_ge(S("xq_in"), j + 1))

            def filters(m):
                if m == 0:
                    pe.wait_ge(S("phi_cols"), 1)
                    pe.wait_ge(S("wm_seg"), 1)
                else:
                    pe.wait_ge(S("filt_sb"), m)
                for e in (2 * m, 2 * m + 1):
                    last = full(bank[:, 1, (e % 2) * T:(e % 2 + 1) * T],
                                wm_raw.rearrange("p f (d e) -> p (f d) e", e=C)[:, :, e], phi_cols)
                last.then_inc(S("filt_ps"), 1)

            pe.wait_ge(S("w_attn_in"), 16)
            pe.wait_ge(S("ln_logged"), CH)
            full(bank[:, 6, 0:P], wv_t, wo_bd).then_inc(S("wvo_ps"), 1)

            def attn_proj(u):
                j, q = divmod(u, NQ)
                pe.wait_ge(S("ln_applied"), j + 1)
                if u == 0:
                    pe.wait_ge(S("ln_applied"), CH)
                    pe.wait_ge(S("wvo"), 1)
                if u >= 2:
                    pe.wait_ge(S("k_exp"), u - 1)
                full(bank[:, 5 * (u % 2), :], wk[:, q, :], flat(xn, j)).then_inc(S("k_ps"), 1)
                if u >= 1:
                    pe.wait_ge(S("q_shift"), u)
                full(bank[:, 2, :], wq[:, q, :], flat(xn, j)).then_inc(S("q_ps"), 1)
                if u >= 1:
                    pe.wait_ge(S("v_sb"), u)
                for i in range(4):
                    last = full(bank[:, 4, i * P:(i + 1) * P], xn[:, j * BANK + i * P:j * BANK + (i + 1) * P],
                                wvo[:, q, :])
                last.then_inc(S("v_ps"), 1)

            def attn_mid(u):
                pe.wait_ge(S("k_exp"), u + 1)
                if u >= 1:
                    pe.wait_ge(S("k_rows"), u)
                for i in range(4):
                    last = pe.transpose(bank[:, 3, i * P:(i + 1) * P], kE[:, u % 2, i * P:(i + 1) * P], ident)
                last.then_inc(S("k_tr"), 1)

            def attn_ctx(u):
                pe.wait_ge(S("k_rows"), u + 1)
                pe.wait_ge(S("v_sb"), u + 1)
                if u >= 1:
                    pe.wait_ge(S("ctx_sb"), u)
                for g in range(2):
                    for h in range(2):
                        i = 2 * g + h
                        last = mm(bank[:, 6, g * P:(g + 1) * P], kN[:, u % 2, i * P:(i + 1) * P],
                                  vo[:, u % 2, i * P:(i + 1) * P], start=(h == 0), stop=(h == 1))
                last.then_inc(S("ctx_ps"), 1)

            def attn_out(u):
                j, q = divmod(u, NQ)
                pe.wait_ge(S("ctx_sb"), u + 1)
                pe.wait_ge(S("q_norm"), u + 1)
                if j >= 1:
                    pe.wait_ge(S("attn_y"), j)
                for g in range(2):
                    last = full(bank[C * q:C * q + C, 7, g * T:(g + 1) * T], cwt[:, u % 3, g, :],
                                qn[:, u % 3, g * T:(g + 1) * T])
                last.then_inc(S("attn_ps"), 1)

            for i in range(U + 3):
                if i < U:
                    attn_proj(i)
                if 0 <= i - 1 < U:
                    attn_mid(i - 1)
                for m in filter_turns(i):
                    filters(m)
                if 0 <= i - 2 < U:
                    attn_ctx(i - 2)
                if 0 <= i - 3 < U:
                    attn_out(i - 3)
            def attention_done(j):
                pe.wait_ge(S("filt_sb"), C // 2)
                pe.wait_ge(S("attn_y"), [1, 2, CH, CH][j])

            ln_pe(pe, 1, ln_src[1], attention_done)

            keep_busy(BUSY[2], 4)
            pe.wait_ge(S("xr_v"), 1)
            pe.wait_ge(S("xr_a"), 1)
            ln_pe(pe, 2, ln_src[2], lambda j: None)
            pe.wait_ge(S("toep_in"), 16 * FRACS * NQ)
            pe.wait_ge(S("ln_applied"), 3 * CH)

            def lag(seg, m):
                return toep[:, SEG_AT[seg] + 4 * m:SEG_AT[seg] + 4 * m + 4, :]

            def onto(k, lo, hi, lhs, cols, at, start=False, stop=False, **kw):
                return mm(bank[:, k, lo * B:hi * B], lhs, cols[:, at * B:(at + hi - lo) * B], start=start, stop=stop, **kw)

            for seg, lo, hi in ((3, 0, 8), (2, 8, 16), (1, 16, 32)):
                for m in range(hi):
                    t0 = max(lo, m)
                    last = onto(4 + lo // 16, t0 % 16, t0 % 16 + hi - t0, lag(seg, m), xn, t0 - m,
                                start=(m == 0 and seg != 2), stop=(m == hi - 1), skip_group_check=(seg >= 2))
                if hi % 16 == 0:
                    last.then_inc(S("stu_ps"), 1)
            pe.wait_ge(S("stu_halves"), 3)
            for n, m in enumerate([QH] + [m for m in range(1, 2 * QH) if m != QH]):
                lo, hi = max(0, m - QH), min(QH, m)
                last = onto(3, lo, hi, lag(0, m + QH), x01, lo + QH - m, start=(n == 0), stop=(n == 2 * QH - 2))
            last.then_inc(S("both_ps"), 1)
            for k, first, diff in ((6, 2 * QH, diff12), (7, 3 * QH, diff32)):
                for m in range(first - QH):
                    lo = max(0, m + 2 * QH - first)
                    onto(k, lo, QH, lag(0, m), xn, first + lo - m, start=(m == 0))
                    for j, bk, m_centre, m_spread in ((0, 6, 4, 8), (1, 7, 2, 6), (2, 7, 14, 18)):
                        if k == bk and m == m_centre:
                            pe.wait_ge(S("x_stu"), j + 1)
                            ln_centre(pe, CH * LN_TRI + j, tokens(xQ, j))
                        if k == bk and m == m_spread:
                            ln_spread(pe, CH * LN_TRI + j)
                for m in range(1, 2 * QH):
                    lo, hi = max(0, m - QH), min(QH, m)
                    onto(k, lo, hi, diff[:, 4 * (m - 1):4 * m, :], xn, (QH if k == 6 else 0) + lo + QH - m)
                pe.wait_ge(S("both_sb"), 1)
                mm(bank[:, k, :], ident, both, start=False, stop=True).then_inc(S("stu_ps"), 1)

            keep_busy(BUSY[3], 6)
            pe.wait_ge(S("x_stu"), CH)
            ln_centre(pe, CH * LN_TRI + CH - 1, tokens(xQ, CH - 1))
            ln_spread(pe, CH * LN_TRI + CH - 1)
            pe.wait_ge(S("w_late_in"), 16)
            pe.wait_ge(S("ln_applied"), 4 * CH)
            for k in range(2):
                for m in range(16):
                    cols = (xnH[:, m, :, :].rearrange("p g w -> p (g w)") if k == 0
                            else xmQ.rearrange("p g (h w) -> p (g h) w", w=W)[:, :, m])
                    last = full(bank[:, 4 * k + m // 4, (m % 4) * P:(m % 4 + 1) * P], cols, [wa, wb][k])
                    if m % 8 == 7:
                        last.then_inc(S("ab_ps"), 1)
            pe.wait_ge(S("a_pre"), 1)
            for j in range(CH):
                last = full(bank[:, j, :], wg, flat(xm, j))
            last.then_inc(S("gate_ps"), 1)
            pe.wait_ge(S("b_pre"), 1)
            pe.wait_ge(S("a_bd"), 2)
            pe.wait_ge(S("b_s"), 1)
            pe.wait_ge(S("b_zero"), 1)
            for m in range(64):
                at, part = m // 8, m % 8 // 2
                last = mm(bank[C * part:C * part + C, 4 + at // 4, (at % 4) * P:(at % 4 + 1) * P], b_s[:, m, :],
                          a_bd[:, m, :, :], start=(m % 2 == 0), stop=(m % 2 == 1))
                if m % 32 == 31:
                    last.then_inc(S("z_cols"), 1)
            for m in range(8):
                pe.wait_ge(S("z_cols_sb"), m // 4 + 1)
                last = pe.transpose(bank[:, 4 + m // 4, (m % 4) * P:(m % 4 + 1) * P], z_cols[:, m * P:(m + 1) * P], ident)
            last.then_inc(S("z_ps"), 1)
            full(bank[:, 6, 0:1], wz_rows, b2).then_inc(S("bz_ps"), 1)
            pe.wait_ge(S("z_n"), 1)
            pe.wait_ge(S("bz2"), 1)
            for m in range(8):
                last = pe.transpose(bank[:, 6 + m // 4, (m % 4) * P:(m % 4 + 1) * P], zn[:, m * P:(m + 1) * P],
                                    ident)
            last.then_inc(S("z_tr"), 1)
            pe.wait_ge(S("z_t"), 1)
            pe.wait_ge(S("wz_g"), 1)
            pe.wait_ge(S("gate"), 1)
            for jj in range(16):
                for q in range(NQ):
                    last = full(bank[C * q:C * q + C, jj // 4, (jj % 4) * P:(jj % 4 + 1) * P], wz[:, jj % 8, :],
                                zT[:, (2 * q + jj // 8) * P:(2 * q + jj // 8 + 1) * P])
                if jj % 4 == 3:
                    last.then_inc(S("tri_ps"), 1)
            ln_pe(pe, LN_RNN, ln_src[LN_RNN], lambda k: pe.wait_ge(S("x_tri"), k + 1))

            def wx(i, k, j):
                pe.wait_ge(S("ln_applied"), CH * k + j + 1)
                full(bank[:, j, :], rwt[i], flat([xn, xm][i], j)).then_inc(S("wx_ps"), 1)

            def rnn(i, k):
                for j in range(WX_EARLY[i], CH):
                    wx(i, k, j)
                pe.wait_ge(S("bn_mean_in"), i + 1)
                full(bank[:, 4, 0:1], quarter, mv[:, 0:1]).then_inc(S("bn_mean"), 1)
                full(bank[:, 5, 1:2], rvt[i], rst[:, 12:13])
                pe.wait_ge(S("bn_var_in"), i + 1)
                full(bank[:, 5, 0:1], quarter, rst[:, 2:3]).then_inc(S("bn_var"), 1)
                for n in range(1, SWEEPS):
                    for j in range(CH):
                        if n == 1:
                            pe.wait_ge(S("bn_v"), i + 1)
                        pe.wait_ge(S(f"sweep_y{i}"), CH * (n - 1) + j + 1)
                        full(bank[:, 4 + j, :], rvt[i], yS[:, 2 * j:2 * j + 2, 0:T])\
                            .then_inc(S(f"sweep_ps{i}"), 1)
                pe.wait_ge(S("settled_rows"), i + 1)
                full(bank[0:1, 0, 0:1], moved[:, CH + 1:CH + 2], ones[:, 0:1]).then_inc(S("settled_sum"), 1)
                pe.wait_ge(S("verdict"), i + 1)
                by_steps = pe.value_load(unsettled[0:1, i:i + 1], min_val=0, max_val=1)
                zt = zs.rearrange("p (g t) -> p g t", g=G)
                with pe.If(by_steps != 0):
                    with pe.Fori(0, T // 2) as t2:
                        for k2 in range(2):
                            mm(bank[:, 6 + k2, 0:G], ident, zt[:, :, bass.ds(t2 * 2 + k2, 1)], start=True, stop=False)
                            pe.wait_ge(S(f"y_step{i}"), t2 * 2 + (k2 + 1))
                            mm(bank[:, 6 + k2, 0:G], rvt[i], yF[:, :, bass.ds(t2 * 2 + k2, 1)],
                               start=False, stop=True).then_inc(S(f"v_step{i}"), 1)

            def scan(i, k):
                keep_busy(BUSY[k], [5, 0][i])
                pe.wait_ge(S("xr_v"), 2 + i)
                pe.wait_ge(S("xr_a"), 2 + i)
                ln_pe(pe, k, ln_src[k], lambda j: None)

                def centre_next(j):
                    pe.wait_ge(S("back_v"), CH * i + j + 1)
                    pe.wait_ge(S("back_a"), CH * i + j + 1)
                    ln_centre(pe, CH * (k + 1) + j, tokens(xQ, j))

                for h in range(1, H):
                    pe.wait_ge(S("row_done"), H * i + h)
                    for w in range(3):
                        last = mm(bank[:, 4 + h % 2, 0:P], band[i][:, w, :], carry[:, h - 1, w:w + 4, :],
                                  start=(w == 0), stop=(w == 2))
                    last.then_inc(S("row_ps"), 1)
                    if h >= ROW_LN and (h - ROW_LN) % 4 == 0:
                        centre_next((h - ROW_LN) // 4)
                    elif h > ROW_LN and (h - ROW_LN) % 4 == 1:
                        ln_spread(pe, CH * (k + 1) + (h - ROW_LN) // 4)
                    else:
                        keep_busy(BUSY_ROW, 3, P)
                ln_spread(pe, CH * (k + 1) + 2)
                keep_busy(BUSY[k + 1], 4)
                if i == 1:
                    for j in range(WX_EARLY[1]):
                        wx(1, k + 1, j)
                centre_next(3)
                ln_spread(pe, CH * (k + 1) + 3)

            def experts():
                pe.wait_ge(S("ln_applied"), CH * 7)
                for j in range(4):
                    for gg in range(2):
                        last = full(bank[64 * gg:64 * gg + 64, 4 + j // 2, (j % 2) * T:(j % 2 + 1) * T],
                                    gwc, xmQ[:, 2 * j + gg, :])
                last.then_inc(S("gate_l"), 1)
                pe.wait_ge(S("ln_applied"), CH * 7)
                for g in range(G):
                    for h in range(2):
                        m = 2 * g + h
                        last = pe.transpose(bank[:, m // 4, (m % 4) * P:(m % 4 + 1) * P],
                                            xmQ[:, g, h * P:(h + 1) * P], ident)
                last.then_inc(S("xtok_ps"), 1)
                for half in range(2):
                    for j in (2 * half, 2 * half + 1):
                        pe.wait_ge(S("pm"), j + 1)
                        for h in range(2):
                            m = 2 * j + h
                            last = pe.transpose(bank[:, 6 + half, (m % 4) * P:(m % 4 + 1) * P],
                                                pm[:, j, h * P:(h + 1) * P], ident)
                    last.then_inc(S("pmt_ps"), 1)
                    pe.wait_ge(S("xtok"), 1)
                    pe.wait_ge(S("pmt"), half + 1)
                    for g in range(4 * half, 4 * half + 4):
                        for h in range(2):
                            last = mm(bank[:, 0, g * 64:(g + 1) * 64], xtok[:, g, h, :],
                                      pmt[:, g // 2, h, 64 * (g % 2):64 * (g % 2) + 64], start=(h == 0), stop=(h == 1))
                last.then_inc(S("pool_ps"), 1)
                pe.wait_ge(S("pooled"), 1)
                pe.wait_ge(S("w_moe"), 32)
                for e in range(E):
                    last = full(bank[:, 1, e * B:(e + 1) * B], w1[:, e, :], pool_[0:C + 1, e, :])
                last.then_inc(S("hid_ps"), 1)
                pe.wait_ge(S("hid"), 1)
                for e in range(E):
                    last = full(bank[0:C, 2, e * B:(e + 1) * B], w2[:, e, :], hid[:, e, :])
                last.then_inc(S("eo_ps"), 1)
                keep_busy(BUSY_MOE, 0)
                pe.wait_ge(S("eo_bd"), 1)
                for g in range(G):
                    last = full(bank[:, 4 + g // 2, (g % 2) * T:(g % 2 + 1) * T],
                                moD[:, g // 2, 4 * (g % 2):4 * (g % 2) + 4, :], pm[:, g // 2, :])
                    if g % 2:
                        last.then_inc(S("moe_ps"), 1)

            rnn(0, 4)
            scan(0, 5)
            experts()
            scan(1, 7)
            rnn(1, 8)

        @block.scalar
        def _(act):
            n = [0]

            def link(ins):
                n[0] += 1
                ins.then_inc(S("act_step"), 1)
                act.wait_ge(S("act_step"), n[0])

            def lnexp():
                act.preload_act_table_set("natural_log_exp_and_others")

            lnexp()
            ln_act(act, 0)

            act.wait_ge(S("fw_z"), 1)
            act.activation(fw[:, 1, :], fw[:, 0, :], ACT.Exp, bias=fw[:, 2, 0:1], accum_out=fw[:, 2, 1:2])\
                .then_inc(S("fw_exp"), 1)
            act.wait_ge(S("w_stu_in"), 16)
            link(act.activation(sig4[0:64, :], sigma[0:64, :], ACT.Ln))
            link(act.activation(sig4[0:64, :], sig4[0:64, :], ACT.Exp, scale=0.25))
            act.activation(nsig4[32:64, :], sig4[32:64, :], ACT.Copy, scale=-1.0).then_inc(S("sig4"), 1)
            act.wait_ge(S("wvo_ps"), 1)
            act.wait_ge(S("wvo_zero"), 1)
            for q in range(NQ):
                rows = slice(C * q, C * q + C)
                last = act.activation(wvo[rows, q, :], bank[rows, 6, 0:P], ACT.Copy, scale=DH ** -0.5 / T)
            last.then_inc(S("wvo"), 1)

            def a_k(u):
                act.wait_ge(S("k_max"), u + 1)
                if u >= 2:
                    act.wait_ge(S("k_tr"), u - 1)
                for g in range(2):
                    last = act.activation(kE[:, u % 2, g * T:(g + 1) * T], bank[:, 5 * (u % 2), g * T:(g + 1) * T], ACT.Exp,
                                          bias=nkm[:, 2 * u + g:2 * u + g + 1],
                                          accum_out=kz[:, 2 * u + g:2 * u + g + 1])
                last.then_inc(S("k_exp"), 1)

            def a_v(u):
                act.wait_ge(S("v_ps"), u + 1)
                if u >= 2:
                    act.wait_ge(S("ctx_ps"), u - 1)
                act.activation(vo[:, u % 2, :], bank[:, 4, :], ACT.Copy).then_inc(S("v_sb"), 1)

            def a_q(u):
                act.wait_ge(S("q_shift"), u + 1)
                if u >= 2:
                    act.wait_ge(S("q_norm"), u - 1)
                act.activation(qe[:, u % 2, :], qs[:, u % 2, :], ACT.Exp).then_inc(S("q_exp"), 1)

            def a_kn(u):
                act.wait_ge(S("k_tr"), u + 1)
                if u >= 2:
                    act.wait_ge(S("ctx_ps"), u - 1)
                act.activation(kN[:, u % 2, :], bank[:, 3, :], ACT.Copy).then_inc(S("k_rows"), 1)

            def a_y(j):
                act.wait_ge(S("attn_ps"), NQ * (j + 1))
                act.activation(flat(yb, j), bank[:, 7, :], ACT.Identity, bias=bout).then_inc(S("attn_y"), 1)

            def a_filters(m):
                act.wait_ge(S("filt_ps"), m + 1)
                act.activation(filt[:, AR:, 2 * m:2 * m + 2].rearrange("p t e -> p e t"),
                               bank[:, 1, :].rearrange("p (e t) -> p e t", e=2), ACT.Copy).then_inc(S("filt_sb"), 1)

            for i in range(U + 3):
                if i in (1, 2):
                    act.wait_ge(S("w_spec_in"), 32)
                    act.wait_ge(S("fw_done"), 1)
                    for n_ in (2 * i - 2, 2 * i - 1):
                        act.activation(wm_raw[:, n_, :], wm_raw[:, n_, :], ACT.Copy, scale=fw[:, 7, n_:n_ + 1])\
                            .then_inc(S("wm_scaled"), 1)
                if i < U:
                    a_k(i)
                if 0 <= i - 1 < U:
                    a_kn(i - 1)
                if i < U:
                    a_v(i)
                    a_q(i)
                for m in filter_turns(i):
                    a_filters(m)
                if i >= 3 and (i - 3) % NQ == NQ - 1:
                    a_y((i - 3) // NQ)
            ln_act(act, 1)

            def to_layout_r(k, dep, v):
                act.wait_ge(S(dep), v)
                for q in range(NQ):
                    for r in range(NQ):
                        if (q, r) in ACT_TO_R:
                            last = act.activation(
                                xR[C * r:C * r + C, :, q:B:NQ].rearrange("p t g -> p g t"),
                                (by_batch(xn) if dep == "x_rnn0" else xQ)[C * q:C * q + C, :, r:T:NQ], ACT.Copy)
                last.then_inc(S("xr_a"), 1)

            to_layout_r(0, "x_attn", CH)
            ln_act(act, 2)
            act.wait_ge(S("both_ps"), 1)
            act.activation(both, bank[:, 3, :], ACT.Copy).then_inc(S("both_sb"), 1)
            for i in range(CH * LN_TRI, CH * LN_TRI + CH):
                ln_square(act, i)
                ln_rstd(act, i)

            def sigmoids():
                act.preload_act_table_set("sigmoid_and_others")

            sigmoids()
            act.wait_ge(S("a_in"), 1)
            act.activation(a_s[:, :], a_in[:, :].rearrange("p (h m) -> p m h", h=16), ACT.Sigmoid).then_inc(S("a_s"), 1)
            act.wait_ge(S("b_in"), 1)
            act.wait_ge(S("b_zero"), 1)
            for par in range(2):
                last = act.activation(b_s[:, par::2, W * par:W * par + W],
                                      b_in[:, :].rearrange("p (h m) -> p m h", h=16)[:, par::2, :], ACT.Sigmoid)
            last.then_inc(S("b_s"), 1)
            act.wait_ge(S("a_s"), 1)
            for g in range(ACT_BD):
                last = act.activation(a_bd[:, :, g, :], a_s.rearrange("p (m i) -> p m i", i=16), ACT.Copy,
                                      scale=par16[:, g:g + 1])
            last.then_inc(S("a_bd"), 1)
            act.wait_ge(S("gate_ps"), 1)
            act.activation(gate[:, :], bank[:, 0:4, :], ACT.Sigmoid, bias=bg).then_inc(S("gate"), 1)
            lnexp()
            for k in range(2):
                act.wait_ge(S("z_cols"), k + 1)
                act.activation(flat(z_cols, k), bank[:, 4 + k, :], ACT.Copy).then_inc(S("z_cols_sb"), 1)
            act.wait_ge(S("z_c"), 1)
            act.activation(zq[:, :], zc[:, :], ACT.Square).then_inc(S("z_sq"), 1)
            act.wait_ge(S("z_var"), 1)
            link(act.activation(zst[:, 2, :], zst[:, 1, :], ACT.Ln, bias=LN_TOK, scale=1.0 / CT))
            act.activation(zst[:, 3, :], zst[:, 2, :], ACT.Exp, scale=-0.5).then_inc(S("z_rstd"), 1)
            act.wait_ge(S("z_tr"), 1)
            act.activation(zT[:, :], bank[:, 6:8, :], ACT.Copy).then_inc(S("z_t"), 1)
            ln_act(act, LN_RNN)

            def rnn(i, k):
                act.wait_ge(S("bn_v"), i + 1)
                link(act.activation(rst[:, 5:6], rst[:, 10:11], ACT.Ln, bias=LN_TOK))
                act.activation(rst[:, 6:7], rst[:, 5:6], ACT.Exp, scale=-0.5).then_inc(S("bn_rstd"), 1)
                sigmoids()
                for j in range(CH):
                    act.wait_ge(S("z_in"), CH * i + j + 1)
                    act.activation(yS[:, 2 * j:2 * j + 2, 1:T + 1], flat(zs, j).rearrange("p (g t) -> p g t", g=2),
                                   ACT.Sigmoid, bias=rst[:, 11:12]).then_inc(S(f"sweep_y{i}"), 1)
                for n in range(1, SWEEPS):
                    y = yF if n == SWEEPS - 1 else yS
                    for j in range(CH):
                        act.wait_ge(S(f"sweep_pre{i}"), CH * (n - 1) + j + 1)
                        act.activation(y[:, 2 * j:2 * j + 2, 1:T + 1], pre[:, j, :].rearrange("p (g t) -> p g t", g=2),
                                       ACT.Sigmoid).then_inc(S(f"sweep_y{i}"), 1)
                act.wait_ge(S("verdict"), i + 1)
                by_steps = act.value_load(unsettled[0:1, i:i + 1], min_val=0, max_val=1)
                with act.If(by_steps != 0):
                    act.wait_ge(S(f"x_early{i}"), 1)
                    act.sem_inc(S(f"y_step{i}"), 1)
                    with act.Fori(0, T // 2) as t2:
                        for k2 in range(2):
                            act.wait_ge(S(f"v_step{i}"), t2 * 2 + (k2 + 1))
                            act.activation(yF[:, :, bass.ds(t2 * 2 + (k2 + 1), 1)], bank[:, 6 + k2, 0:G],
                                           ACT.Sigmoid).then_inc(S(f"y_step{i}"), 1)
                    act.wait_ge(S(f"y_step{i}"), T + 1)
                act.sem_inc(S("y_final"), 1)

            def scan_back(i, k):
                for j in range(CH):
                    act.wait_ge(S("back_sum"), CH * i + j + 1)
                    for q in range(NQ):
                        for r in ACT_PHASES[j]:
                            last = act.activation(*back(j, q, r), ACT.Copy)
                    last.then_inc(S("back_a"), 1)
                    if j == CH - 1:
                        ln_rstd(act, CH * (k + 1) + j - 1)
                    ln_square(act, CH * (k + 1) + j)
                    if j != CH - 2:
                        ln_rstd(act, CH * (k + 1) + j)

            rnn(0, 4)
            to_layout_r(1, "x_rnn0", 1)
            lnexp()
            ln_act(act, 5)
            scan_back(0, 5)
            for j in range(4):
                act.wait_ge(S("moe_max"), j + 1)
                act.activation(ex[:, j, :], lg[:, j, :], ACT.Exp, bias=mo[:, j:j + 1], accum_out=mo[:, 4 + j:5 + j])\
                    .then_inc(S("moe_exp"), 1)
            act.wait_ge(S("xtok_ps"), 1)
            act.activation(xtok.rearrange("p g h n -> p (g h n)"), bank[:, 0:4, :].rearrange("p k n -> p (k n)"), ACT.Copy).then_inc(S("xtok"), 1)
            act.preload_act_table_set("gelu_and_others")
            act.wait_ge(S("pmt_ps"), 1)
            act.activation(pmt[:, 0:2].rearrange("p j h n -> p (j h n)"), bank[:, 6, :], ACT.Copy).then_inc(S("pmt"), 1)
            act.wait_ge(S("hid_ps"), 1)
            act.activation(hid.rearrange("p e b -> p (e b)"), bank[:, 1, :], ACT.Gelu).then_inc(S("hid"), 1)
            lnexp()
            to_layout_r(2, "x_moe", CH)
            ln_act(act, 7)
            scan_back(1, 7)
            rnn(1, 8)
            store(act, (2, 3))

        @block.vector
        def _(dve):
            n = [0]

            def link(ins):
                n[0] += 1
                ins.then_inc(S("dve_step"), 1)
                dve.wait_ge(S("dve_step"), n[0])

            dve.wait_ge(S("x_in"), 16 * NQ)
            for g in range(G):
                last = dve.transpose(xQ[:, g, :].rearrange("p (r k) -> p k r", k=8), xN[:, g, :, :])
                if g % 2:
                    last.then_inc(S("xq_in"), 1)
            ln_dve(dve, 0)
            dve.wait_ge(S("w_stu_in"), 16)
            link(dve.tensor_tensor(fw[:, 0, :], lw, gum, ALU.add))
            dve.tensor_reduce(out=fw[:, 2, 0:1], in_=fw[:, 0, :], axis=AX, op=ALU.max, negate=True).then_inc(S("fw_z"), 1)
            dve.wait_ge(S("fw_exp"), 1)
            link(dve.reciprocal(fw[:, 2, 2:3], fw[:, 2, 1:2]))
            link(dve.tensor_scalar(fw[:, 3, :], fw[:, 1, :], fw[:, 2, 2:3], None, ALU.mult))
            link(dve.tensor_reduce(out=fw[:, 2, 3:4], in_=fw[:, 3, :], axis=AX, op=ALU.max))
            link(dve.tensor_scalar(fw[:, 4, :], fw[:, 3, :], fw[:, 2, 3:4], None, ALU.is_equal))
            link(dve.memset(fw[:, 5, :], 0.0))
            for f in range(1, FRACS):
                link(dve.tensor_tensor(fw[:, 5, f:f + 1], fw[:, 5, f - 1:f], fw[:, 4, f - 1:f], ALU.max))
            link(dve.tensor_tensor(fw[:, 4, :], fw[:, 4, :], fw[:, 5, :], ALU.is_gt))
            link(dve.tensor_tensor(fw[:, 6, :], fw[:, 4, :], fw[:, 3, :], ALU.subtract))
            dve.tensor_tensor(fw[:, 7, :], fw[:, 6, :], fw[:, 3, :], ALU.add).then_inc(S("fw_done"), 1)

            def v_k(u):
                dve.wait_ge(S("k_ps"), u + 1)
                dve.tensor_reduce(out=nkm[:, 2 * u:2 * u + 2],
                                  in_=bank[:, 5 * (u % 2), :].rearrange("p (g t) -> p g t", g=2),
                                  axis=AX, op=ALU.max, negate=True).then_inc(S("k_max"), 1)

            def v_q(u):
                dve.wait_ge(S("q_ps"), u + 1)
                link(dve.tensor_reduce(out=qm[:, u % 2, :], in_=bank[:, 2, :].rearrange("p (k r) -> p k r", r=32),
                                       axis=AX, op=ALU.max, negate=True, apply_transpose=True))
                link(dve.transpose(qb[:, u % 2, :].rearrange("p (k r) -> p k r", r=32),
                                   qm[:, u % 2, :].rearrange("p (k o) -> p k o", o=1).to_broadcast([P, 16, 32])))
                if u >= 2:
                    dve.wait_ge(S("q_exp"), u - 1)
                dve.tensor_tensor(qs[:, u % 2, :], bank[:, 2, :], qb[:, u % 2, :], ALU.add).then_inc(S("q_shift"), 1)

            def v_qw(u):
                dve.wait_ge(S("q_exp"), u + 1)
                link(dve.tensor_reduce(out=qz[:, u % 2, :], in_=qe[:, u % 2, :].rearrange("p (k r) -> p k r", r=32),
                                       axis=AX, op=ALU.add, apply_transpose=True))
                link(dve.reciprocal(qrz[:, u % 2, :], qz[:, u % 2, :]))
                if u >= 2:
                    dve.wait_ge(S("q_norm"), u - 1)
                dve.transpose(qw[:, u % 2, :].rearrange("p (k r) -> p k r", r=32),
                              qrz[:, u % 2, :].rearrange("p (k o) -> p k o", o=1).to_broadcast([P, 16, 32]))\
                    .then_inc(S("q_weight"), 1)

            def v_ctx(u):
                link(dve.reciprocal(rkz[:, 2 * u:2 * u + 2], kz[:, 2 * u:2 * u + 2]))
                dve.wait_ge(S("ctx_ps"), u + 1)
                if u >= 3:
                    dve.wait_ge(S("attn_ps"), u - 2)
                rz = rkz[:, 2 * u:2 * u + 2].rearrange("p (g o) -> p g o", o=1).to_broadcast([P, 2, C])
                heads = bank[:, 6, 0:2 * P].rearrange("p (g h c) -> p g h c", g=2, h=HEADS)
                for h in range(HEADS):
                    rows = slice(C * h, C * h + C)
                    last = dve.tensor_tensor(cwt[rows, u % 3, :, :], heads[rows, :, h, :], rz[rows], ALU.mult)
                last.then_inc(S("ctx_sb"), 1)

            for i in range(U + 2):
                if i < U:
                    v_k(i)
                    v_q(i)
                if 0 <= i - 1 < U:
                    v_qw(i - 1)
                if 0 <= i - 2 < U:
                    v_ctx(i - 2)

            def attn_apply(j, i):
                dve.tensor_tensor(flat(xn, j), bank[:, j, :], rs[:, i % 2, :], ALU.mult).then_inc(S("ln_applied"), 1)
                dve.wait_ge(S("ln_applied"), i + 1)
                dve.scalar_tensor_tensor(out=flat(xQf, j), in0=flat(xn, j), scalar=lnsc,
                                         in1=flat(xQf, j), op0=ALU.mult, op1=ALU.add).then_inc(S("x_attn"), 1)

            ln_dve(dve, 1, attn_apply)

            def to_layout_r(dep, v):
                dve.wait_ge(S(dep), v)
                for q in range(NQ):
                    for r in range(NQ):
                        if (q, r) not in ACT_TO_R:
                            last = dve.tensor_copy(
                                xR[C * r:C * r + C, :, q:B:NQ].rearrange("p t g -> p g t"),
                                (by_batch(xn) if dep == "x_rnn0" else xQ)[C * q:C * q + C, :, r:T:NQ])
                last.then_inc(S("xr_v"), 1)

            to_layout_r("x_attn", CH)
            ln_dve(dve, 2)
            dve.wait_ge(S("xr_a"), 1)

            dve.wait_ge(S("toep_in"), 16 * FRACS * NQ)
            dve.tensor_tensor(x01, xn[:, 0:QH * B], xn[:, QH * B:2 * QH * B], ALU.add).then_inc(S("stu_halves"), 1)
            a1, a2, a3 = (toep[:, 4 * m:4 * (m + 2 * QH - 1), :] for m in (1, 1 + QH, 1 + 2 * QH))
            dve.tensor_tensor(diff12, a1, a2, ALU.subtract).then_inc(S("stu_halves"), 1)
            dve.tensor_tensor(diff32, a3, a2, ALU.subtract).then_inc(S("stu_halves"), 1)

            def add_stu(j):
                dve.wait_ge(S("stu_ps"), j + 1)
                stu = bank[:, 4 + j, :].rearrange("p (t b) -> p t b", b=B)
                for q in range(NQ):
                    for r in range(NQ):
                        xs, _ = back(j, q, r)
                        last = dve.tensor_tensor(xs, stu[C * r:C * r + C, :, q:B:NQ].rearrange("p t g -> p g t"), xs,
                                                 ALU.add)
                last.then_inc(S("x_stu"), 1)

            def twice(j, i):
                h4 = xnH[:, 4 * j:4 * j + 4, :, :].rearrange("p h g w -> p g h w")
                for out_ in (tokens(xmQ, j).rearrange("p g (h w) -> p g h w", w=W), h4):
                    last = dve.tensor_tensor(out_, bank[:, j, :].rearrange("p (g h w) -> p g h w", g=G, w=W),
                                             rs[:, i % 2, :].rearrange("p (g h w) -> p g h w", g=G, w=W), ALU.mult)
                last.then_inc(S("ln_applied"), 1)

            def normalise(j):
                dve.wait_ge(S("ln_rstd"), CH * LN_TRI + j + 1)
                twice(j, CH * LN_TRI + j)

            add_stu(0)
            add_stu(1)
            normalise(0)
            normalise(1)
            add_stu(2)
            normalise(2)
            add_stu(3)
            normalise(3)
            dve.wait_ge(S("w_late_in"), 16)
            for k in range(2):
                if k:
                    dve.wait_ge(S("a_in"), 1)
                pre4 = ab_pre.rearrange("p (m n) -> p m n", n=2 * CT)
                for half in range(2):
                    dve.wait_ge(S("ab_ps"), 2 * k + half + 1)
                    first = 4 * k + 2 * half
                    last = dve.tensor_tensor(pre4[:, 32 * half:32 * half + 32, :],
                                             bank[:, first:first + 2, :].rearrange("p k (m n) -> p (k m) n", n=2 * CT),
                                             ab_bias[:, k:k + 1, :].to_broadcast([P, 32, 2 * CT]), ALU.add)
                last.then_inc(S(["a_pre", "b_pre"][k]), 1)
                dve.wait_ge(S(["a_pre", "b_pre"][k]), 1)
                dve.tensor_tensor((b_in if k else a_in).rearrange("p (m c) -> p m c", c=CT), pre4[:, :, 0:CT], pre4[:, :, CT:2 * CT],
                                  ALU.mult).then_inc(S(["a_in", "b_in"][k]), 1)
            dve.wait_ge(S("a_s"), 1)
            for g in range(ACT_BD, 8):
                last = dve.tensor_scalar(a_bd[:, :, g, :], a_s.rearrange("p (m i) -> p m i", i=16),
                                         par16[:, g:g + 1], None, ALU.mult)
            last.then_inc(S("a_bd"), 1)
            dve.wait_ge(S("z_ps"), 1)
            zp = bank[:, 4:6, :].rearrange("p k n -> p (k n)").rearrange("p (q c j) -> p q j c", q=NQ, c=CT)
            z4 = [a.rearrange("p (q j c) -> p q j c", q=NQ, j=16) for a in (zc, zq, zn)]
            link(dve.tensor_reduce(out=zst[:, 0, :], in_=zp, axis=AX, op=ALU.add))
            link(dve.tensor_scalar(zst[:, 0, :], zst[:, 0, :], -1.0 / CT, None, ALU.mult))
            zm = zst[:, 0, :].rearrange("p (q j o) -> p q j o", q=NQ, o=1).to_broadcast([P, NQ, 16, CT])
            dve.tensor_tensor(z4[0], zp, zm, ALU.add).then_inc(S("z_c"), 1)
            dve.wait_ge(S("bz_ps"), 1)
            dve.tensor_tensor(bz2[:, :], bank[:, 6, 0:1], bz, ALU.add).then_inc(S("bz2"), 1)
            dve.tensor_scalar(wz[:, :, :], wz[:, :, :], g2, None, ALU.mult).then_inc(S("wz_g"), 1)
            dve.wait_ge(S("z_sq"), 1)
            dve.tensor_reduce(out=zst[:, 1, :], in_=z4[1], axis=AX, op=ALU.add).then_inc(S("z_var"), 1)
            dve.wait_ge(S("z_rstd"), 1)
            zr = zst[:, 3, :].rearrange("p (m o) -> p m o", o=1).to_broadcast([P, 64, CT])
            dve.wait_ge(S("z_c"), 1)
            dve.tensor_tensor(zn.rearrange("p (m c) -> p m c", c=CT), zc.rearrange("p (m c) -> p m c", c=CT), zr,
                              ALU.mult).then_inc(S("z_n"), 1)
            dve.wait_ge(S("gate"), 1)
            dve.wait_ge(S("bz2"), 1)
            def add_triangle(k):
                dve.wait_ge(S("tri_ps"), k + 1)
                up, ga, xc = (grid_cols(a, k) for a in (upd, gate, xQf))
                link(dve.scalar_tensor_tensor(out=up, in0=bank[:, k, :].rearrange("p (j n) -> p n j", j=4),
                                              scalar=bz2[:, :], in1=ga, op0=ALU.add, op1=ALU.mult))
                dve.tensor_tensor(xc, xc, up, ALU.add).then_inc(S("x_tri"), 1)

            def normalise_cols(k):
                n = CH * LN_RNN + k
                dve.wait_ge(S("ln_rstd"), n + 1)
                dve.tensor_tensor(flat(xn, k), bank[:, k, :], rs[:, n % 2, :], ALU.mult).then_inc(S("ln_applied"), 1)

            for k in range(4):
                add_triangle(k)
            for k in range(4):
                normalise_cols(k)

            def rnn(i, k):
                dve.wait_ge(S(["x_tri", "back_v"][i]), [CH, 2 * CH][i])
                dve.memset(yS[:, :, 0:1], 0.0)
                dve.memset(yF[:, :, 0:1], 0.0)
                dve.memset(rst[:, 12:13], 0.5)
                for j in range(CH):
                    dve.wait_ge(S("wx_ps"), CH * i + j + 1)
                    link(dve.bn_stats(out=bst[:, j, :], in_=bank[:, j, :]))
                dve.bn_aggr(out=mv[:, :], in_=bst[:, :, :]).then_inc(S("bn_mean_in"), 1)
                dve.wait_ge(S("bn_mean_in"), i + 1)
                dve.wait_ge(S("bn_mean"), i + 1)
                link(dve.tensor_copy(rst[:, 0:1], bank[:, 4, 0:1]))
                link(dve.tensor_tensor(rst[:, 1:2], mv[:, 0:1], rst[:, 0:1], ALU.subtract))
                link(dve.tensor_tensor(rst[:, 3:4], rst[:, 1:2], rst[:, 1:2], ALU.mult))
                dve.tensor_tensor(rst[:, 2:3], rst[:, 3:4], mv[:, 1:2], ALU.add).then_inc(S("bn_var_in"), 1)
                dve.wait_ge(S("bn_var"), i + 1)
                dve.tensor_copy(rst[:, 10:12], bank[:, 5, 0:2]).then_inc(S("bn_v"), 1)
                dve.wait_ge(S("bn_rstd"), i + 1)
                link(dve.tensor_tensor(rst[:, 7:8], rst[:, 6:7], rgam[i], ALU.mult))
                link(dve.tensor_tensor(rst[:, 8:9], rst[:, 7:8], rst[:, 0:1], ALU.mult))
                link(dve.tensor_tensor(rst[:, 9:10], rbet[i], rst[:, 8:9], ALU.subtract))
                for j in range(CH):
                    if i == 0:
                        wx_cols = bank[:, 0:4, G * H * j:G * H * (j + 1)].rearrange("p k (n w) -> p n k w", w=4)
                        z_cols = flat(zs, j).rearrange("p (n k w) -> p n k w", k=4, w=4)
                    else:
                        wx_cols = bank[:, 0:4, 2 * TC * j:2 * TC * (j + 1)].rearrange("p k (g t) -> p g k t", g=2)
                        z_cols = flat(zs, j).rearrange("p (g k t) -> p g k t", g=2, k=4)
                    dve.tensor_scalar(z_cols, wx_cols, rst[:, 7:8], rst[:, 9:10], ALU.mult, ALU.add)\
                        .then_inc(S("z_in"), 1)
                dve.wait_ge(S("z_in"), CH * (i + 1))
                for n in range(1, SWEEPS):
                    for j in range(CH):
                        dve.wait_ge(S(f"sweep_ps{i}"), CH * (n - 1) + j + 1)
                        dve.tensor_tensor(pre[:, j, :], bank[:, 4 + j, :], flat(zs, j), ALU.add)\
                            .then_inc(S(f"sweep_pre{i}"), 1)
                for j in range(CH):
                    dve.wait_ge(S(f"sweep_y{i}"), CH * (SWEEPS - 1) + j + 1)
                    link(dve.tensor_tensor(pre[:, j, :].rearrange("p (g t) -> p g t", g=2),
                                           yF[:, 2 * j:2 * j + 2, 1:T + 1], yS[:, 2 * j:2 * j + 2, 1:T + 1], ALU.subtract))
                    link(dve.tensor_reduce(out=moved[:, j:j + 1], in_=pre[:, j, :], axis=AX, op=ALU.max,
                                           apply_absolute_value=True))
                link(dve.tensor_reduce(out=moved[:, CH:CH + 1], in_=moved[:, 0:CH], axis=AX, op=ALU.max))
                dve.tensor_scalar(moved[:, CH + 1:CH + 2], moved[:, CH:CH + 1], -1.0 if force_steps else SETTLED, None,
                                  ALU.is_le).then_inc(S("settled_rows"), 1)
                dve.wait_ge(S("settled_sum"), i + 1)
                dve.tensor_scalar(unsettled[0:1, i:i + 1], bank[0:1, 0, 0:1], P - 0.5, None, ALU.is_lt)\
                    .then_inc(S("verdict"), 1)

            def scan(i, k):
                to_layout_r(["x_rnn0", "x_moe"][i], [1, CH][i])
                ln_dve(dve, k)
                dve.wait_ge(S("edges"), 1)
                dve.wait_ge(S("ln_applied"), CH * (k + 1))
                dve.tensor_copy(carry[:, 0, 1:5, :], xn[:, 0:P].rearrange("p (w b) -> p w b", b=B)).then_inc(S("row_done"), 1)
                def back_half(j, qs):
                    dve.wait_ge(S("back_sum"), CH * i + j + 1)
                    for q in qs:
                        for r in range(NQ):
                            if r not in ACT_PHASES[j]:
                                last = dve.tensor_copy(*back(j, q, r))
                    if qs[-1] == NQ - 1:
                        last.then_inc(S("back_v"), 1)

                def normalise(j):
                    n = CH * (k + 1) + j
                    dve.wait_ge(S("ln_rstd"), n + 1)
                    dve.tensor_tensor([tokens(xmQ, j), by_batch(flat(xm, j))][i], by_batch(bank[:, j, :]),
                                      by_batch(rs[:, n % 2, :]), ALU.mult)\
                        .then_inc(S("ln_applied"), 1)

                for h in range(1, H):
                    dve.wait_ge(S("row_ps"), (H - 1) * i + h)
                    dve.scalar_tensor_tensor(out=carry[:, h, 1:5, :],
                                             in0=bank[:, 4 + h % 2, 0:P].rearrange("p (w b) -> p w b", b=B), scalar=0.0,
                                             in1=xn[:, h * P:(h + 1) * P].rearrange("p (w b) -> p w b", b=B),
                                             op0=ALU.max, op1=ALU.add).then_inc(S("row_done"), 1)
                    if h in (5, 9, 13):
                        back_half(h // 4 - 1, (0, 1))
                    if h in (6, 10, 14):
                        back_half(h // 4 - 1, (2, 3))
                    if h in (9, 13):
                        normalise(h // 4 - 2)
                back_half(3, (0, 1, 2, 3))
                normalise(2)
                normalise(3)

            def experts():
                dve.wait_ge(S("gate_l"), 1)
                link(dve.tensor_scalar(lg.rearrange("p j t -> p (j t)"), bank[:, 4:6, :].rearrange("p k n -> p (k n)"), gb, None, ALU.add))
                for j in range(4):
                    dve.tensor_reduce(out=mo[:, j:j + 1], in_=lg[:, j, :], axis=AX, op=ALU.max, negate=True)\
                        .then_inc(S("moe_max"), 1)
                for j in range(4):
                    dve.wait_ge(S("moe_exp"), j + 1)
                    link(dve.reciprocal(mo[:, 8 + j:9 + j], mo[:, 4 + j:5 + j]))
                    link(dve.tensor_scalar(ex[:, j, :], ex[:, j, :], mo[:, 8 + j:9 + j], None, ALU.mult))
                    link(dve.max(mo[:, 16 + 8 * j:24 + 8 * j], ex[:, j, :]))
                    link(dve.match_replace(out=rep[:, j, :], in_to_replace=mo[:, 16 + 8 * j:24 + 8 * j],
                                           in_values=ex[:, j, :], imm_value=0.0))
                    dve.tensor_tensor(pm[:, j, :], ex[:, j, :], rep[:, j, :], ALU.subtract).then_inc(S("pm"), 1)
                dve.wait_ge(S("pmt_ps"), 2)
                dve.wait_ge(S("pmt"), 1)
                dve.tensor_copy(pmt[:, 2:4].rearrange("p j h n -> p (j h n)"), bank[:, 7, :]).then_inc(S("pmt"), 1)
                dve.memset(pool_[32:33, :, :], 1.0)
                dve.wait_ge(S("pool_ps"), 1)
                pp = bank[:, 0, :].rearrange("p (g m) -> p g m", g=G)
                for q in range(NQ):
                    last = dve.tensor_copy(pool_[0:C, :, q:B:NQ].rearrange("p e g -> p g e"),
                                           pp[C * q:C * q + C, :, E * q:E * q + E])
                last.then_inc(S("pooled"), 1)
                dve.wait_ge(S("eo_ps"), 1)
                link(dve.tensor_tensor(moT[0:C, :].rearrange("p (b e) -> p b e", e=E),
                                       bank[0:C, 2, :].rearrange("p (e b) -> p b e", e=E),
                                       w2b.rearrange("p (o e) -> p o e", o=1).to_broadcast([C, B, E]), ALU.add))
                for gg in range(2):
                    for qp in range(2):
                        m4 = moT[0:C, :].rearrange("p (j n r) -> p j n r", j=4, r=32)[:, :, 2 * gg + qp, :]
                        last = dve.transpose(moB[64 * gg + 32 * qp:64 * gg + 32 * qp + 32, :, :], m4)
                link(last)
                for m in range(8):
                    last = dve.tensor_scalar(moD[:, :, m, :], moB[:, :, :], par16[:, m:m + 1], None, ALU.mult)
                last.then_inc(S("eo_bd"), 1)
                dve.wait_ge(S("back_a"), CH)
                for j in range(CH):
                    dve.wait_ge(S("moe_ps"), j + 1)
                    dve.tensor_tensor(flat(xQf, j), flat(xQf, j), bank[:, 4 + j, :], ALU.add).then_inc(S("x_moe"), 1)

            rnn(0, 4)
            scan(0, 5)
            experts()
            scan(1, 7)
            rnn(1, 8)
            dve.wait_ge(S("x_rnn1"), 1)
            dve.wait_ge(S("xq_in"), CH)
            for g in range(G):
                last = dve.transpose(xN[:, g, :, :], xnQ[:, g, :].rearrange("p (r k) -> p k r", k=8))
                if g % (G // 2) == G // 2 - 1:
                    last.then_inc(S("out_rows"), 1)


def lay_out(x, **w):
    import numpy as np

    w = {k: np.asarray(v) for k, v in w.items()}
    f = np.float32

    def blocks(m, n=NQ):
        r, c = m.shape
        out = np.zeros((n * r, n * c), f)
        for q in range(n):
            out[q * r:(q + 1) * r, q * c:(q + 1) * c] = m
        return out

    def by_block(m):
        out = np.zeros((NQ, C, NQ, m.shape[-1]), f)
        for q in range(NQ):
            out[q, :, q] = m[q] if m.ndim == 3 else m
        return out.reshape(P, -1)

    def rows(v, n=P):
        return np.tile(v.reshape(1, -1), (n, 1))

    def column(v):
        return np.tile(v.reshape(-1, 1), (P // v.size, 1))

    def padded(m):
        return np.concatenate([m, np.zeros((P - m.shape[0], m.shape[1]), f)])

    def gather(parts, table):
        for name, n in parts:
            assert table[name].shape == (P, n), (name, table[name].shape)
        return np.ascontiguousarray(np.concatenate([table[n] for n, _ in parts], axis=1))

    eye = np.eye(P, dtype=f)
    mean = blocks(np.full((C, C), 1.0 / C, f))
    consts = {"centre": blocks(np.eye(C, dtype=f) - f(1.0 / C)), "mean32": mean, "ident": eye,
              "quarter": np.tile(np.eye(C, dtype=f) / NQ, (NQ, NQ)), "ones": np.ones((P, 1), f),
              "par16": np.kron(np.eye(8, dtype=f), np.ones((16, 1), f))}

    qkv = w["L0_conv_w_qkv"]
    attn = {"wv_t": np.tile(qkv[:, 2 * P:].T, (1, NQ)),
            "wo_bd": by_block(w["L0_conv_w_out"].reshape(HEADS, C, C)),
            "wk": by_block(qkv[:, P:2 * P]), "wq": by_block(qkv[:, 0:P]),
            "bout": column(w["L0_conv_b_out"]), "lnsc": column(w["L0_conv_ln_scale"])}

    spec = np.zeros((P, FRACS, C, C), f)
    spec[0:KF] = w["L0_ffn_M_phi_plus"].transpose(1, 0, 2, 3)
    spec[32:32 + KF] = w["L0_ffn_M_phi_minus"].transpose(1, 0, 2, 3)
    spec[64:64 + AR] = w["L0_ffn_M_u"].transpose(1, 0, 2, 3)
    phi, sigma = np.zeros((P, T), f), np.ones((P, 1), f)
    for k in (0, 32):
        phi[k:k + KF] = w["L0_ffn_phi"][0:T].T
        sigma[k:k + KF, 0] = w["L0_ffn_sigma"]
    phi[64:64 + AR, 0:AR] = np.eye(AR, dtype=f)
    stu = {"phi_cols": phi, "sigma": sigma, "lw": rows(w["L0_ffn_log_weights"]), "gum": rows(w["L0_ffn_gumbel"])}

    t = {k[len("L1_conv_"):]: v for k, v in w.items() if k.startswith("L1_conv_")}
    late = {"wa": blocks(np.concatenate([t["Wa1"], t["Wa2"]], axis=1)),
            "wb": blocks(np.concatenate([t["Wb1"], t["Wb2"]], axis=1)), "wg": blocks(t["Wg"]),
            "ab_bias": rows(np.concatenate([t["ba1"], t["ba2"], t["bb1"], t["bb2"]])), "bg": column(t["bg"]),
            "wz": blocks(t["Wz"], 8), "wz_rows": padded(np.tile(t["Wz"], (1, NQ))), "g2": column(t["ln2_g"]),
            "b2": column(t["ln2_b"]), "bz": column(t["bz"])}
    for i, (cell, scan) in enumerate((("L1_ffn_", "L2_conv_W"), ("L3_ffn_", "L3_conv_W"))):
        band = np.zeros((NQ, C, 3, NQ, C), f)
        for p in range(NQ):
            for b in range(3):
                for r in range(NQ):
                    k = 4 * (b - 1) + p - r + 4
                    if 0 <= k < TAPS:
                        band[p, :, b, r] = w[scan][k]
        late |= {f"rwt{i}": blocks(w[cell + "W"].T), f"rvt{i}": blocks(w[cell + "V"].T),
                 f"rgam{i}": column(w[cell + "gamma"]), f"rbet{i}": column(w[cell + "beta"]),
                 f"band{i}": band.reshape(P, -1)}
    late |= {"gwc": blocks(w["L2_ffn_gate_w"].T), "gb": column(w["L2_ffn_gate_b"]),
             "w2b": padded(w["L2_ffn_weight2"][:, HID, :].T)}
    return {"x": np.asarray(x), "consts": gather(CONSTS, consts), "w_attn": gather(W_ATTN, attn),
            "w_stu": gather(W_STU, stu), "w_spec": spec.reshape(P, -1), "w_late": gather(W_LATE, late),
            "w1": w["L2_ffn_weight1"], "w2": w["L2_ffn_weight2"]}


def kernel(**inputs):
    import numpy as _np
    import concourse.bacc as _bacc
    from concourse import mybir as _mybir
    from concourse.bass_utils import run_bass_kernel_spmd as _run

    nc = _bacc.Bacc("TRN2", target_bir_lowering=False, num_devices=1)
    arrays, args = {}, {}
    for name, a in lay_out(**inputs).items():
        arrays[f"in_{name}"] = _np.ascontiguousarray(a)
        args[name] = nc.dram_tensor(f"in_{name}", a.shape, _mybir.dt.from_np(a.dtype), kind="ExternalInput").ap()
    args["out"] = nc.dram_tensor("out_0", (B, H, W, C), _mybir.dt.float32, kind="ExternalOutput").ap()
    build(nc, **args)
    r = _run(nc, [arrays], core_ids=[0])
    return r.results[0]["out_0"]
```
